# Optimizing a Trainium2 kernel written in Bass

```python
import numpy as np
import jax
import jax.numpy as jnp

def _softmax(x, axis=-1):
    return jax.nn.softmax(x, axis=axis)

def _gelu(x):
    return jax.nn.gelu(x, approximate=True)

def _silu(x):
    return jax.nn.silu(x)

def _sigmoid(x):
    return jax.nn.sigmoid(x)

def _layernorm(x, axis=-1, eps=1e-05):
    m = jnp.mean(x, axis=axis, keepdims=True)
    v = jnp.var(x, axis=axis, keepdims=True)
    return (x - m) / jnp.sqrt(v + eps)

def _scatter_add(tgt, idx, src, axis=0):
    return tgt.at[idx].add(src)

def _segment_sum(src, seg, n):
    return jax.ops.segment_sum(src, seg, n)
kernel_name = 'mk_seq_postln_d1_jaxref_r8_2254fb'

def setup_inputs(seed: int=0):
    np.random.seed(seed)
    _w = jnp.asarray

    def _L0_attn_setup():
        import jax, jax.numpy as jnp
        import numpy as np
        D_MODEL = 128
        D_INNER = 256
        D_STATE = 16
        DT_RANK = 64
        D_CONV = 4
        B = 1
        L = 256

        def _forward(x, in_w, conv_w, conv_b, x_proj_w, dt_w, dt_b, A_log, D, out_w, norm_w):
            eps = 1e-05
            h = x * jax.lax.rsqrt(jnp.mean(x * x, axis=-1, keepdims=True) + eps) * norm_w
            xr = h @ in_w
            u, res = jnp.split(xr, 2, axis=-1)
            ut = jnp.transpose(u, (0, 2, 1))
            conv = jax.lax.conv_general_dilated(ut, conv_w, window_strides=(1,), padding=((D_CONV - 1, 0),), feature_group_count=D_INNER, dimension_numbers=('NCH', 'OIH', 'NCH'))
            conv = conv + conv_b[None, :, None]
            u = jax.nn.silu(jnp.transpose(conv, (0, 2, 1)))
            x_dbl = u @ x_proj_w
            dt, Bm, Cm = jnp.split(x_dbl, [DT_RANK, DT_RANK + D_STATE], axis=-1)
            delta = jax.nn.softplus(dt @ dt_w + dt_b)
            A = -jnp.exp(A_log)
            dA = jnp.exp(jnp.einsum('bld,dn->bldn', delta, A))
            dBu = jnp.einsum('bld,bln->bldn', delta * u, Bm)

            def step(s, inp):
                dA_t, dBu_t, C_t = inp
                s = dA_t * s + dBu_t
                y = jnp.einsum('bdn,bn->bd', s, C_t)
                return (s, y)
            s0 = jnp.zeros((x.shape[0], D_INNER, D_STATE), dtype=jnp.float32)
            _, ys = jax.lax.scan(step, s0, (jnp.transpose(dA, (1, 0, 2, 3)), jnp.transpose(dBu, (1, 0, 2, 3)), jnp.transpose(Cm, (1, 0, 2))))
            y = jnp.transpose(ys, (1, 0, 2)) + u * D
            y = y * jax.nn.silu(res)
            return y @ out_w + x
        key = jax.random.key(seed)
        ks = jax.random.split(key, 8)
        s = 0.02
        x = jax.random.normal(ks[0], (B, L, D_MODEL), dtype=jnp.float32)
        in_w = jax.random.normal(ks[1], (D_MODEL, 2 * D_INNER), dtype=jnp.float32) * s
        conv_w = jax.random.normal(ks[2], (D_INNER, 1, D_CONV), dtype=jnp.float32) * s
        conv_b = jnp.zeros((D_INNER,), dtype=jnp.float32)
        x_proj_w = jax.random.normal(ks[3], (D_INNER, DT_RANK + 2 * D_STATE), dtype=jnp.float32) * s
        dt_w = jax.random.normal(ks[4], (DT_RANK, D_INNER), dtype=jnp.float32) * s
        dt_b = jax.random.normal(ks[5], (D_INNER,), dtype=jnp.float32) * s
        A_log = jnp.log(jnp.broadcast_to(jnp.arange(1, D_STATE + 1, dtype=jnp.float32), (D_INNER, D_STATE)))
        D = jnp.ones((D_INNER,), dtype=jnp.float32)
        out_w = jax.random.normal(ks[6], (D_INNER, D_MODEL), dtype=jnp.float32) * s
        norm_w = jnp.ones((D_MODEL,), dtype=jnp.float32)
        return dict(x=x, in_w=in_w, conv_w=conv_w, conv_b=conv_b, x_proj_w=x_proj_w, dt_w=dt_w, dt_b=dt_b, A_log=A_log, D=D, out_w=out_w, norm_w=norm_w)
    _L0_attn_in = _L0_attn_setup()

    def _L0_ffn_setup():
        import jax, jax.numpy as jnp
        import numpy as np
        B, S, D, F, E = (8, 128, 128, 512, 8)
        EPS = 1e-05
        key = jax.random.key(seed)
        ks = jax.random.split(key, 4)
        s = 0.02
        return {'input_features': jax.random.normal(ks[0], (B, S, D), jnp.float32), 'centroids': jax.random.normal(ks[1], (E, D), jnp.float32) * 0.1, 'ln_g': jnp.ones((E, D), jnp.float32), 'ln_b': jnp.zeros((E, D), jnp.float32), 'w1': jax.random.normal(ks[2], (E, D, F), jnp.float32) * s, 'b1': jnp.zeros((E, F), jnp.float32), 'w2': jax.random.normal(ks[3], (E, F, D), jnp.float32) * s, 'b2': jnp.zeros((E, D), jnp.float32)}
    _L0_ffn_in = _L0_ffn_setup()
    _d = {'L0_attn_x': _L0_attn_in['x'], 'L0_attn_in_w': _L0_attn_in['in_w'], 'L0_attn_conv_w': _L0_attn_in['conv_w'], 'L0_attn_conv_b': _L0_attn_in['conv_b'], 'L0_attn_x_proj_w': _L0_attn_in['x_proj_w'], 'L0_attn_dt_w': _L0_attn_in['dt_w'], 'L0_attn_dt_b': _L0_attn_in['dt_b'], 'L0_attn_A_log': _L0_attn_in['A_log'], 'L0_attn_D': _L0_attn_in['D'], 'L0_attn_out_w': _L0_attn_in['out_w'], 'L0_attn_norm_w': _L0_attn_in['norm_w'], 'L0_ffn_centroids': _L0_ffn_in['centroids'], 'L0_ffn_ln_g': _L0_ffn_in['ln_g'], 'L0_ffn_ln_b': _L0_ffn_in['ln_b'], 'L0_ffn_w1': _L0_ffn_in['w1'], 'L0_ffn_b1': _L0_ffn_in['b1'], 'L0_ffn_w2': _L0_ffn_in['w2'], 'L0_ffn_b2': _L0_ffn_in['b2']}
    _x0 = _d['L0_attn_x']
    _d['L0_attn_x'] = jax.random.normal(jax.random.fold_in(jax.random.key(seed), 1), (2, 1024, 128), dtype=_x0.dtype)
    del _x0
    return _d

def reference(L0_attn_x, L0_attn_in_w, L0_attn_conv_w, L0_attn_conv_b, L0_attn_x_proj_w, L0_attn_dt_w, L0_attn_dt_b, L0_attn_A_log, L0_attn_D, L0_attn_out_w, L0_attn_norm_w, L0_ffn_centroids, L0_ffn_ln_g, L0_ffn_ln_b, L0_ffn_w1, L0_ffn_b1, L0_ffn_w2, L0_ffn_b2):

    def _L0_attn_ref(x, in_w, conv_w, conv_b, x_proj_w, dt_w, dt_b, A_log, D, out_w, norm_w):
        import jax, jax.numpy as jnp
        import numpy as np
        D_MODEL = 128
        D_INNER = 256
        D_STATE = 16
        DT_RANK = 64
        D_CONV = 4
        B = 1
        L = 256

        def _forward(x, in_w, conv_w, conv_b, x_proj_w, dt_w, dt_b, A_log, D, out_w, norm_w):
            eps = 1e-05
            h = x * jax.lax.rsqrt(jnp.mean(x * x, axis=-1, keepdims=True) + eps) * norm_w
            xr = h @ in_w
            u, res = jnp.split(xr, 2, axis=-1)
            ut = jnp.transpose(u, (0, 2, 1))
            conv = jax.lax.conv_general_dilated(ut, conv_w, window_strides=(1,), padding=((D_CONV - 1, 0),), feature_group_count=D_INNER, dimension_numbers=('NCH', 'OIH', 'NCH'))
            conv = conv + conv_b[None, :, None]
            u = jax.nn.silu(jnp.transpose(conv, (0, 2, 1)))
            x_dbl = u @ x_proj_w
            dt, Bm, Cm = jnp.split(x_dbl, [DT_RANK, DT_RANK + D_STATE], axis=-1)
            delta = jax.nn.softplus(dt @ dt_w + dt_b)
            A = -jnp.exp(A_log)
            dA = jnp.exp(jnp.einsum('bld,dn->bldn', delta, A))
            dBu = jnp.einsum('bld,bln->bldn', delta * u, Bm)

            def step(s, inp):
                dA_t, dBu_t, C_t = inp
                s = dA_t * s + dBu_t
                y = jnp.einsum('bdn,bn->bd', s, C_t)
                return (s, y)
            s0 = jnp.zeros((x.shape[0], D_INNER, D_STATE), dtype=jnp.float32)
            _, ys = jax.lax.scan(step, s0, (jnp.transpose(dA, (1, 0, 2, 3)), jnp.transpose(dBu, (1, 0, 2, 3)), jnp.transpose(Cm, (1, 0, 2))))
            y = jnp.transpose(ys, (1, 0, 2)) + u * D
            y = y * jax.nn.silu(res)
            return y @ out_w + x
        return _forward(x, in_w, conv_w, conv_b, x_proj_w, dt_w, dt_b, A_log, D, out_w, norm_w)

    def _L0_ffn_ref(input_features, centroids, ln_g, ln_b, w1, b1, w2, b2):
        import jax, jax.numpy as jnp
        import numpy as np
        B, S, D, F, E = (8, 128, 128, 512, 8)
        EPS = 1e-05
        x = input_features.reshape(-1, D)
        aff = jax.lax.stop_gradient(x @ centroids.T)
        eid = jnp.argmax(aff, axis=-1)
        alpha = jax.nn.sigmoid(jnp.sum(x * centroids[eid], axis=-1, keepdims=True))
        mu = jnp.mean(x, axis=-1, keepdims=True)
        var = jnp.mean((x - mu) ** 2, axis=-1, keepdims=True)
        xn = (x - mu) * jax.lax.rsqrt(var + EPS)
        xln = xn * ln_g[eid] + ln_b[eid]
        onehot = jax.nn.one_hot(eid, E, dtype=x.dtype)
        ffn = jnp.zeros_like(x)
        for e in range(E):
            h = jax.nn.relu(xln @ w1[e] + b1[e])
            ffn = ffn + onehot[:, e:e + 1] * (h @ w2[e] + b2[e])
        out = x + alpha * ffn
        return out.reshape(input_features.shape)
    x = L0_attn_x
    x = _layernorm(x + _L0_attn_ref(x, L0_attn_in_w, L0_attn_conv_w, L0_attn_conv_b, L0_attn_x_proj_w, L0_attn_dt_w, L0_attn_dt_b, L0_attn_A_log, L0_attn_D, L0_attn_out_w, L0_attn_norm_w), axis=-1)
    x = _layernorm(x + _L0_ffn_ref(x, L0_ffn_centroids, L0_ffn_ln_g, L0_ffn_ln_b, L0_ffn_w1, L0_ffn_b1, L0_ffn_w2, L0_ffn_b2), axis=-1)
    return x

_drawn_inputs = setup_inputs


def setup_inputs(seed=0):
    import zlib

    import numpy as np

    out = dict(_drawn_inputs(seed))
    spreads = {'L0_attn_conv_b': (0.0, 0.8),
     'L0_attn_D': (1.0, 0.6),
     'L0_attn_norm_w': (1.0, 0.6),
     'L0_ffn_ln_g': (1.0, 0.6),
     'L0_ffn_ln_b': (0.0, 2.0),
     'L0_ffn_b1': (0.0, 0.64),
     'L0_ffn_b2': (0.0, 0.1)}
    factors = {'L0_attn_in_w': 8.0,
     'L0_attn_conv_w': 8.0,
     'L0_attn_x_proj_w': 8.0,
     'L0_attn_dt_w': 8.0,
     'L0_attn_dt_b': 8.0,
     'L0_attn_A_log': 8.0,
     'L0_attn_out_w': 8.0}
    for name, (base, spread) in spreads.items():
        noise = np.random.default_rng([zlib.crc32(name.encode()), seed]).standard_normal(out[name].shape)
        drawn = base * np.exp(spread * noise) if base else spread * noise
        out[name] = jnp.asarray(drawn.astype(out[name].dtype))
    for name, factor in factors.items():
        out[name] = (out[name] * factor).astype(out[name].dtype)
    return out
```

```python
from contextlib import ExitStack

import concourse.bass as bass
from concourse import mybir

ALU = mybir.AluOpType
ACT = mybir.ActivationFunctionType
F32 = mybir.dt.float32
BF16 = mybir.dt.bfloat16
U32 = mybir.dt.uint32
AX_X = mybir.AxisListType.X

P = 128
D_MODEL = 128
D_INNER = 256
D_STATE = 16
DT_RANK = 64
D_CONV = 4
E = 8
F = 512
EPS = 1e-5

T = 512
TT = T // P
H = D_INNER // P
CG = P // D_STATE
NK = 4
NR = P // (CG * NK)
GROUPS = H * NR * NK
PARTS = 3
QROWS = NK * CG

DA_RING = 3
DUX_RING = 2
DBU_RING = 3
S_RING = 5
P_RING = 8
SUM_LAG = 4
FJ = F // P


def fused_mamba_routed_ffn(nc, x, in_wu, in_wr, conv_w, conv_b, x_proj_w, dt_w, dt_b, a_log, d_skip,
                           out_w, norm_w, centroids, w_pack, b2, ident_c, sel_c, sely_c, perm_c,
                           ltri_c, iota8_c, first_c, steps_c, kidx_c, out, xs_dram, ys_dram):
    B, L, _ = x.shape
    CPB = L // T
    NCH = B * CPB
    NT = B * L // P
    NS = NT + E - 1
    NG = NCH * GROUPS
    PACK = w_pack.shape[2]

    x_v = x.rearrange("b (t p) d -> p (b t) d", p=P)
    out_v = out.rearrange("b (t p) d -> p (b t) d", p=P)

    with ExitStack() as ctx:
        def sb(name, shape, dt=F32):
            return ctx.enter_context(nc.sbuf_tensor(name, shape, dt))

        def ps(name, shape, dt=F32):
            return ctx.enter_context(nc.psum_tensor(name, shape, dt))

        def sem(name):
            return ctx.enter_context(nc.semaphore(name))

        dA_ps = ps("dA_ps", [P, DA_RING, T])
        dux_ps = ps("dux_ps", [P, DUX_RING, T])
        y_ps = ps("y_ps", [P, T])
        m_ps = ps("m_ps", [P, 2, T])

        ident = sb("ident", [P, P])
        sel_f = sb("sel_f", [PARTS * QROWS, NK, P])
        sel = sb("sel", [PARTS * QROWS, NK, P], BF16)
        sely = sb("sely", [P, NR, QROWS])
        perm = sb("perm", [P, P])
        dperm = sb("dperm", [P, H, P])
        ltri_f = sb("ltri_f", [P, P])
        ltri = sb("ltri", [P, P], BF16)
        ones_b = sb("ones_b", [P, P], BF16)
        ones_f = sb("ones_f", [1, P])
        zeros = sb("zeros", [P, 8])
        zrow = sb("zrow", [P, P])
        iota8 = sb("iota8", [P, E])
        first = sb("first", [P, E * NT])
        steps = sb("steps", [P, NT])
        kidx = sb("kidx", [P, NS])
        w_u = sb("w_u", [P, D_INNER])
        w_r = sb("w_r", [P, D_INNER])
        w_conv = sb("w_conv", [P, H, D_CONV])
        b_conv = sb("b_conv", [P, H])
        w_xp = sb("w_xp", [P, H, DT_RANK + 2 * D_STATE])
        w_dt = sb("w_dt", [DT_RANK, D_INNER])
        b_dt = sb("b_dt", [P, H])
        a_in = sb("a_in", [P, GROUPS])
        a_exp = sb("a_exp", [P, GROUPS])
        a_neg = sb("a_neg", [P, GROUPS])
        d_in = sb("d_in", [P, H])
        w_out = sb("w_out", [P, H, D_MODEL])
        w_norm = sb("w_norm", [P, 1])
        cent = sb("cent", [P, E])

        x_sb = sb("x_sb", [P, NT, D_MODEL])
        junk = sb("junk", [P, TT, P])
        ss = sb("ss", [P, NT])
        lnss = sb("lnss", [P, NT])
        rms = sb("rms", [P, NT])
        h_sb = sb("h_sb", [P, TT, P])
        hT = sb("hT", [P, T])
        u_raw = sb("u_raw", [P, H, D_CONV - 1 + T])
        u_sb = sb("u_sb", [P, 2, H, T])
        res_raw = sb("res_raw", [P, H, T])
        res_sb = sb("res_sb", [P, 2, H, T])
        xdbl = sb("xdbl", [DT_RANK + 2 * D_STATE, T])
        b_rep = sb("b_rep", [P, 2, T])
        c_rep = sb("c_rep", [P, 2, T])
        dt_abs = sb("dt_abs", [P, H, T])
        dt_pos = sb("dt_pos", [P, H, T])
        delta = sb("delta", [P, 2, H, T])
        du = sb("du", [P, 2, H, T])
        delta_p = sb("delta_p", [P, PARTS, H, T], BF16)
        du_p = sb("du_p", [P, PARTS, H, T], BF16)
        delta_q = sb("delta_q", [PARTS * QROWS, 2, H * NR, T], BF16)
        du_q = sb("du_q", [PARTS * QROWS, 2, H * NR, T], BF16)
        dbu = sb("dbu", [P, DBU_RING, T])
        s_sb = sb("s_sb", [P, S_RING, T])
        carry = sb("carry", [P, GROUPS])
        cs = sb("cs", [P, P_RING, T])
        yg = sb("yg", [P, 2, H, T])
        v_sb = sb("v_sb", [P, TT, P])
        st = sb("st", [P, 2, TT, 6])
        mv = sb("mv", [P, 2, TT, 2])
        lnv = sb("lnv", [P, 2, TT])
        rstd = sb("rstd", [P, 2, TT])
        x1 = sb("x1", [P, NT, P])
        xn = sb("xn", [P, NT, P])
        x1T = sb("x1T", [P, T])
        aff = sb("aff", [P, TT, E])
        top = sb("top", [P, NT, 8])
        topi = sb("topi", [P, TT, 8], U32)
        eid = sb("eid", [P, TT])
        onehot = sb("onehot", [P, NT, E], BF16)

        eps_t = sb("eps_t", [P, 1])
        eps_ap = eps_t[:, 0:1]
        ones8 = sb("ones8", [P, E])
        one_ap = ones8[:, 0:1]
        cnt = sb("cnt", [P, E, NT])
        incl = sb("incl", [P, E, NT])
        rk = sb("rk", [P, E, NT])
        cmp1 = sb("cmp1", [P, E, NT])
        ntile = sb("ntile", [P, E])
        tend = sb("tend", [P, E])
        base = sb("base", [P, E])
        cmp2 = sb("cmp2", [P, NS, E])
        posf = sb("posf", [P, NT])
        pos = sb("pos", [P, NT], U32)
        etf = sb("etf", [P, NS])
        et = sb("et", [P, NS], U32)
        al_e = sb("al_e", [P, NT])
        al_1 = sb("al_1", [P, NT])
        alpha = sb("alpha", [P, NT])
        xs = sb("xs", [P, 2, P])
        wp = sb("wp", [P, 2, PACK])
        b2row = sb("b2row", [1, 2, P])
        xsT = sb("xsT", [P, 2, P])
        hh = delta[:, 0, :, :].rearrange("p b (j d) -> p b j d", d=P)
        ys = du[:, 0, 0, :].rearrange("p (a d) -> p a d", d=P)
        yt = cs[:, 0:NT * P // T, :].rearrange("p a (b d) -> p (a b) d", d=P)
        x1x2, z_sb, o_sb = x_sb, yt, xn
        st3 = sb("st3", [P, NT, 6])
        mv3 = sb("mv3", [P, NT, 2])
        lnv3 = sb("lnv3", [P, NT])
        rstd3 = sb("rstd3", [P, NT])

        s_x_in = sem("x_in")
        s_w_in = sem("w_in")
        s_const_ready = sem("const_ready")
        s_aneg_ready = sem("aneg_ready")
        s_ss_ready = sem("ss_ready")
        s_lnss_ready = sem("lnss_ready")
        s_rms_ready = sem("rms_ready")
        s_h_ready = sem("h_ready")
        s_hT_ps = sem("hT_ps")
        s_hT_ready = sem("hT_ready")
        s_res_ps = sem("res_ps")
        s_res_raw_ready = sem("res_raw_ready")
        s_u_ps = sem("u_ps")
        s_u_raw_ready = sem("u_raw_ready")
        s_u_acc_ready = sem("u_acc_ready")
        s_conv_done = sem("conv_done")
        s_u_ready = sem("u_ready")
        s_res_ready = sem("res_ready")
        s_xdbl_ps = sem("xdbl_ps")
        s_xdbl_ready = sem("xdbl_ready")
        s_bc_ready = sem("bc_ready")
        s_dt_ps = sem("dt_ps")
        s_dt_parts = sem("dt_parts")
        s_dt_exp = sem("dt_exp")
        s_dt_log = sem("dt_log")
        s_delta_ready = sem("delta_ready")
        s_du_ready = sem("du_ready")
        s_part_ready = sem("part_ready")
        s_rest_ready = sem("rest_ready")
        s_parts_in = sem("parts_in")
        s_dlx_ready = sem("dlx_ready")
        s_dA_ready = sem("dA_ready")
        s_dux_ready = sem("dux_ready")
        s_dbu_done = sem("dbu_done")
        s_scan_done = sem("scan_done")
        s_carry_done = sem("carry_done")
        s_cs_ready = sem("cs_ready")
        s_ysum_done = sem("ysum_done")
        s_yg_ready = sem("yg_ready")
        s_out_ps = sem("out_ps")
        s_v_ready = sem("v_ready")
        s_st_done = sem("st_done")
        s_mv_done = sem("mv_done")
        s_lnv_ready = sem("lnv_ready")
        s_rstd_ready = sem("rstd_ready")
        s_x1_ready = sem("x1_ready")
        s_xn_ready = sem("xn_ready")
        s_x1T_ps = sem("x1T_ps")
        s_x1T_ready = sem("x1T_ready")
        s_aff_ps = sem("aff_ps")
        s_aff_ready = sem("aff_ready")
        s_top_ready = sem("top_ready")
        s_topi_ready = sem("topi_ready")
        s_eid_ready = sem("eid_ready")
        s_onehot_ready = sem("onehot_ready")
        s_zfill = sem("zfill")
        s_scattered = sem("scattered")
        s_count_ps = sem("count_ps")
        s_pos_ready = sem("pos_ready")
        s_et_ready = sem("et_ready")
        s_xsT_ps = sem("xsT_ps")
        s_xsT_ready = sem("xsT_ready")
        s_h_ps = sem("h_ps")
        s_hh_ready = sem("hh_ready")
        s_y_e_ps = sem("y_e_ps")
        s_ys_ready = sem("ys_ready")
        s_al_ready = sem("al_ready")
        s_mv3_ready = sem("mv3_ready")
        s_st3_done = sem("st3_done")
        s_o_ready = sem("o_ready")
        s_stored = sem("stored")
        s_a0 = sem("a0")
        s_count_read = sem("count_read")
        s_route = sem("route")
        s_alpha_ready = sem("alpha_ready")
        s_z_ready = sem("z_ready")
        s_x2_ready = sem("x2_ready")
        s_xs_in = [sem(f"xs_in{i}") for i in range(2)]
        s_w_e = [sem(f"w_e{i}") for i in range(2)]
        s_ys_out = [sem(f"ys_out{i}") for i in range(2)]
        s_gathered = [sem(f"gathered{i}") for i in range(4)]

        block = ctx.enter_context(nc.Block())
        N_W = 22

        def buf(g):
            return g % 2

        def tiles(g):
            return slice(TT * g, TT * g + TT)

        @block.sync
        def _(sp):
            for g in range(NCH):
                sp.dma_start(x_sb[:, tiles(g), :], x_v[:, tiles(g), :]).then_inc(s_x_in, 16)
                if g == 0:
                    for dst, src in ((ident, ident_c), (w_u, in_wu), (w_r, in_wr), (w_norm, norm_w),
                                     (w_conv, conv_w), (b_conv, conv_b), (w_xp, x_proj_w), (w_dt, dt_w),
                                     (b_dt, dt_b), (a_in, a_log), (sel_f, sel_c), (sely, sely_c),
                                     (perm, perm_c), (d_in, d_skip), (w_out, out_w), (cent, centroids),
                                     (ltri_f, ltri_c), (iota8, iota8_c), (first, first_c),
                                     (steps, steps_c), (kidx, kidx_c)):
                        sp.dma_start(dst[:], src).then_inc(s_w_in, 16)
            sp.wait_ge(s_const_ready, 1)
            sp.dma_start(xs_dram.rearrange("(n p) d -> p n d", p=P), zrow[:].unsqueeze(1).to_broadcast([P, NS, P])).then_inc(s_zfill, 16)

            def bc(g):
                sp.wait_ge(s_xdbl_ready, g + 1)
                if GROUPS * (g - 1) > 0:
                    sp.wait_ge(s_cs_ready, GROUPS * (g - 1))
                if GROUPS * (g - 1) > 0:
                    sp.wait_ge(s_dbu_done, GROUPS * (g - 1))
                for row, dst in ((DT_RANK, b_rep), (DT_RANK + D_STATE, c_rep)):
                    src = xdbl[row:row + D_STATE, :].unsqueeze(1).to_broadcast([D_STATE, CG, T])
                    sp.dma_start(dst[:, buf(g), :], src).then_inc(s_bc_ready, 16)

            def parts(g):
                if GROUPS * (g - 1) > 0:
                    sp.wait_ge(s_dux_ready, GROUPS * (g - 1))
                for n, (src, dst) in enumerate(((delta_p, delta_q), (du_p, du_q))):
                    for part in range(PARTS):
                        if part < 2:
                            sp.wait_ge(s_part_ready, 4 * g + 2 * n + part + 1)
                        else:
                            sp.wait_ge(s_rest_ready, 4 * g + 2 * n + 2)
                        for r in range(NR):
                            sp.dma_start(dst[part * QROWS:(part + 1) * QROWS, buf(g), r::NR, :],
                                         src[r * QROWS:(r + 1) * QROWS, part, :, :]).then_inc(s_parts_in, 16)

            for g in range(NCH):
                bc(g)
                parts(g)

            sp.wait_ge(s_scattered, 16 * NT)
            sp.wait_ge(s_et_ready, 1)
            for k in range(NS):
                if k - 1 > 0:
                    sp.wait_ge(s_xsT_ps, k - 1)
                sp.dma_start(xs[:, k % 2, :], xs_dram[k * P:(k + 1) * P, :]).then_inc(s_xs_in[k % 2], 16)
                if k - 1 > 0:
                    sp.wait_ge(s_y_e_ps, k - 1)
                e = sp.value_load(et[0:1, k:k + 1], min_val=0, max_val=E - 1)
                sp.dma_start(wp[:, k % 2, :], w_pack[bass.ds(e, 1), :, :].rearrange("e p f -> (e p) f")).then_inc(s_w_e[k % 2], 16)
                sp.dma_start(b2row[:, k % 2, :], b2[bass.ds(e, 1), :]).then_inc(s_w_e[k % 2], 16)
                if k >= 1:
                    if k > 0:
                        sp.wait_ge(s_ys_ready, k)
                    sp.dma_start(ys_dram[(k - 1) * P:k * P, :], ys[:, (k - 1) % 2, :]).then_inc(s_ys_out[(k - 1) % 2], 16)
            sp.wait_ge(s_ys_ready, NS)
            sp.dma_start(ys_dram[(NS - 1) * P:NS * P, :], ys[:, (NS - 1) % 2, :]).then_inc(s_ys_out[(NS - 1) % 2], 16)
            for g in range(NCH):
                sp.wait_ge(s_o_ready, TT * (g + 1))
                sp.dma_start(out_v[:, tiles(g), :], o_sb[:, tiles(g), :]).then_inc(s_stored, 16)
            sp.wait_ge(s_stored, 16 * NCH)

        @block.tensor
        def _(pe):
            mm = nc.tensor.matmul

            def hT_fill(g):
                pe.wait_ge(s_h_ready, g + 1)
                if g - 2 > 0:
                    pe.wait_ge(s_aff_ready, g - 2)
                if 2 * g > 0:
                    pe.wait_ge(s_dt_parts, 2 * g)
                for j in range(TT):
                    last = nc.tensor.transpose(m_ps[:, 0, j * P:(j + 1) * P], h_sb[:, j, :], ident[:])
                last.then_inc(s_hT_ps, 1)

            def res_fill(g, h):
                if h == 0:
                    pe.wait_ge(s_hT_ready, g + 1)
                    if g - 2 > 0:
                        pe.wait_ge(s_x1T_ready, g - 2)
                    if 2 * g - 1 > 0:
                        pe.wait_ge(s_dt_parts, 2 * g - 1)
                mm(m_ps[:, 1 - h, :], w_r[:, h * P:(h + 1) * P], hT[:], start=True, stop=True).then_inc(s_res_ps, 1)

            def u_fill(g, h):
                pe.wait_ge(s_res_raw_ready, 2 * g + h + 1)
                mm(m_ps[:, 1 - h, :], w_u[:, h * P:(h + 1) * P], hT[:], start=True, stop=True).then_inc(s_u_ps, 1)

            def xdbl_fill(g):
                pe.wait_ge(s_u_ready, 2 * g + 2)
                n = DT_RANK + 2 * D_STATE
                for h in range(H):
                    last = mm(m_ps[0:n, 1, :], w_xp[:, h, :], u_sb[:, buf(g), h, :], start=(h == 0), stop=(h == H - 1))
                last.then_inc(s_xdbl_ps, 1)

            def dt_fill(g, h):
                pe.wait_ge(s_xdbl_ready, g + 1)
                if h == 1:
                    if g - 1 > 0:
                        pe.wait_ge(s_v_ready, g - 1)
                mm(m_ps[:, 1 - h, :], w_dt[:, h * P:(h + 1) * P], xdbl[0:DT_RANK, :], start=True, stop=True).then_inc(s_dt_ps, 1)

            def out_fill(g):
                pe.wait_ge(s_yg_ready, H * (g + 1))
                pe.wait_ge(s_u_ready, min(2 * (g + 3), 2 * NCH))
                if g > 0:
                    pe.wait_ge(s_aff_ready, g)
                for j in range(TT):
                    for h in range(H):
                        last = mm(m_ps[:, 0, j * P:(j + 1) * P], yg[:, buf(g), h, j * P:(j + 1) * P], w_out[:, h, :],
                                  start=(h == 0), stop=(h == H - 1))
                last.then_inc(s_out_ps, 1)

            def x1T_fill(g):
                pe.wait_ge(s_x1_ready, g + 1)
                pe.wait_ge(s_dt_parts, min(2 * (g + 3), 2 * NCH) - 1)
                if g > 0:
                    pe.wait_ge(s_aff_ready, g)
                for j in range(TT):
                    last = nc.tensor.transpose(m_ps[:, 1, j * P:(j + 1) * P], x1[:, TT * g + j, :], ident[:])
                last.then_inc(s_x1T_ps, 1)

            def aff_fill(g):
                pe.wait_ge(s_x1T_ready, g + 1)
                pe.wait_ge(s_dt_parts, min(2 * (g + 3), 2 * NCH))
                for j in range(TT):
                    last = mm(m_ps[:, 0, j * E:(j + 1) * E], x1T[:, j * P:(j + 1) * P], cent[:], start=True, stop=True)
                last.then_inc(s_aff_ps, 1)

            def expand(G):
                g, q, k = G // GROUPS, G % GROUPS // NK, G % NK
                if G % GROUPS == 0:
                    pe.wait_ge(s_parts_in, 16 * 2 * PARTS * NR * (g + 1))
                if G - DA_RING + 1 > 0:
                    pe.wait_ge(s_scan_done, G - DA_RING + 1)
                mm(dA_ps[:, G % DA_RING, :], sel[:, k, :], delta_q[:, buf(g), q, :], start=True, stop=True).then_inc(s_dlx_ready, 1)
                if G - DUX_RING + 1 > 0:
                    pe.wait_ge(s_dbu_done, G - DUX_RING + 1)
                mm(dux_ps[:, G % DUX_RING, :], sel[:, k, :], du_q[:, buf(g), q, :], start=True, stop=True).then_inc(s_dux_ready, 1)

            def state_sum(Q):
                g, h, r = Q // (H * NR), Q // NR % H, Q % NR
                if r == 0:
                    if Q // NR > 0:
                        pe.wait_ge(s_yg_ready, Q // NR)
                    mm(y_ps[:], dperm[:, h, :], u_sb[:, buf(g), h, :], start=True, stop=False, skip_group_check=True)
                pe.wait_ge(s_cs_ready, NK * (Q + 1))
                for k in range(NK):
                    last = mm(y_ps[k * QROWS:(k + 1) * QROWS, :], sely[:, r, :], cs[:, (Q * NK + k) % P_RING, :], start=False,
                              stop=(r == NR - 1), skip_group_check=True, tile_position=(0, k * QROWS))
                last.then_inc(s_ysum_done, 1)

            pieces_prep = {0: [hT_fill], 2: [lambda g: res_fill(g, 0)], 3: [lambda g: res_fill(g, 1)], 4: [lambda g: u_fill(g, 0)],
                           5: [lambda g: u_fill(g, 1)], 10: [xdbl_fill], 13: [lambda g: dt_fill(g, 0)], 14: [lambda g: dt_fill(g, 1)]}
            pieces_post = {11: [out_fill], 18: [x1T_fill], 20: [aff_fill]}

            pe.wait_ge(s_w_in, 16 * (N_W - 1))
            pe.wait_ge(s_const_ready, 2)
            for s in sorted(pieces_prep):
                for f in pieces_prep[s]:
                    f(0)
            for G in range(NG):
                g, s = G // GROUPS, G % GROUPS
                expand(G)
                Gs = G - SUM_LAG
                if Gs >= 0 and Gs % NK == NK - 1:
                    state_sum(Gs // NK)
                if g + 1 < NCH:
                    for f in pieces_prep.get(s, []):
                        f(g + 1)
                if g >= 1:
                    for f in pieces_post.get(s, []):
                        f(g - 1)
            state_sum(NG // NK - 1)
            for s in sorted(pieces_post):
                for f in pieces_post[s]:
                    f(NCH - 1)

            pe.wait_ge(s_onehot_ready, NCH)
            oh = onehot[:].rearrange("p t e -> p e t")
            mm(m_ps[:, 1, 0:NT * E], ones_b[:], oh, start=True, stop=True)
            mm(m_ps[:, 1, NT * E:2 * NT * E], ltri[:], oh, start=True, stop=True).then_inc(s_count_ps, 1)

            def ffn_T(k):
                pe.wait_ge(s_xs_in[k % 2], 16 * (k // 2 + 1))
                if k == 0:
                    pe.wait_ge(s_count_read, 2)
                if k > 0:
                    pe.wait_ge(s_xsT_ready, k)
                nc.tensor.transpose(m_ps[:, 1, 0:P], xs[:, k % 2, :], ident[:]).then_inc(s_xsT_ps, 1)

            def ffn_up(k):
                pe.wait_ge(s_xsT_ready, k + 1)
                pe.wait_ge(s_w_e[k % 2], 32 * (k // 2 + 1))
                if FJ * (k - 1) > 0:
                    pe.wait_ge(s_hh_ready, FJ * (k - 1))
                for j in range(FJ):
                    last = mm(dA_ps[:, k % 2, j * P:(j + 1) * P], wp[:, k % 2, j * P:(j + 1) * P], xsT[:, k % 2, :], start=True, stop=True)
                last.then_inc(s_h_ps, 1)

            def ffn_down(k):
                pe.wait_ge(s_hh_ready, FJ * (k + 1))
                if k - 1 > 0:
                    pe.wait_ge(s_ys_ready, k - 1)
                o = dux_ps[:, k % 2, 0:P]
                for j in range(FJ):
                    mm(o, hh[:, k % 2, j, :], wp[:, k % 2, F + j * P:F + (j + 1) * P], start=(j == 0), stop=False)
                mm(o, ones_f[:], b2row[:, k % 2, :], start=False, stop=True).then_inc(s_y_e_ps, 1)

            for k in range(NS + 1):
                if k < NS:
                    ffn_T(k)
                    ffn_up(k)
                if k >= 1:
                    ffn_down(k - 1)

        @block.scalar
        def _(act):
            A = nc.scalar.activation

            def ln_exp():
                nc.scalar.preload_act_table_set("natural_log_exp_and_others")

            def rms_scale(g):
                act.wait_ge(s_x_in, 16 * (g + 1))
                if TT * g > 0:
                    act.wait_ge(s_ss_ready, TT * g)
                for j in range(TT):
                    A(junk[:, j, :], x_sb[:, TT * g + j, :], ACT.Square, accum_out=ss[:, TT * g + j:TT * g + j + 1]).then_inc(s_ss_ready, 1)
                act.wait_ge(s_ss_ready, TT * (g + 1))
                A(lnss[:, tiles(g)], ss[:, tiles(g)], ACT.Ln, scale=1.0 / D_MODEL, bias=eps_ap).then_inc(s_lnss_ready, 1)
                act.wait_ge(s_lnss_ready, g + 1)
                A(rms[:, tiles(g)], lnss[:, tiles(g)], ACT.Exp, scale=-0.5).then_inc(s_rms_ready, 1)
                act.wait_ge(s_rms_ready, g + 1)
                if g > 0:
                    act.wait_ge(s_hT_ps, g)
                if g > 0:
                    act.wait_ge(s_h_ready, g)
                for j in range(TT):
                    last = A(h_sb[:, j, :], x_sb[:, TT * g + j, :], ACT.Copy, scale=rms[:, TT * g + j:TT * g + j + 1])
                last.then_inc(s_h_ready, 1)

            def hT_copy(g):
                act.wait_ge(s_hT_ps, g + 1)
                if 2 * g > 0:
                    act.wait_ge(s_u_ps, 2 * g)
                A(hT[:], m_ps[:, 0, :], ACT.Copy, scale=w_norm[:, 0:1]).then_inc(s_hT_ready, 1)

            def res_copy(g, h):
                act.wait_ge(s_res_ps, 2 * g + h + 1)
                A(res_raw[:, h, :], m_ps[:, 1 - h, :], ACT.Copy).then_inc(s_res_raw_ready, 1)

            def u_copy(g, h):
                act.wait_ge(s_u_ps, 2 * g + h + 1)
                if 6 * g > 0:
                    act.wait_ge(s_conv_done, 6 * g)
                if g % CPB == 0:
                    A(u_raw[:, h, 0:D_CONV - 1], zeros[:, 0:D_CONV - 1], ACT.Copy).then_inc(s_a0, 1)
                else:
                    A(u_raw[:, h, 0:D_CONV - 1], u_raw[:, h, T:T + D_CONV - 1], ACT.Copy).then_inc(s_a0, 1)
                act.wait_ge(s_a0, 2 * g + h + 1)
                A(u_raw[:, h, D_CONV - 1:], m_ps[:, 1 - h, :], ACT.Copy).then_inc(s_u_raw_ready, 1)
                A(m_ps[:, 1 - h, :], m_ps[:, 1 - h, :], ACT.Identity, bias=b_conv[:, h:h + 1], scale=w_conv[:, h, D_CONV - 1:]).then_inc(s_u_acc_ready, 1)

            def silu(g):
                act.wait_ge(s_conv_done, 6 * (g + 1))
                if H * NR * (g - 1) > 0:
                    act.wait_ge(s_ysum_done, H * NR * (g - 1))
                for h in range(H):
                    A(u_sb[:, buf(g), h, :], m_ps[:, 1 - h, :], ACT.Silu).then_inc(s_u_ready, 1)
                if H * (g - 1) > 0:
                    act.wait_ge(s_yg_ready, H * (g - 1))
                act.wait_ge(s_res_raw_ready, 2 * g + 2)
                A(res_sb[:, buf(g), :, :], res_raw[:], ACT.Silu).then_inc(s_res_ready, 1)
                ln_exp()

            def xdbl_copy(g):
                act.wait_ge(s_xdbl_ps, g + 1)
                if 32 * g > 0:
                    act.wait_ge(s_bc_ready, 32 * g)
                if 2 * g > 0:
                    act.wait_ge(s_dt_ps, 2 * g)
                A(xdbl[:], m_ps[0:DT_RANK + 2 * D_STATE, 1, :], ACT.Copy).then_inc(s_xdbl_ready, 1)

            def softplus_in(g, h):
                act.wait_ge(s_dt_ps, 2 * g + h + 1)
                if g > 0:
                    act.wait_ge(s_delta_ready, g)
                A(dt_abs[:, h, :], m_ps[:, 1 - h, :], ACT.Abs, bias=b_dt[:, h:h + 1])
                A(dt_pos[:, h, :], m_ps[:, 1 - h, :], ACT.Relu, bias=b_dt[:, h:h + 1]).then_inc(s_dt_parts, 1)

            def softplus_log(g):
                act.wait_ge(s_dt_parts, 2 * g + 2)
                A(dt_abs[:], dt_abs[:], ACT.Exp, scale=-1.0).then_inc(s_dt_exp, 1)
                act.wait_ge(s_dt_exp, g + 1)
                A(dt_abs[:], dt_abs[:], ACT.Ln, bias=one_ap).then_inc(s_dt_log, 1)

            def cast_part(g, n, part):
                src, parts = ((delta, delta_p), (du, du_p))[n]
                act.wait_ge(s_delta_ready if n == 0 else s_du_ready, g + 1)
                if part:
                    act.wait_ge(s_rest_ready, 4 * g + 2 * n + 1)
                if 16 * 2 * PARTS * NR * g > 0:
                    act.wait_ge(s_parts_in, 16 * 2 * PARTS * NR * g)
                A(parts[:, part, :, :], src[:, part, :, :], ACT.Copy).then_inc(s_part_ready, 1)

            def decay(G):
                act.wait_ge(s_dlx_ready, G + 1)
                A(dA_ps[:, G % DA_RING, :], dA_ps[:, G % DA_RING, :], ACT.Exp, scale=a_neg[:, G % GROUPS:G % GROUPS + 1]).then_inc(s_dA_ready, 1)

            def keep_state(G):
                if G >= 0 and G // GROUPS % CPB < CPB - 1:
                    act.wait_ge(s_scan_done, G + 1)
                    A(carry[:, G % GROUPS:G % GROUPS + 1], s_sb[:, G % S_RING, T - 1:T], ACT.Copy).then_inc(s_carry_done, 1)

            def rstd_of(g, n):
                act.wait_ge(s_mv_done, TT * (2 * g + n + 1))
                A(lnv[:, n, :], mv[:, n, :, 1], ACT.Ln, bias=eps_ap).then_inc(s_lnv_ready, 1)
                act.wait_ge(s_lnv_ready, 2 * g + n + 1)
                A(rstd[:, n, :], lnv[:, n, :], ACT.Exp, scale=-0.5).then_inc(s_rstd_ready, 1)

            def x1T_copy(g):
                act.wait_ge(s_x1T_ps, g + 1)
                if g > 0:
                    act.wait_ge(s_aff_ps, g)
                A(x1T[:], m_ps[:, 1, :], ACT.Copy).then_inc(s_x1T_ready, 1)

            pieces_prep = {0: [rms_scale], 1: [hT_copy], 2: [lambda g: res_copy(g, 0)], 3: [lambda g: res_copy(g, 1)],
                           4: [lambda g: u_copy(g, 0)], 5: [lambda g: u_copy(g, 1)], 9: [silu], 11: [xdbl_copy],
                           14: [lambda g: softplus_in(g, 0)], 15: [lambda g: softplus_in(g, 1)], 16: [softplus_log],
                           18: [lambda g: cast_part(g, 0, 0)], 20: [lambda g: cast_part(g, 0, 1)],
                           21: [lambda g: cast_part(g, 1, 0)], 23: [lambda g: cast_part(g, 1, 1)]}
            pieces_post = {13: [lambda g: rstd_of(g, 0)], 17: [lambda g: rstd_of(g, 1)], 19: [x1T_copy]}

            ln_exp()
            act.wait_ge(s_const_ready, 1)
            act.wait_ge(s_w_in, 16 * (N_W - 1))
            A(a_exp[:], a_in[:], ACT.Exp).then_inc(s_aneg_ready, 1)
            for s in sorted(pieces_prep):
                for f in pieces_prep[s]:
                    f(0)
            act.wait_ge(s_aneg_ready, 2)
            for G in range(NG):
                g, s = G // GROUPS, G % GROUPS
                decay(G)
                keep_state(G - DA_RING)
                if g + 1 < NCH:
                    for f in pieces_prep.get(s, []):
                        f(g + 1)
                if g >= 1:
                    for f in pieces_post.get(s, []):
                        f(g - 1)
            for s in sorted(pieces_post):
                for f in pieces_post[s]:
                    f(NCH - 1)
            act.wait_ge(s_top_ready, TT * NCH)
            A(al_e[:], top[:, :, 0], ACT.Exp, scale=-1.0).then_inc(s_al_ready, 1)

            for k in range(NS):
                act.wait_ge(s_xsT_ps, k + 1)
                act.wait_ge(s_w_e[k % 2], 32 * (k // 2 + 1))
                if k - 1 > 0:
                    act.wait_ge(s_h_ps, k - 1)
                A(xsT[:, k % 2, :], m_ps[:, 1, 0:P], ACT.Identity, scale=wp[:, k % 2, 2 * F + FJ:2 * F + FJ + 1],
                  bias=wp[:, k % 2, 2 * F + FJ + 1:2 * F + FJ + 2]).then_inc(s_xsT_ready, 1)
                act.wait_ge(s_h_ps, k + 1)
                if k - 1 > 0:
                    act.wait_ge(s_y_e_ps, k - 1)
                for j in range(FJ):
                    A(hh[:, k % 2, j, :], dA_ps[:, k % 2, j * P:(j + 1) * P], ACT.Relu,
                      bias=wp[:, k % 2, 2 * F + j:2 * F + j + 1]).then_inc(s_hh_ready, 1)
            act.wait_ge(s_mv3_ready, NT)
            A(lnv3[:], mv3[:, :, 1], ACT.Ln, bias=eps_ap).then_inc(s_al_ready, 1)
            act.wait_ge(s_al_ready, 2)
            A(rstd3[:], lnv3[:], ACT.Exp, scale=-0.5).then_inc(s_al_ready, 1)


        @block.vector
        def _(dve):
            V = nc.vector

            def taps(g, h):
                dve.wait_ge(s_u_acc_ready, 2 * g + h + 1)
                for k in range(D_CONV - 1):
                    if k:
                        if 6 * g + 3 * h + k > 0:
                            dve.wait_ge(s_conv_done, 6 * g + 3 * h + k)
                    V.scalar_tensor_tensor(out=m_ps[:, 1 - h, :], in0=u_raw[:, h, k:k + T], scalar=w_conv[:, h, k:k + 1],
                                           in1=m_ps[:, 1 - h, :], op0=ALU.mult, op1=ALU.add).then_inc(s_conv_done, 1)

            def make_delta(g):
                dve.wait_ge(s_dt_log, g + 1)
                if 4 * g > 0:
                    dve.wait_ge(s_rest_ready, 4 * g)
                if g > 0:
                    dve.wait_ge(s_du_ready, g)
                if 4 * g > 0:
                    dve.wait_ge(s_part_ready, 4 * g)
                V.tensor_tensor(delta[:, 0, :, :], dt_pos[:], dt_abs[:], ALU.add).then_inc(s_delta_ready, 1)

            def make_du(g):
                dve.wait_ge(s_delta_ready, g + 1)
                dve.wait_ge(s_u_ready, 2 * g + 2)
                V.tensor_tensor(du[:, 0, :, :], delta[:, 0, :, :], u_sb[:, buf(g), :, :], ALU.mult).then_inc(s_du_ready, 1)

            def dbu_of(G):
                if G >= NG:
                    return
                g = G // GROUPS
                dve.wait_ge(s_dux_ready, G + 1)
                if G - DBU_RING + 1 > 0:
                    dve.wait_ge(s_scan_done, G - DBU_RING + 1)
                if G % GROUPS == 0:
                    dve.wait_ge(s_bc_ready, 32 * (g + 1))
                V.tensor_tensor(dbu[:, G % DBU_RING, :], b_rep[:, buf(g), :], dux_ps[:, G % DUX_RING, :], ALU.mult).then_inc(s_dbu_done, 1)

            def scan(G):
                g, n = G // GROUPS, G % GROUPS
                dve.wait_ge(s_dA_ready, G + 1)
                dve.wait_ge(s_dbu_done, G + 1)
                if G - S_RING + 1 > 0:
                    dve.wait_ge(s_cs_ready, G - S_RING + 1)
                if G >= S_RING:
                    Gp = G - S_RING
                    kept = sum(1 for i in range(Gp + 1) if i // GROUPS % CPB < CPB - 1)
                    if kept > 0:
                        dve.wait_ge(s_carry_done, kept)
                init = 0.0
                if g % CPB:
                    if g // CPB * GROUPS * (CPB - 1) + (g % CPB - 1) * GROUPS + n + 1 > 0:
                        dve.wait_ge(s_carry_done, g // CPB * GROUPS * (CPB - 1) + (g % CPB - 1) * GROUPS + n + 1)
                    init = carry[:, n:n + 1]
                V.tensor_tensor_scan(s_sb[:, G % S_RING, :], dA_ps[:, G % DA_RING, :], dbu[:, G % DBU_RING, :], init,
                                     ALU.mult, ALU.add).then_inc(s_scan_done, 1)

            def gate(Hi):
                g, h = Hi // H, Hi % H
                dve.wait_ge(s_ysum_done, NR * (Hi + 1))
                dve.wait_ge(s_res_ready, g + 1)
                if g - 1 > 0:
                    dve.wait_ge(s_out_ps, g - 1)
                V.tensor_tensor(yg[:, buf(g), h, :], res_sb[:, buf(g), h, :], y_ps[:], ALU.mult).then_inc(s_yg_ready, 1)

            def residual(g):
                dve.wait_ge(s_out_ps, g + 1)
                V.scalar_tensor_tensor(out=v_sb[:], in0=x_sb[:, tiles(g), :], scalar=2.0,
                                       in1=m_ps[:, 0, :].rearrange("p (t d) -> p t d", t=TT), op0=ALU.mult, op1=ALU.add).then_inc(s_v_ready, 1)

            def stats(g, n):
                dve.wait_ge(s_v_ready if n == 0 else s_x1_ready, g + 1)
                for j in range(TT):
                    V.bn_stats(st[:, n, j, :], v_sb[:, j, :] if n == 0 else x1[:, TT * g + j, :]).then_inc(s_st_done, 1)
                for j in range(TT):
                    dve.wait_ge(s_st_done, TT * (2 * g + n) + j + 1)
                    V.bn_aggr(mv[:, n, j, :], st[:, n, j, :]).then_inc(s_mv_done, 1)

            def normed(g, n):
                dve.wait_ge(s_rstd_ready, 2 * g + n + 1)
                for j in range(TT):
                    t = TT * g + j
                    o, i = (x1[:, t, :], v_sb[:, j, :]) if n == 0 else (xn[:, t, :], x1[:, t, :])
                    last = V.tensor_scalar(o, i, mv[:, n, j, 0:1], rstd[:, n, j:j + 1], ALU.subtract, ALU.mult)
                last.then_inc(s_x1_ready if n == 0 else s_xn_ready, 1)

            def route_tokens(g):
                dve.wait_ge(s_aff_ps, g + 1)
                V.tensor_copy(aff[:], m_ps[:, 0, 0:TT * E].rearrange("p (t e) -> p t e", t=TT)).then_inc(s_aff_ready, 1)
                dve.wait_ge(s_aff_ready, g + 1)
                for j in range(TT):
                    V.max(top[:, TT * g + j, :], aff[:, j, :]).then_inc(s_top_ready, 1)
                for j in range(TT):
                    dve.wait_ge(s_top_ready, TT * g + j + 1)
                    V.max_index(topi[:, j, :], top[:, TT * g + j, :], aff[:, j, :]).then_inc(s_topi_ready, 1)
                dve.wait_ge(s_topi_ready, TT * (g + 1))
                V.tensor_copy(eid[:], topi[:, :, 0]).then_inc(s_eid_ready, 1)
                dve.wait_ge(s_eid_ready, g + 1)
                V.tensor_tensor(onehot[:, tiles(g), :], iota8[:].unsqueeze(1).to_broadcast([P, TT, E]),
                                eid[:].unsqueeze(2).to_broadcast([P, TT, E]), ALU.is_equal).then_inc(s_onehot_ready, 1)

            V.memset(zeros[:], 0.0)
            V.memset(zrow[:], 0.0)
            V.memset(eps_t[:], EPS)
            V.memset(ones8[:], 1.0)
            V.memset(ones_f[:], 1.0)
            V.memset(ones_b[:], 1.0).then_inc(s_const_ready, 1)
            dve.wait_ge(s_w_in, 16 * (N_W - 1))
            V.tensor_copy(sel[:], sel_f[:])
            V.tensor_copy(ltri[:], ltri_f[:])
            for h in range(H):
                last = V.tensor_scalar(dperm[:, h, :], perm[:], d_in[:, h:h + 1], None, ALU.mult)
            last.then_inc(s_const_ready, 1)
            dve.wait_ge(s_aneg_ready, 1)
            V.tensor_scalar(a_neg[:], a_exp[:], -1.0, None, ALU.mult).then_inc(s_aneg_ready, 1)

            pieces_prep = {7: [lambda g: taps(g, 0)], 8: [lambda g: taps(g, 1)], 18: [make_delta], 19: [make_du]}
            pieces_post = {12: [residual, lambda g: stats(g, 0)], 15: [lambda g: normed(g, 0), lambda g: stats(g, 1)],
                           19: [lambda g: normed(g, 1)], 22: [route_tokens]}
            for s in sorted(pieces_prep):
                for f in pieces_prep[s]:
                    f(0)
            dbu_of(0)
            for G in range(NG):
                g, s = G // GROUPS, G % GROUPS
                dbu_of(G + 1)
                scan(G)
                Gs = G - SUM_LAG - 2
                if Gs >= 0 and (Gs + 1) % (NK * NR) == 0:
                    gate(Gs // (NK * NR))
                if g + 1 < NCH:
                    for f in pieces_prep.get(s, []):
                        f(g + 1)
                if g >= 1:
                    for f in pieces_post.get(s, []):
                        f(g - 1)
            gate(NCH * H - 1)
            for s in sorted(pieces_post):
                for f in pieces_post[s]:
                    f(NCH - 1)

            n_route = [0]

            def routed(ins):
                n_route[0] += 1
                ins.then_inc(s_route, 1)
                dve.wait_ge(s_route, n_route[0])

            flat = lambda t: t[:].rearrange("p a b -> p (a b)")
            dve.wait_ge(s_count_ps, 1)
            V.tensor_copy(flat(cnt), m_ps[:, 1, 0:NT * E]).then_inc(s_count_read, 1)
            V.tensor_copy(flat(rk), m_ps[:, 1, NT * E:2 * NT * E]).then_inc(s_count_read, 1)
            dve.wait_ge(s_count_read, 2)
            routed(V.tensor_tensor_scan(flat(incl), first[:], flat(cnt), 0.0, ALU.mult, ALU.add))
            routed(V.tensor_tensor(rk[:], rk[:], incl[:], ALU.add))
            routed(V.tensor_tensor(rk[:], rk[:], cnt[:], ALU.subtract))
            routed(V.tensor_tensor(cmp1[:], incl[:, :, NT - 1:NT].to_broadcast([P, E, NT]),
                                   steps[:].unsqueeze(1).to_broadcast([P, E, NT]), ALU.is_gt))
            routed(V.tensor_reduce(ntile[:], cmp1[:], AX_X, ALU.add))
            routed(V.tensor_tensor_scan(tend[:], ones8[:], ntile[:], 0.0, ALU.mult, ALU.add))
            routed(V.tensor_tensor(base[:], tend[:], ntile[:], ALU.subtract))
            routed(V.scalar_tensor_tensor(out=rk[:], in0=base[:].unsqueeze(2).to_broadcast([P, E, NT]), scalar=float(P),
                                          in1=rk[:], op0=ALU.mult, op1=ALU.add))
            routed(V.tensor_tensor(cmp1[:], rk[:], onehot[:].rearrange("p t e -> p e t"), ALU.mult))
            routed(V.tensor_reduce(posf[:], cmp1[:].rearrange("p e t -> p t e"), AX_X, ALU.add))
            V.tensor_copy(pos[:], posf[:]).then_inc(s_pos_ready, 1)
            routed(V.tensor_tensor(cmp2[:], kidx[:].unsqueeze(2).to_broadcast([P, NS, E]),
                                   tend[:].unsqueeze(1).to_broadcast([P, NS, E]), ALU.is_ge))
            routed(V.tensor_reduce(etf[:], cmp2[:], AX_X, ALU.add))
            V.tensor_scalar(et[:], etf[:], float(E - 1), None, ALU.min).then_inc(s_et_ready, 1)
            dve.wait_ge(s_al_ready, 1)
            routed(V.tensor_scalar(al_1[:], al_e[:], 1.0, None, ALU.add))
            V.reciprocal(alpha[:], al_1[:]).then_inc(s_alpha_ready, 1)
            V.tensor_scalar(x1x2[:], x1[:], 2.0, None, ALU.mult).then_inc(s_x2_ready, 1)

            for k in range(NS):
                dve.wait_ge(s_y_e_ps, k + 1)
                if 16 * (k // 2) > 0:
                    dve.wait_ge(s_ys_out[k % 2], 16 * (k // 2))
                V.tensor_copy(ys[:, k % 2, :], dux_ps[:, k % 2, 0:P]).then_inc(s_ys_ready, 1)

            dve.wait_ge(s_alpha_ready, 1)
            dve.wait_ge(s_x2_ready, 1)
            for t in range(NT):
                dve.wait_ge(s_gathered[t // TT], 16 * TT)
                V.scalar_tensor_tensor(out=z_sb[:, t, :], in0=yt[:, t, :], scalar=alpha[:, t:t + 1], in1=x1x2[:, t, :],
                                       op0=ALU.mult, op1=ALU.add).then_inc(s_z_ready, 1)
                dve.wait_ge(s_z_ready, t + 1)
                V.bn_stats(st3[:, t, :], z_sb[:, t, :]).then_inc(s_st3_done, 1)
            for t in range(NT):
                dve.wait_ge(s_st3_done, t + 1)
                V.bn_aggr(mv3[:, t, :], st3[:, t, :]).then_inc(s_mv3_ready, 1)
            dve.wait_ge(s_al_ready, 3)
            for t in range(NT):
                V.tensor_scalar(o_sb[:, t, :], z_sb[:, t, :], mv3[:, t, 0:1], rstd3[:, t:t + 1], ALU.subtract,
                                ALU.mult).then_inc(s_o_ready, 1)

        @block.gpsimd
        def _(pool):
            G_ = nc.gpsimd

            def rest(g, n, part):
                src, parts = ((delta, delta_p), (du, du_p))[n]
                pool.wait_ge(s_part_ready, 4 * g + 2 * n + part + 1)
                flat = lambda t, i: t[:, i, :, :].rearrange("p h t -> p (h t)")
                dst = flat(src, 1) if part == 0 else flat(parts, 2)
                if part:
                    pool.wait_ge(s_rest_ready, 4 * g + 2 * n + 1)
                    if 16 * 2 * PARTS * NR * g > 0:
                        pool.wait_ge(s_parts_in, 16 * 2 * PARTS * NR * g)
                G_.tensor_tensor(dst, flat(src, part), flat(parts, part), ALU.subtract).then_inc(s_rest_ready, 1)

            def c_times_s(G):
                g = G // GROUPS
                pool.wait_ge(s_scan_done, G + 1)
                if G % GROUPS == 0:
                    pool.wait_ge(s_bc_ready, 32 * (g + 1))
                if G // NK - P_RING // NK + 1 > 0:
                    pool.wait_ge(s_ysum_done, G // NK - P_RING // NK + 1)
                G_.tensor_tensor(cs[:, G % P_RING, :], s_sb[:, G % S_RING, :], c_rep[:, buf(g), :], ALU.mult).then_inc(s_cs_ready, 1)

            pieces = {20: [lambda g: rest(g, 0, 0)], 21: [lambda g: rest(g, 0, 1)], 22: [lambda g: rest(g, 1, 0)],
                      23: [lambda g: rest(g, 1, 1)]}
            for s in sorted(pieces):
                for f in pieces[s]:
                    f(0)
            for G in range(NG):
                g, s = G // GROUPS, G % GROUPS
                c_times_s(G)
                if g + 1 < NCH:
                    for f in pieces.get(s, []):
                        f(g + 1)
            pool.wait_ge(s_pos_ready, 1)
            pool.wait_ge(s_zfill, 16)
            pool.wait_ge(s_xn_ready, NCH)
            for t in range(NT):
                G_.indirect_dma_start(xs_dram, bass.IndirectOffsetOnAxis(ap=pos[:, t:t + 1], axis=0), xn[:, t, :], None).then_inc(s_scattered, 16)
            pool.wait_ge(s_ys_out[0], 16 * ((NS + 1) // 2))
            pool.wait_ge(s_ys_out[1], 16 * (NS // 2))
            for t in range(NT):
                G_.indirect_dma_start(yt[:, t, :], None, ys_dram, bass.IndirectOffsetOnAxis(ap=pos[:, t:t + 1], axis=0)).then_inc(s_gathered[t // TT], 16)


def kernel(**inputs):
    import numpy as np
    import concourse.bacc as bacc
    from concourse.bass_utils import run_bass_kernel_spmd

    a = {k: np.asarray(v) for k, v in inputs.items()}
    B, L, D = a["L0_attn_x"].shape
    NT = B * L // P
    NS = NT + E - 1
    y_order = np.arange(P).reshape(NR, NK, CG).transpose(1, 0, 2).reshape(-1)
    in_w = a["L0_attn_in_w"]
    w_r = in_w[:, D_INNER:].reshape(D, H, P)[:, :, y_order].reshape(D, D_INNER)
    w_out = a["L0_attn_out_w"].reshape(H, P, D)[:, y_order, :].transpose(1, 0, 2)
    by_half = lambda v: v.reshape(H, P, -1).transpose(1, 0, 2)
    a_log = a["L0_attn_A_log"].reshape(H, NR, NK, CG, D_STATE).transpose(4, 3, 0, 1, 2).reshape(P, GROUPS)
    w2 = a["L0_ffn_w2"].reshape(E, FJ, P, D).transpose(0, 2, 1, 3).reshape(E, P, FJ * D)
    b1 = a["L0_ffn_b1"].reshape(E, FJ, P).transpose(0, 2, 1)
    w_pack = np.concatenate([a["L0_ffn_w1"], w2, b1, a["L0_ffn_ln_g"][:, :, None], a["L0_ffn_ln_b"][:, :, None]], axis=2)
    sel = np.zeros((PARTS, NK, CG, NK, D_STATE, CG), np.float32)
    for k in range(NK):
        for i in range(CG):
            sel[:, k, i, k, :, i] = 1
    sely = np.zeros((D_STATE, CG, NR, NR, CG), np.float32)
    for r in range(NR):
        for i in range(CG):
            sely[:, i, r, r, i] = 1
    perm = np.zeros((P, P), np.float32)
    perm[y_order, np.arange(P)] = 1
    rows = lambda v: np.broadcast_to(v.astype(np.float32), (P, v.size))
    first = np.ones((E, NT), np.float32)
    first[:, 0] = 0
    arrays = {
        "x": a["L0_attn_x"], "in_wu": in_w[:, :D_INNER], "in_wr": w_r,
        "conv_w": by_half(a["L0_attn_conv_w"]), "conv_b": by_half(a["L0_attn_conv_b"])[:, :, 0],
        "x_proj_w": by_half(a["L0_attn_x_proj_w"]), "dt_w": a["L0_attn_dt_w"],
        "dt_b": by_half(a["L0_attn_dt_b"])[:, :, 0], "a_log": a_log, "d_skip": by_half(a["L0_attn_D"])[:, :, 0],
        "out_w": w_out, "norm_w": a["L0_attn_norm_w"][:, None], "centroids": a["L0_ffn_centroids"].T,
        "w_pack": w_pack, "b2": a["L0_ffn_b2"],
        "ident_c": np.eye(P, dtype=np.float32), "sel_c": sel.reshape(PARTS * QROWS, NK, P),
        "sely_c": sely.reshape(P, NR, QROWS), "perm_c": perm, "ltri_c": np.triu(np.ones((P, P), np.float32), 1),
        "iota8_c": rows(np.arange(E)), "first_c": rows(first.reshape(-1)), "steps_c": rows(P * np.arange(NT)),
        "kidx_c": rows(np.arange(NS)),
    }
    nc = bacc.Bacc("TRN2", target_bir_lowering=False, num_devices=1)
    feed, args = {}, []
    for name, v in arrays.items():
        v = np.ascontiguousarray(v)
        feed[f"in_{name}"] = v
        args.append(nc.dram_tensor(f"in_{name}", v.shape, mybir.dt.from_np(v.dtype), kind="ExternalInput").ap())
    args.append(nc.dram_tensor("out_0", (B, L, D), F32, kind="ExternalOutput").ap())
    args.append(nc.dram_tensor("xs_dram", (NS * P, D), F32, kind="Internal").ap())
    args.append(nc.dram_tensor("ys_dram", (NS * P, D), F32, kind="Internal").ap())
    fused_mamba_routed_ffn(nc, *args)
    r = run_bass_kernel_spmd(nc, [feed], core_ids=[0])
    return r.results[0]["out_0"]
```

```python
from contextlib import ExitStack

import concourse.bass as bass
from concourse import mybir

ALU = mybir.AluOpType
ACT = mybir.ActivationFunctionType
F32 = mybir.dt.float32
BF16 = mybir.dt.bfloat16
U32 = mybir.dt.uint32
AX_X = mybir.AxisListType.X

P = 128
D_MODEL = 128
D_INNER = 256
D_STATE = 16
DT_RANK = 64
D_CONV = 4
E = 8
F = 512
EPS = 1e-5

T = 512
TT = T // P
H = D_INNER // P
CG = P // D_STATE
NK = 4
NR = P // (CG * NK)
GROUPS = H * NR * NK
PARTS = 3
QROWS = NK * CG

DA_RING = 3
DUX_RING = 2
DBU_RING = 3
S_RING = 8
P_RING = 8
SUM_LAG = 4
FJ = F // P
ROW = D_MODEL + 2
W_ROW = 2 * F + FJ + 3
XS_RING = 6
W_RING = 5
XN_RING = 4
XT_RING = 3
H_RING = 3
Z_RING = 8


def fused_mamba_routed_ffn(nc, x, in_w, x_proj_w, dt_w, out_w, small, w_pack, ident_c, sel_c, route_c, tok_c, consts, out, xs_dram):
    B, L, _ = x.shape
    CPB = L // T
    NCH = B * CPB
    NT = B * L // P
    NS = NT + E - 1
    NG = NCH * GROUPS
    REGION = B * L + 2 * P
    N_TOK = B * L

    x_v = x.rearrange("b (t p) d -> p (b t) d", p=P)
    out_rows = out.rearrange("b t d -> (b t) d")

    with ExitStack() as ctx:
        def sb(name, shape, dt=F32):
            return ctx.enter_context(nc.sbuf_tensor(name, shape, dt))

        def ps(name, shape, dt=F32):
            return ctx.enter_context(nc.psum_tensor(name, shape, dt))

        def sem(name):
            return ctx.enter_context(nc.semaphore(name))

        dA_ps = ps("dA_ps", [P, DA_RING, T])
        dux_ps = ps("dux_ps", [P, DUX_RING, T])
        y_ps = ps("y_ps", [P, T])
        m_ps = ps("m_ps", [P, 2, T])

        ident = sb("ident", [P, P])
        sel_f = sb("sel_f", [PARTS * QROWS, NK, P])
        sel = sb("sel", [PARTS * QROWS, NK, P], BF16)
        const_sb = sb("const_sb", [P, consts.shape[1]])
        sely = const_sb[:, 0:NR * QROWS].rearrange("p (r m) -> p r m", r=NR)
        perm = const_sb[:, P:2 * P]
        ltri_f = const_sb[:, 2 * P:3 * P]
        route_sb = sb("route_sb", [P, route_c.shape[1]])
        o_ = [0]

        def view(t, n):
            o_[0] += n
            return t[:, o_[0] - n:o_[0]]

        iota8 = view(route_sb, E)
        steps = view(route_sb, NT)
        kidx = view(route_sb, NS)
        region0 = view(route_sb, E)
        region_b = sb("region_b", [1, TT, E], BF16)
        tok = sb("tok", [P, NT + 1], U32)
        dperm = sb("dperm", [P, H, P])
        ltri = sb("ltri", [P, P], BF16)
        ones_b = sb("ones_b", [P, P], BF16)
        ones_f = sb("ones_f", [P, P])
        zeros = sb("zeros", [P, 8])
        zrow = sb("zrow", [P, 2, ROW])
        w_in = sb("w_in", [P, 2 * D_INNER])
        w_r, w_u = w_in[:, 0:D_INNER], w_in[:, D_INNER:2 * D_INNER]
        w_xp = sb("w_xp", [P, H, DT_RANK + 2 * D_STATE])
        w_dt = sb("w_dt", [DT_RANK, D_INNER])
        w_out = sb("w_out", [P, H, D_MODEL])
        small_sb = sb("small_sb", [P, small.shape[1]])
        o_[0] = 0
        w_norm = view(small_sb, 1)
        w_conv = view(small_sb, H * D_CONV).rearrange("p (h k) -> p h k", h=H)
        b_conv = view(small_sb, H)
        b_dt = view(small_sb, H)
        d_in = view(small_sb, H)
        a_in = view(small_sb, GROUPS)
        cent = view(small_sb, E)
        a_exp = sb("a_exp", [P, GROUPS])
        a_neg = sb("a_neg", [P, GROUPS])

        x_sb = sb("x_sb", [P, NT, D_MODEL])
        junk = sb("junk", [P, TT, P])
        ss = sb("ss", [P, NT])
        lnss = sb("lnss", [P, NT])
        rms = sb("rms", [P, NT])
        h_sb = sb("h_sb", [P, TT, P])
        hT = sb("hT", [P, T])
        u_raw = sb("u_raw", [P, H, D_CONV - 1 + T])
        late = sb("late", [P, 2, 2, H, T])
        u_sb, yg = late[:, 0, :, :, :], late[:, 1, :, :, :]
        res_raw = sb("res_raw", [P, H, T])
        res_sb = sb("res_sb", [P, 2, H, T])
        xdbl = sb("xdbl", [DT_RANK + 2 * D_STATE, T])
        b_rep = sb("b_rep", [P, 2, T])
        c_rep = sb("c_rep", [P, 2, T])
        early = sb("early", [P, 6, H, T])
        delta, du = early[:, 0:2, :, :], early[:, 2:4, :, :]
        dt_abs, dt_pos = early[:, 4, :, :], early[:, 5, :, :]
        delta_p = sb("delta_p", [P, PARTS, H, T], BF16)
        du_p = sb("du_p", [P, PARTS, H, T], BF16)
        delta_q = sb("delta_q", [PARTS * QROWS, 2, H * NR, T], BF16)
        du_q = sb("du_q", [PARTS * QROWS, 2, H * NR, T], BF16)
        dbu = sb("dbu", [P, DBU_RING, T])
        s_sb = sb("s_sb", [P, S_RING, T])
        carry = sb("carry", [P, GROUPS])
        cs = sb("cs", [P, P_RING, T])
        v_sb = sb("v_sb", [P, TT, P])
        st = sb("st", [P, TT, 6])
        mv = sb("mv", [P, TT, 2])
        lnv = sb("lnv", [P, TT])
        rstd = sb("rstd", [P, TT])
        rows = sb("rows", [P, NT, ROW])
        x2 = rows[:, :, 0:D_MODEL]
        x1T = sb("x1T", [P, T])
        aff = sb("aff", [P, TT, E])
        top = sb("top", [P, NT, 8])
        topi = sb("topi", [P, TT, 8], U32)
        eid = sb("eid", [P, TT])
        onehot = sb("onehot", [P, NT, E], BF16)

        eps_t = sb("eps_t", [P, 1])
        eps_ap = eps_t[:, 0:1]
        eps4_t = sb("eps4_t", [P, 1])
        eps4_ap = eps4_t[:, 0:1]
        epsq_t = sb("epsq_t", [P, 1])
        epsq_ap = epsq_t[:, 0:1]
        ones8 = sb("ones8", [P, E])
        one_ap = ones8[:, 0:1]
        al_e = sb("al_e", [P, TT])
        al_1 = sb("al_1", [P, TT])
        rank = sb("rank", [P, TT, E])
        posf = sb("posf", [P, TT])
        pos = sb("pos", [P, NT], U32)
        cnt = sb("cnt", [P, E])
        fill_row = sb("fill_row", [P, E], U32)
        past = sb("past", [P, E, NT])
        ntile = sb("ntile", [P, E])
        tend = sb("tend", [P, E])
        jump = sb("jump", [P, E])
        lim = sb("lim", [P, 1])
        beyond = sb("beyond", [P, NS, E])
        etf = sb("etf", [P, NS])
        et = sb("et", [P, NS], U32)
        jumps = sb("jumps", [P, NS, E])
        rowf = sb("rowf", [P, NS])
        row0 = sb("row0", [P, NS], U32)
        flat = lambda t: t.rearrange("p a b c -> p (a b c)")
        xs = cs[:].rearrange("p a t -> p (a t)")[:, 0:NS * ROW].rearrange("p (k d) -> p k d", d=ROW)
        wp = flat(early[:])[:, 0:W_RING * W_ROW].rearrange("p (k f) -> p k f", f=W_ROW)
        s_flat = s_sb[:].rearrange("p a t -> p (a t)")
        hh = s_flat[:, 0:H_RING * F].rearrange("p (k j d) -> p k j d", k=H_RING, d=P)
        s_off = H_RING * F
        xn = s_flat[:, s_off:s_off + XN_RING * P].rearrange("p (k d) -> p k d", d=P)
        s_off += XN_RING * P
        xsT = s_flat[:, s_off:s_off + XT_RING * P].rearrange("p (k d) -> p k d", d=P)
        s_off += XT_RING * P
        b2d = s_flat[:, s_off:s_off + H_RING * P].rearrange("p (k d) -> p k d", d=P)
        z = dbu[:].rearrange("p a t -> p (a t)")[:, 0:Z_RING * P].rearrange("p (k d) -> p k d", d=P)
        o_sb = late[:].rearrange("p a b c t -> p (a b c t)")[:, 0:NS * P].rearrange("p (k d) -> p k d", d=P)
        st_i = sb("st_i", [P, NS, 6])
        mv_i = sb("mv_i", [P, NS, 2])
        ln_i = sb("ln_i", [P, NS])
        rstd_i = sb("rstd_i", [P, NS])
        st_o = sb("st_o", [P, NS, 6])
        mv_o = sb("mv_o", [P, NS, 2])
        ln_o = sb("ln_o", [P, NS])
        rstd_o = sb("rstd_o", [P, NS])

        s_x_in = [sem(f"x_in{g}") for g in range(NCH)]
        s_ident_in = sem("ident_in")
        s_in_w_in = sem("in_w_in")
        s_small_in = sem("small_in")
        s_xp_in = sem("xp_in")
        s_dt_in = sem("dt_in")
        s_sel_in = sem("sel_in")
        s_late_in = sem("late_in")
        s_vconst_ready = sem("vconst_ready")
        s_dperm_ready = sem("dperm_ready")
        s_tok_ready = sem("tok_ready")
        s_const_ready = sem("const_ready")
        s_aneg_ready = sem("aneg_ready")
        s_ss_ready = sem("ss_ready")
        s_lnss_ready = sem("lnss_ready")
        s_rms_ready = sem("rms_ready")
        s_h_ready = sem("h_ready")
        s_hT_ps = sem("hT_ps")
        s_hT_ready = sem("hT_ready")
        s_res_ps = sem("res_ps")
        s_res_raw_ready = sem("res_raw_ready")
        s_u_ps = sem("u_ps")
        s_u_raw_ready = sem("u_raw_ready")
        s_u_acc_ready = sem("u_acc_ready")
        s_conv_done = sem("conv_done")
        s_u_ready = sem("u_ready")
        s_res_ready = sem("res_ready")
        s_xdbl_ps = sem("xdbl_ps")
        s_xdbl_ready = sem("xdbl_ready")
        s_bc_ready = sem("bc_ready")
        s_dt_ps = sem("dt_ps")
        s_dt_parts = sem("dt_parts")
        s_dt_exp = sem("dt_exp")
        s_dt_log = sem("dt_log")
        s_delta_ready = sem("delta_ready")
        s_du_ready = sem("du_ready")
        s_part_ready = sem("part_ready")
        s_rest_ready = sem("rest_ready")
        s_parts_in = sem("parts_in")
        s_dlx_ready = sem("dlx_ready")
        s_dA_ready = sem("dA_ready")
        s_dux_ready = sem("dux_ready")
        s_dbu_done = sem("dbu_done")
        s_scan_done = sem("scan_done")
        s_carry_done = sem("carry_done")
        s_cs_ready = sem("cs_ready")
        s_ysum_done = sem("ysum_done")
        s_yg_ready = sem("yg_ready")
        s_out_ps = sem("out_ps")
        s_v_ready = sem("v_ready")
        s_st_done = sem("st_done")
        s_mv_done = sem("mv_done")
        s_lnv_ready = sem("lnv_ready")
        s_rstd_ready = sem("rstd_ready")
        s_x1_ready = sem("x1_ready")
        s_x1T_ps = sem("x1T_ps")
        s_x1T_ready = sem("x1T_ready")
        s_aff_ps = sem("aff_ps")
        s_aff_ready = sem("aff_ready")
        s_top_ready = sem("top_ready")
        s_topi_ready = sem("topi_ready")
        s_eid_ready = sem("eid_ready")
        s_onehot_ready = sem("onehot_ready")
        s_al_ready = sem("al_ready")
        s_al1_ready = sem("al1_ready")
        s_alpha_ready = sem("alpha_ready")
        s_rank_ps = sem("rank_ps")
        s_rank_ready = sem("rank_ready")
        s_posf_ready = sem("posf_ready")
        s_pos_ready = sem("pos_ready")
        s_count_ps = sem("count_ps")
        s_route = sem("route")
        s_fill_ready = sem("fill_ready")
        s_slots_ready = sem("slots_ready")
        s_filled = sem("filled")
        s_scattered = sem("scattered")
        s_a0 = sem("a0")
        s_xs_in = [sem(f"xs_in{i}") for i in range(XS_RING)]
        s_w_e = [sem(f"w_e{i}") for i in range(W_RING)]
        s_sti_ready = sem("sti_ready")
        s_mvi_ready = sem("mvi_ready")
        s_lni_ready = sem("lni_ready")
        s_rstdi_ready = sem("rstdi_ready")
        s_xn_ready = sem("xn_ready")
        s_xsT_ps = sem("xsT_ps")
        s_xsT_ready = sem("xsT_ready")
        s_h_ps = sem("h_ps")
        s_h_last_ps = sem("h_last_ps")
        s_hh_act = sem("hh_act")
        s_hh_dve = sem("hh_dve")
        s_b2d_ready = sem("b2d_ready")
        s_y_e_ps = sem("y_e_ps")
        s_z_ready = sem("z_ready")
        s_sto_ready = sem("sto_ready")
        s_mvo_ready = sem("mvo_ready")
        s_lno_ready = sem("lno_ready")
        s_rstdo_ready = sem("rstdo_ready")
        s_o_ready = sem("o_ready")
        s_stored = sem("stored")

        block = ctx.enter_context(nc.Block())

        def buf(g):
            return g % 2

        def tiles(g):
            return slice(TT * g, TT * g + TT)

        def pair(m):
            return range(2 * m, min(2 * m + 2, NS))

        N_PAIRS = (NS + 1) // 2

        def h_last(k):
            return (y_ps[:] if k % 2 else dA_ps[:, 2, :])[:, 0:P]

        @block.sync
        def _(sp):
            sp.dma_start(x_sb[:, tiles(0), :], x_v[:, tiles(0), :]).then_inc(s_x_in[0], 16)
            sp.dma_start(ident[:], ident_c).then_inc(s_ident_in, 16)
            sp.dma_start(w_in[:], in_w).then_inc(s_in_w_in, 16)
            sp.dma_start(w_xp[:], x_proj_w).then_inc(s_xp_in, 16)
            sp.dma_start(w_dt[:], dt_w).then_inc(s_dt_in, 16)
            sp.dma_start(sel_f[:], sel_c).then_inc(s_sel_in, 16)
            for g in range(1, NCH):
                sp.dma_start(x_sb[:, tiles(g), :], x_v[:, tiles(g), :]).then_inc(s_x_in[g], 16)

            def bc(g):
                sp.wait_ge(s_xdbl_ready, g + 1)
                if GROUPS * (g - 1) > 0:
                    sp.wait_ge(s_cs_ready, GROUPS * (g - 1))
                if GROUPS * (g - 1) > 0:
                    sp.wait_ge(s_dbu_done, GROUPS * (g - 1))
                for row, dst in ((DT_RANK, b_rep), (DT_RANK + D_STATE, c_rep)):
                    src = xdbl[row:row + D_STATE, :].unsqueeze(1).to_broadcast([D_STATE, CG, T])
                    sp.dma_start(dst[:, buf(g), :], src).then_inc(s_bc_ready, 16)

            def parts(g):
                if GROUPS * (g - 1) > 0:
                    sp.wait_ge(s_dux_ready, GROUPS * (g - 1))
                for n, (src, dst) in enumerate(((delta_p, delta_q), (du_p, du_q))):
                    for part in range(PARTS):
                        if part < 2:
                            sp.wait_ge(s_part_ready, 4 * g + 2 * n + part + 1)
                        else:
                            sp.wait_ge(s_rest_ready, 4 * g + 2 * n + 2)
                        for r in range(NR):
                            sp.dma_start(dst[part * QROWS:(part + 1) * QROWS, buf(g), r::NR, :],
                                         src[r * QROWS:(r + 1) * QROWS, part, :, :]).then_inc(s_parts_in, 16)

            for g in range(NCH):
                bc(g)
                parts(g)

            def fill(e):
                row = sp.value_load(fill_row[0:1, e:e + 1], min_val=0, max_val=E * REGION - 2 * P)
                sp.dma_start(xs_dram[bass.ds(row, 2 * P), :].rearrange("(p a) d -> p a d", a=2), zrow[:]).then_inc(s_filled, 16)

            sp.wait_ge(s_fill_ready, 1)
            for e in range(E):
                fill(e)
            sp.wait_ge(s_slots_ready, 2)

            def load_rows(k):
                if k >= XS_RING:
                    sp.wait_ge(s_xn_ready, k - XS_RING + 1)
                row = sp.value_load(row0[0:1, k:k + 1], min_val=0, max_val=E * REGION - P)
                sp.dma_start(xs[:, k, :], xs_dram[bass.ds(row, P), :]).then_inc(s_xs_in[k % XS_RING], 16)

            def load_weights(k):
                if k >= W_RING:
                    sp.wait_ge(s_y_e_ps, k - W_RING + 1)
                e = sp.value_load(et[0:1, k:k + 1], min_val=0, max_val=E - 1)
                sp.dma_start(wp[:, k % W_RING, :], w_pack[bass.ds(e, 1), :, :].rearrange("e p f -> (e p) f")).then_inc(s_w_e[k % W_RING], 16)

            load_weights(0)
            sp.wait_ge(s_filled, 16 * E)
            sp.wait_ge(s_scattered, 16 * NT)
            for k in range(4):
                load_rows(k)
            for k in range(1, NS):
                load_weights(k)
                if k + 3 < NS:
                    load_rows(k + 3)
            sp.wait_ge(s_stored, 16 * NS)

        @block.tensor
        def _(pe):
            mm = nc.tensor.matmul

            def hT_fill(g):
                if g == 0:
                    pe.wait_ge(s_ident_in, 16)
                pe.wait_ge(s_h_ready, g + 1)
                if g >= 3:
                    pe.wait_ge(s_aff_ready, g - 2)
                if 2 * g > 0:
                    pe.wait_ge(s_dt_parts, 2 * g)
                for j in range(TT):
                    last = nc.tensor.transpose(m_ps[:, 0, j * P:(j + 1) * P], h_sb[:, j, :], ident[:])
                last.then_inc(s_hT_ps, 1)

            def res_fill(g, h):
                if h == 0:
                    if g == 0:
                        pe.wait_ge(s_in_w_in, 16)
                    pe.wait_ge(s_hT_ready, g + 1)
                    if g >= 3:
                        pe.wait_ge(s_rank_ready, g - 2)
                    if 2 * g - 1 > 0:
                        pe.wait_ge(s_dt_parts, 2 * g - 1)
                mm(m_ps[:, 1 - h, :], w_r[:, h * P:(h + 1) * P], hT[:], start=True, stop=True).then_inc(s_res_ps, 1)

            def u_fill(g, h):
                pe.wait_ge(s_res_raw_ready, 2 * g + h + 1)
                mm(m_ps[:, 1 - h, :], w_u[:, h * P:(h + 1) * P], hT[:], start=True, stop=True).then_inc(s_u_ps, 1)

            def xdbl_fill(g):
                if g == 0:
                    pe.wait_ge(s_xp_in, 16)
                pe.wait_ge(s_u_ready, 2 * g + 2)
                n = DT_RANK + 2 * D_STATE
                for h in range(H):
                    last = mm(m_ps[0:n, 1, :], w_xp[:, h, :], u_sb[:, buf(g), h, :], start=(h == 0), stop=(h == H - 1))
                last.then_inc(s_xdbl_ps, 1)

            def dt_fill(g, h):
                if g == 0:
                    pe.wait_ge(s_dt_in, 16)
                pe.wait_ge(s_xdbl_ready, g + 1)
                if h == 1 and g >= 2:
                    pe.wait_ge(s_v_ready, g - 1)
                mm(m_ps[:, 1 - h, :], w_dt[:, h * P:(h + 1) * P], xdbl[0:DT_RANK, :], start=True, stop=True).then_inc(s_dt_ps, 1)

            def out_fill(g):
                pe.wait_ge(s_yg_ready, H * (g + 1))
                pe.wait_ge(s_u_ready, min(2 * (g + 3), 2 * NCH))
                if g > 0:
                    pe.wait_ge(s_aff_ready, g)
                for j in range(TT):
                    for h in range(H):
                        last = mm(m_ps[:, 0, j * P:(j + 1) * P], yg[:, buf(g), h, j * P:(j + 1) * P], w_out[:, h, :],
                                  start=(h == 0), stop=(h == H - 1))
                last.then_inc(s_out_ps, 1)

            def x1T_fill(g):
                pe.wait_ge(s_x1_ready, g + 1)
                pe.wait_ge(s_dt_parts, min(2 * (g + 3), 2 * NCH) - 1)
                if g > 0:
                    pe.wait_ge(s_rank_ready, g)
                for j in range(TT):
                    last = nc.tensor.transpose(m_ps[:, 1, j * P:(j + 1) * P], x2[:, TT * g + j, :], ident[:])
                last.then_inc(s_x1T_ps, 1)

            def aff_fill(g):
                pe.wait_ge(s_x1T_ready, g + 1)
                pe.wait_ge(s_dt_parts, min(2 * (g + 3), 2 * NCH))
                for j in range(TT):
                    last = mm(m_ps[:, 0, j * E:(j + 1) * E], x1T[:, j * P:(j + 1) * P], cent[:], start=True, stop=True)
                last.then_inc(s_aff_ps, 1)

            def rank_fill(g):
                pe.wait_ge(s_onehot_ready, g + 1)
                pe.wait_ge(s_x1T_ready, g + 1)
                o = m_ps[:, 1, 0:TT * E]
                mm(o, ones_b[0:1, :], region_b[:].rearrange("p t e -> p (t e)"), start=True, stop=False, skip_group_check=True)
                for t in range(TT * g):
                    mm(o.rearrange("p (t e) -> p t e", t=TT), ones_b[:], onehot[:, t:t + 1, :].to_broadcast([P, TT, E]),
                       start=False, stop=False, skip_group_check=True)
                for j in range(1, TT):
                    mm(m_ps[:, 1, j * E:TT * E].rearrange("p (t e) -> p t e", e=E), ones_b[:], onehot[:, TT * g:TT * g + TT - j, :],
                       start=False, stop=False, skip_group_check=True)
                mm(o.rearrange("p (t e) -> p t e", t=TT), ltri[:], onehot[:, tiles(g), :], start=False, stop=True,
                   skip_group_check=True).then_inc(s_rank_ps, 1)

            def count_fill():
                pe.wait_ge(s_yg_ready, H * NCH)
                o = y_ps[:, 0:E]
                for t in range(NT):
                    last = mm(o, ones_b[:], onehot[:, t, :], start=(t == 0), stop=(t == NT - 1))
                last.then_inc(s_count_ps, 1)

            def expand(G):
                g, q, k = G // GROUPS, G % GROUPS // NK, G % NK
                if G == 0:
                    pe.wait_ge(s_const_ready, 1)
                if G % GROUPS == 0:
                    pe.wait_ge(s_parts_in, 16 * 2 * PARTS * NR * (g + 1))
                if G - DA_RING + 1 > 0:
                    pe.wait_ge(s_scan_done, G - DA_RING + 1)
                mm(dA_ps[:, G % DA_RING, :], sel[:, k, :], delta_q[:, buf(g), q, :], start=True, stop=True).then_inc(s_dlx_ready, 1)
                if G - DUX_RING + 1 > 0:
                    pe.wait_ge(s_dbu_done, G - DUX_RING + 1)
                mm(dux_ps[:, G % DUX_RING, :], sel[:, k, :], du_q[:, buf(g), q, :], start=True, stop=True).then_inc(s_dux_ready, 1)

            def state_sum(Q):
                g, h, r = Q // (H * NR), Q // NR % H, Q % NR
                if r == 0:
                    if Q // NR > 0:
                        pe.wait_ge(s_yg_ready, Q // NR)
                    else:
                        pe.wait_ge(s_dperm_ready, 1)
                    mm(y_ps[:], dperm[:, h, :], u_sb[:, buf(g), h, :], start=True, stop=False, skip_group_check=True)
                pe.wait_ge(s_cs_ready, NK * (Q + 1))
                for k in range(NK):
                    last = mm(y_ps[k * QROWS:(k + 1) * QROWS, :], sely[:, r, :], cs[:, (Q * NK + k) % P_RING, :], start=False,
                              stop=(r == NR - 1), skip_group_check=True, tile_position=(0, k * QROWS))
                last.then_inc(s_ysum_done, 1)

            pieces_prep = {0: [hT_fill], 2: [lambda g: res_fill(g, 0)], 3: [lambda g: res_fill(g, 1)], 4: [lambda g: u_fill(g, 0)],
                           5: [lambda g: u_fill(g, 1)], 10: [xdbl_fill], 13: [lambda g: dt_fill(g, 0)], 14: [lambda g: dt_fill(g, 1)]}
            pieces_post = {11: [out_fill], 15: [x1T_fill], 17: [aff_fill], 20: [rank_fill]}

            for s in sorted(pieces_prep):
                for f in pieces_prep[s]:
                    f(0)
            for G in range(NG):
                g, s = G // GROUPS, G % GROUPS
                expand(G)
                Gs = G - SUM_LAG
                if Gs >= 0 and Gs % NK == NK - 1:
                    state_sum(Gs // NK)
                if g + 1 < NCH:
                    for f in pieces_prep.get(s, []):
                        f(g + 1)
                if g >= 1:
                    for f in pieces_post.get(s, []):
                        f(g - 1)
            state_sum(NG // NK - 1)
            for s in sorted(pieces_post):
                for f in pieces_post[s]:
                    f(NCH - 1)

            count_fill()

            def ffn_T(k):
                pe.wait_ge(s_xn_ready, k + 1)
                if k >= 2:
                    pe.wait_ge(s_xsT_ready, k - 1)
                nc.tensor.transpose(m_ps[:, k % 2, 0:P], xn[:, k % XN_RING, :], ident[:]).then_inc(s_xsT_ps, 1)

            def ffn_up(k):
                pe.wait_ge(s_xsT_ready, k + 1)
                pe.wait_ge(s_w_e[k % W_RING], 16 * (k // W_RING + 1))
                if k >= 2:
                    pe.wait_ge(s_hh_dve, k - 1)
                mm(h_last(k), wp[:, k % W_RING, (FJ - 1) * P:FJ * P], xsT[:, k % XT_RING, :], start=True, stop=True).then_inc(s_h_last_ps, 1)
                if k >= 2:
                    pe.wait_ge(s_hh_act, (FJ - 1) * (k - 1))
                for j in range(FJ - 1):
                    last = mm(dA_ps[:, k % 2, j * P:(j + 1) * P], wp[:, k % W_RING, j * P:(j + 1) * P], xsT[:, k % XT_RING, :],
                              start=True, stop=True)
                last.then_inc(s_h_ps, 1)

            def ffn_down(k):
                pe.wait_ge(s_b2d_ready, k + 1)
                if k >= 2:
                    pe.wait_ge(s_z_ready, k - 1)
                o = dux_ps[:, k % 2, 0:P]
                mm(o, ones_f[:], b2d[:, k % H_RING, :], start=True, stop=False)
                pe.wait_ge(s_hh_act, (FJ - 1) * (k + 1))
                pe.wait_ge(s_hh_dve, k + 1)
                for j in range(FJ):
                    last = mm(o, hh[:, k % H_RING, j, :], wp[:, k % W_RING, F + j * P:F + (j + 1) * P], start=False, stop=(j == FJ - 1))
                last.then_inc(s_y_e_ps, 1)

            ffn_T(0)
            ffn_T(1)
            for k in range(NS + 1):
                if k < NS:
                    ffn_up(k)
                if k + 2 < NS:
                    ffn_T(k + 2)
                if k >= 1:
                    ffn_down(k - 1)

        @block.scalar
        def _(act):
            A = nc.scalar.activation

            def ln_exp():
                nc.scalar.preload_act_table_set("natural_log_exp_and_others")

            def rms_scale(g):
                act.wait_ge(s_x_in[g], 16)
                if TT * g > 0:
                    act.wait_ge(s_ss_ready, TT * g)
                for j in range(TT):
                    A(junk[:, j, :], x_sb[:, TT * g + j, :], ACT.Square, accum_out=ss[:, TT * g + j:TT * g + j + 1]).then_inc(s_ss_ready, 1)
                act.wait_ge(s_ss_ready, TT * (g + 1))
                A(lnss[:, tiles(g)], ss[:, tiles(g)], ACT.Ln, scale=1.0 / D_MODEL, bias=eps_ap).then_inc(s_lnss_ready, 1)
                act.wait_ge(s_lnss_ready, g + 1)
                A(rms[:, tiles(g)], lnss[:, tiles(g)], ACT.Exp, scale=-0.5).then_inc(s_rms_ready, 1)
                act.wait_ge(s_rms_ready, g + 1)
                if g > 0:
                    act.wait_ge(s_hT_ps, g)
                if g > 0:
                    act.wait_ge(s_h_ready, g)
                for j in range(TT):
                    last = A(h_sb[:, j, :], x_sb[:, TT * g + j, :], ACT.Copy, scale=rms[:, TT * g + j:TT * g + j + 1])
                last.then_inc(s_h_ready, 1)

            def hT_copy(g):
                if g == 0:
                    act.wait_ge(s_small_in, 16)
                act.wait_ge(s_hT_ps, g + 1)
                if 2 * g > 0:
                    act.wait_ge(s_u_ps, 2 * g)
                A(hT[:], m_ps[:, 0, :], ACT.Copy, scale=w_norm[:, 0:1]).then_inc(s_hT_ready, 1)

            def res_copy(g, h):
                act.wait_ge(s_res_ps, 2 * g + h + 1)
                A(res_raw[:, h, :], m_ps[:, 1 - h, :], ACT.Copy).then_inc(s_res_raw_ready, 1)

            def u_copy(g, h):
                act.wait_ge(s_u_ps, 2 * g + h + 1)
                if 6 * g > 0:
                    act.wait_ge(s_conv_done, 6 * g)
                if g % CPB == 0:
                    A(u_raw[:, h, 0:D_CONV - 1], zeros[:, 0:D_CONV - 1], ACT.Copy).then_inc(s_a0, 1)
                else:
                    A(u_raw[:, h, 0:D_CONV - 1], u_raw[:, h, T:T + D_CONV - 1], ACT.Copy).then_inc(s_a0, 1)
                act.wait_ge(s_a0, 2 * g + h + 1)
                A(u_raw[:, h, D_CONV - 1:], m_ps[:, 1 - h, :], ACT.Copy).then_inc(s_u_raw_ready, 1)
                A(m_ps[:, 1 - h, :], m_ps[:, 1 - h, :], ACT.Identity, bias=b_conv[:, h:h + 1], scale=w_conv[:, h, D_CONV - 1:]).then_inc(s_u_acc_ready, 1)

            def silu(g):
                act.wait_ge(s_conv_done, 6 * (g + 1))
                if H * NR * (g - 1) > 0:
                    act.wait_ge(s_ysum_done, H * NR * (g - 1))
                for h in range(H):
                    A(u_sb[:, buf(g), h, :], m_ps[:, 1 - h, :], ACT.Silu).then_inc(s_u_ready, 1)
                if H * (g - 1) > 0:
                    act.wait_ge(s_yg_ready, H * (g - 1))
                act.wait_ge(s_res_raw_ready, 2 * g + 2)
                A(res_sb[:, buf(g), :, :], res_raw[:], ACT.Silu).then_inc(s_res_ready, 1)
                ln_exp()

            def xdbl_copy(g):
                act.wait_ge(s_xdbl_ps, g + 1)
                if 32 * g > 0:
                    act.wait_ge(s_bc_ready, 32 * g)
                if 2 * g > 0:
                    act.wait_ge(s_dt_ps, 2 * g)
                A(xdbl[:], m_ps[0:DT_RANK + 2 * D_STATE, 1, :], ACT.Copy).then_inc(s_xdbl_ready, 1)

            def softplus_in(g, h):
                act.wait_ge(s_dt_ps, 2 * g + h + 1)
                if g > 0:
                    act.wait_ge(s_delta_ready, g)
                A(dt_abs[:, h, :], m_ps[:, 1 - h, :], ACT.Abs, bias=b_dt[:, h:h + 1])
                A(dt_pos[:, h, :], m_ps[:, 1 - h, :], ACT.Relu, bias=b_dt[:, h:h + 1]).then_inc(s_dt_parts, 1)

            def softplus_log(g):
                act.wait_ge(s_dt_parts, 2 * g + 2)
                A(dt_abs[:], dt_abs[:], ACT.Exp, scale=-1.0).then_inc(s_dt_exp, 1)
                act.wait_ge(s_dt_exp, g + 1)
                A(dt_abs[:], dt_abs[:], ACT.Ln, bias=one_ap).then_inc(s_dt_log, 1)

            def cast_part(g, n, part):
                src, parts = ((delta, delta_p), (du, du_p))[n]
                act.wait_ge(s_delta_ready if n == 0 else s_du_ready, g + 1)
                if part:
                    act.wait_ge(s_rest_ready, 4 * g + 2 * n + 1)
                if 16 * 2 * PARTS * NR * g > 0:
                    act.wait_ge(s_parts_in, 16 * 2 * PARTS * NR * g)
                A(parts[:, part, :, :], src[:, part, :, :], ACT.Copy).then_inc(s_part_ready, 1)

            def decay(G):
                act.wait_ge(s_dlx_ready, G + 1)
                A(dA_ps[:, G % DA_RING, :], dA_ps[:, G % DA_RING, :], ACT.Exp, scale=a_neg[:, G % GROUPS:G % GROUPS + 1]).then_inc(s_dA_ready, 1)

            def keep_state(G):
                if G >= 0 and G // GROUPS % CPB < CPB - 1:
                    act.wait_ge(s_scan_done, G + 1)
                    A(carry[:, G % GROUPS:G % GROUPS + 1], s_sb[:, G % S_RING, T - 1:T], ACT.Copy).then_inc(s_carry_done, 1)

            def rstd_of(g):
                act.wait_ge(s_mv_done, TT * (g + 1))
                A(lnv[:], mv[:, :, 1], ACT.Ln, scale=0.25, bias=epsq_ap).then_inc(s_lnv_ready, 1)
                act.wait_ge(s_lnv_ready, g + 1)
                A(rstd[:], lnv[:], ACT.Exp, scale=-0.5).then_inc(s_rstd_ready, 1)

            def alpha_exp(g):
                act.wait_ge(s_top_ready, TT * (g + 1))
                if g > 0:
                    act.wait_ge(s_al1_ready, g)
                A(al_e[:], top[:, tiles(g), 0], ACT.Exp, scale=-0.5).then_inc(s_al_ready, 1)

            def x1T_copy(g):
                act.wait_ge(s_x1T_ps, g + 1)
                if g > 0:
                    act.wait_ge(s_aff_ps, g)
                A(x1T[:], m_ps[:, 1, :], ACT.Copy).then_inc(s_x1T_ready, 1)

            pieces_prep = {0: [rms_scale], 1: [hT_copy], 2: [lambda g: res_copy(g, 0)], 3: [lambda g: res_copy(g, 1)],
                           4: [lambda g: u_copy(g, 0)], 5: [lambda g: u_copy(g, 1)], 9: [silu], 11: [xdbl_copy],
                           14: [lambda g: softplus_in(g, 0)], 15: [lambda g: softplus_in(g, 1)], 16: [softplus_log],
                           18: [lambda g: cast_part(g, 0, 0)], 20: [lambda g: cast_part(g, 0, 1)],
                           21: [lambda g: cast_part(g, 1, 0)], 23: [lambda g: cast_part(g, 1, 1)]}
            pieces_post = {13: [rstd_of], 16: [x1T_copy], 19: [alpha_exp]}

            act.dma_start(small_sb[:], small).then_inc(s_small_in, 16)
            ln_exp()
            act.wait_ge(s_vconst_ready, 1)
            for s in sorted(pieces_prep):
                for f in pieces_prep[s]:
                    f(0)
                if s == 1:
                    A(a_exp[:], a_in[:], ACT.Exp).then_inc(s_aneg_ready, 1)
            act.wait_ge(s_aneg_ready, 2)
            for G in range(NG):
                g, s = G // GROUPS, G % GROUPS
                decay(G)
                keep_state(G - DA_RING)
                if g + 1 < NCH:
                    for f in pieces_prep.get(s, []):
                        f(g + 1)
                if g >= 1:
                    for f in pieces_post.get(s, []):
                        f(g - 1)
            for s in sorted(pieces_post):
                for f in pieces_post[s]:
                    f(NCH - 1)

            def in_rstd(m):
                ks = pair(m)
                act.wait_ge(s_mvi_ready, ks[-1] + 1)
                i = slice(ks[0], ks[-1] + 1)
                A(ln_i[:, i], mv_i[:, i, 1], ACT.Ln, bias=eps4_ap).then_inc(s_lni_ready, 1)
                act.wait_ge(s_lni_ready, m + 1)
                A(rstd_i[:, i], ln_i[:, i], ACT.Exp, scale=-0.5).then_inc(s_rstdi_ready, 1)

            def out_rstd(m):
                ks = pair(m)
                act.wait_ge(s_mvo_ready, ks[-1] + 1)
                i = slice(ks[0], ks[-1] + 1)
                A(ln_o[:, i], mv_o[:, i, 1], ACT.Ln, bias=eps_ap).then_inc(s_lno_ready, 1)
                act.wait_ge(s_lno_ready, m + 1)
                A(rstd_o[:, i], ln_o[:, i], ACT.Exp, scale=-0.5).then_inc(s_rstdo_ready, 1)

            def xsT_affine(k):
                act.wait_ge(s_xsT_ps, k + 1)
                act.wait_ge(s_w_e[k % W_RING], 16 * (k // W_RING + 1))
                if k >= XT_RING:
                    act.wait_ge(s_h_ps, k - XT_RING + 1)
                c = 2 * F + FJ
                A(xsT[:, k % XT_RING, :], m_ps[:, k % 2, 0:P], ACT.Identity, scale=wp[:, k % W_RING, c:c + 1],
                  bias=wp[:, k % W_RING, c + 1:c + 2]).then_inc(s_xsT_ready, 1)

            def relu(k):
                if k >= H_RING:
                    act.wait_ge(s_y_e_ps, k - H_RING + 1)
                act.wait_ge(s_h_ps, k + 1)
                for j in range(FJ - 1):
                    A(hh[:, k % H_RING, j, :], dA_ps[:, k % 2, j * P:(j + 1) * P], ACT.Relu,
                      bias=wp[:, k % W_RING, 2 * F + j:2 * F + j + 1]).then_inc(s_hh_act, 1)

            in_rstd(0)
            in_rstd(1)
            xsT_affine(0)
            xsT_affine(1)
            for k in range(NS):
                relu(k)
                if k + 2 < NS:
                    xsT_affine(k + 2)
                if k % 2 == 0:
                    if k // 2 + 2 < N_PAIRS:
                        in_rstd(k // 2 + 2)
                elif k >= 3:
                    out_rstd((k - 3) // 2)
            for m in range((NS - 4) // 2 + 1 if NS % 2 == 0 else (NS - 3) // 2, N_PAIRS):
                out_rstd(m)

        @block.vector
        def _(dve):
            V = nc.vector

            def taps(g, h):
                if g == 0:
                    dve.wait_ge(s_small_in, 16)
                dve.wait_ge(s_u_acc_ready, 2 * g + h + 1)
                for k in range(D_CONV - 1):
                    if k:
                        if 6 * g + 3 * h + k > 0:
                            dve.wait_ge(s_conv_done, 6 * g + 3 * h + k)
                    V.scalar_tensor_tensor(out=m_ps[:, 1 - h, :], in0=u_raw[:, h, k:k + T], scalar=w_conv[:, h, k:k + 1],
                                           in1=m_ps[:, 1 - h, :], op0=ALU.mult, op1=ALU.add).then_inc(s_conv_done, 1)

            def make_delta(g):
                dve.wait_ge(s_dt_log, g + 1)
                if 4 * g > 0:
                    dve.wait_ge(s_rest_ready, 4 * g)
                if g > 0:
                    dve.wait_ge(s_du_ready, g)
                if 4 * g > 0:
                    dve.wait_ge(s_part_ready, 4 * g)
                V.tensor_tensor(delta[:, 0, :, :], dt_pos[:], dt_abs[:], ALU.add).then_inc(s_delta_ready, 1)

            def make_du(g):
                dve.wait_ge(s_delta_ready, g + 1)
                dve.wait_ge(s_u_ready, 2 * g + 2)
                V.tensor_tensor(du[:, 0, :, :], delta[:, 0, :, :], u_sb[:, buf(g), :, :], ALU.mult).then_inc(s_du_ready, 1)

            def dbu_of(G):
                if G >= NG:
                    return
                g = G // GROUPS
                dve.wait_ge(s_dux_ready, G + 1)
                if G - DBU_RING + 1 > 0:
                    dve.wait_ge(s_scan_done, G - DBU_RING + 1)
                if G % GROUPS == 0:
                    dve.wait_ge(s_bc_ready, 32 * (g + 1))
                V.tensor_tensor(dbu[:, G % DBU_RING, :], b_rep[:, buf(g), :], dux_ps[:, G % DUX_RING, :], ALU.mult).then_inc(s_dbu_done, 1)

            def scan(G):
                g, n = G // GROUPS, G % GROUPS
                dve.wait_ge(s_dA_ready, G + 1)
                dve.wait_ge(s_dbu_done, G + 1)
                if G - S_RING + 1 > 0:
                    dve.wait_ge(s_cs_ready, G - S_RING + 1)
                if G >= S_RING:
                    Gp = G - S_RING
                    kept = sum(1 for i in range(Gp + 1) if i // GROUPS % CPB < CPB - 1)
                    if kept > 0:
                        dve.wait_ge(s_carry_done, kept)
                init = 0.0
                if g % CPB:
                    if g // CPB * GROUPS * (CPB - 1) + (g % CPB - 1) * GROUPS + n + 1 > 0:
                        dve.wait_ge(s_carry_done, g // CPB * GROUPS * (CPB - 1) + (g % CPB - 1) * GROUPS + n + 1)
                    init = carry[:, n:n + 1]
                V.tensor_tensor_scan(s_sb[:, G % S_RING, :], dA_ps[:, G % DA_RING, :], dbu[:, G % DBU_RING, :], init,
                                     ALU.mult, ALU.add).then_inc(s_scan_done, 1)

            def gate(Hi):
                g, h = Hi // H, Hi % H
                dve.wait_ge(s_ysum_done, NR * (Hi + 1))
                dve.wait_ge(s_res_ready, g + 1)
                if g - 1 > 0:
                    dve.wait_ge(s_out_ps, g - 1)
                V.tensor_tensor(yg[:, buf(g), h, :], res_sb[:, buf(g), h, :], y_ps[:], ALU.mult).then_inc(s_yg_ready, 1)

            def residual(g):
                dve.wait_ge(s_out_ps, g + 1)
                V.scalar_tensor_tensor(out=v_sb[:], in0=x_sb[:, tiles(g), :], scalar=2.0,
                                       in1=m_ps[:, 0, :].rearrange("p (t d) -> p t d", t=TT), op0=ALU.mult, op1=ALU.add).then_inc(s_v_ready, 1)

            def stats(g):
                dve.wait_ge(s_v_ready, g + 1)
                for j in range(TT):
                    V.bn_stats(st[:, j, :], v_sb[:, j, :]).then_inc(s_st_done, 1)
                for j in range(TT):
                    dve.wait_ge(s_st_done, TT * g + j + 1)
                    V.bn_aggr(mv[:, j, :], st[:, j, :]).then_inc(s_mv_done, 1)

            def normed(g):
                dve.wait_ge(s_rstd_ready, g + 1)
                for j in range(TT):
                    last = V.tensor_scalar(x2[:, TT * g + j, :], v_sb[:, j, :], mv[:, j, 0:1], rstd[:, j:j + 1], ALU.subtract, ALU.mult)
                last.then_inc(s_x1_ready, 1)

            def route_tokens(g):
                dve.wait_ge(s_aff_ps, g + 1)
                V.tensor_copy(aff[:], m_ps[:, 0, 0:TT * E].rearrange("p (t e) -> p t e", t=TT)).then_inc(s_aff_ready, 1)
                dve.wait_ge(s_aff_ready, g + 1)
                for j in range(TT):
                    V.max(top[:, TT * g + j, :], aff[:, j, :]).then_inc(s_top_ready, 1)
                for j in range(TT):
                    dve.wait_ge(s_top_ready, TT * g + j + 1)
                    V.max_index(topi[:, j, :], top[:, TT * g + j, :], aff[:, j, :]).then_inc(s_topi_ready, 1)
                dve.wait_ge(s_topi_ready, TT * (g + 1))
                V.tensor_copy(eid[:], topi[:, :, 0]).then_inc(s_eid_ready, 1)
                dve.wait_ge(s_eid_ready, g + 1)
                V.tensor_tensor(onehot[:, tiles(g), :], iota8[:].unsqueeze(1).to_broadcast([P, TT, E]),
                                eid[:].unsqueeze(2).to_broadcast([P, TT, E]), ALU.is_equal).then_inc(s_onehot_ready, 1)

            def rank_tokens(g):
                dve.wait_ge(s_rank_ps, g + 1)
                if g > 0:
                    dve.wait_ge(s_posf_ready, g)
                V.tensor_tensor(rank[:], onehot[:, tiles(g), :], m_ps[:, 1, 0:TT * E].rearrange("p (t e) -> p t e", t=TT), ALU.mult).then_inc(s_rank_ready, 1)
                dve.wait_ge(s_rank_ready, g + 1)
                if g > 0:
                    dve.wait_ge(s_pos_ready, g)
                V.tensor_reduce(posf[:], rank[:], AX_X, ALU.add).then_inc(s_posf_ready, 1)
                dve.wait_ge(s_posf_ready, g + 1)
                V.tensor_copy(pos[:, tiles(g)], posf[:]).then_inc(s_pos_ready, 1)

            def make_alpha(g):
                dve.wait_ge(s_al_ready, g + 1)
                if g > 0:
                    dve.wait_ge(s_alpha_ready, g)
                V.tensor_scalar(al_1[:], al_e[:], 1.0, None, ALU.add).then_inc(s_al1_ready, 1)
                dve.wait_ge(s_al1_ready, g + 1)
                V.reciprocal(rows[:, tiles(g), D_MODEL + 1], al_1[:]).then_inc(s_alpha_ready, 1)

            V.memset(zeros[:], 0.0)
            V.memset(eps_t[:], EPS)
            V.memset(eps4_t[:], 4 * EPS)
            V.memset(epsq_t[:], EPS / 4)
            V.memset(ones8[:], 1.0).then_inc(s_vconst_ready, 1)
            V.memset(ones_f[:], 1.0)
            V.memset(ones_b[:], 1.0)
            V.memset(zrow[:], 0.0).then_inc(s_tok_ready, 1)
            dve.wait_ge(s_sel_in, 16)
            V.tensor_copy(sel[:], sel_f[:]).then_inc(s_const_ready, 1)

            pieces_prep = {7: [lambda g: taps(g, 0)], 8: [lambda g: taps(g, 1)], 18: [make_delta], 19: [make_du]}
            pieces_post = {12: [residual, stats], 14: [normed], 18: [route_tokens], 20: [make_alpha], 21: [rank_tokens]}
            for s in sorted(pieces_prep):
                for f in pieces_prep[s]:
                    f(0)
                if s == 8:
                    dve.wait_ge(s_aneg_ready, 1)
                    V.tensor_scalar(a_neg[:], a_exp[:], -1.0, None, ALU.mult).then_inc(s_aneg_ready, 1)
                    dve.wait_ge(s_late_in, 16 * 4)
                    V.tensor_copy(ltri[:], ltri_f)
                    V.tensor_copy(region_b[:], route_sb[0:1, E + NT + NS + E:].rearrange("p (t e) -> p t e", t=TT))
                    V.tensor_copy(rows[:, :, D_MODEL].bitcast(U32), tok[:, 0:NT])
                    dve.wait_ge(s_tok_ready, 1)
                    V.tensor_copy(zrow[:, :, D_MODEL].bitcast(U32), tok[:, NT:NT + 1].to_broadcast([P, 2])).then_inc(s_tok_ready, 1)
                    for h in range(H):
                        last = V.tensor_scalar(dperm[:, h, :], perm, d_in[:, h:h + 1], None, ALU.mult)
                    last.then_inc(s_dperm_ready, 1)
            dbu_of(0)
            for G in range(NG):
                g, s = G // GROUPS, G % GROUPS
                dbu_of(G + 1)
                scan(G)
                Gs = G - SUM_LAG - 2
                if Gs >= 0 and (Gs + 1) % (NK * NR) == 0:
                    gate(Gs // (NK * NR))
                if g + 1 < NCH:
                    for f in pieces_prep.get(s, []):
                        f(g + 1)
                if g >= 1:
                    for f in pieces_post.get(s, []):
                        f(g - 1)
            gate(NCH * H - 1)
            for s in sorted(pieces_post):
                for f in pieces_post[s]:
                    f(NCH - 1)

            n_route = [0]

            def routed(ins):
                n_route[0] += 1
                ins.then_inc(s_route, 1)

            dve.wait_ge(s_count_ps, 1)
            routed(V.tensor_copy(cnt[:], y_ps[:, 0:E]))
            dve.wait_ge(s_route, n_route[0])
            V.tensor_tensor(fill_row[:], cnt[:], region0, ALU.add).then_inc(s_fill_ready, 1)
            routed(V.tensor_tensor(past[:], cnt[:].unsqueeze(2).to_broadcast([P, E, NT]),
                                   steps.unsqueeze(1).to_broadcast([P, E, NT]), ALU.is_gt))
            dve.wait_ge(s_route, n_route[0])
            routed(V.tensor_reduce(ntile[:], past[:], AX_X, ALU.add))
            dve.wait_ge(s_route, n_route[0])
            routed(V.tensor_tensor_scan(tend[:], ones8[:], ntile[:], 0.0, ALU.mult, ALU.add))
            routed(V.tensor_scalar(jump[:], ntile[:], -float(P), float(REGION), ALU.mult, ALU.add))
            routed(V.tensor_scalar(lim[:], ntile[:, E - 1:E], float(P), float((E - 1) * REGION), ALU.mult, ALU.add))
            dve.wait_ge(s_route, n_route[0])
            routed(V.tensor_tensor(beyond[:], kidx.unsqueeze(2).to_broadcast([P, NS, E]),
                                   tend[:].unsqueeze(1).to_broadcast([P, NS, E]), ALU.is_ge))
            dve.wait_ge(s_route, n_route[0])
            routed(V.tensor_reduce(etf[:], beyond[:, :, 0:E - 1], AX_X, ALU.add))
            routed(V.tensor_tensor(jumps[:, :, 0:E - 1], beyond[:, :, 0:E - 1],
                                   jump[:, 0:E - 1].unsqueeze(1).to_broadcast([P, NS, E - 1]), ALU.mult))
            dve.wait_ge(s_route, n_route[0])
            V.tensor_copy(et[:], etf[:]).then_inc(s_slots_ready, 1)
            routed(V.tensor_reduce(rowf[:], jumps[:, :, 0:E - 1], AX_X, ALU.add))
            dve.wait_ge(s_route, n_route[0])
            routed(V.scalar_tensor_tensor(out=rowf[:], in0=kidx, scalar=float(P), in1=rowf[:], op0=ALU.mult, op1=ALU.add))
            dve.wait_ge(s_route, n_route[0])
            V.tensor_scalar(row0[:], rowf[:], lim[:, 0:1], None, ALU.min).then_inc(s_slots_ready, 1)

            def in_stats(m):
                for k in pair(m):
                    dve.wait_ge(s_xs_in[k % XS_RING], 16 * (k // XS_RING + 1))
                    V.bn_stats(st_i[:, k, :], xs[:, k, 0:D_MODEL]).then_inc(s_sti_ready, 1)
                for k in pair(m):
                    dve.wait_ge(s_sti_ready, k + 1)
                    V.bn_aggr(mv_i[:, k, :], st_i[:, k, :]).then_inc(s_mvi_ready, 1)

            def in_norm(k):
                dve.wait_ge(s_rstdi_ready, k // 2 + 1)
                if k >= XN_RING:
                    dve.wait_ge(s_xsT_ps, k - XN_RING + 1)
                V.tensor_scalar(xn[:, k % XN_RING, :], xs[:, k, 0:D_MODEL], mv_i[:, k, 0:1], rstd_i[:, k:k + 1], ALU.subtract,
                                ALU.mult).then_inc(s_xn_ready, 1)

            def relu_last(k):
                j = FJ - 1
                dve.wait_ge(s_h_last_ps, k + 1)
                if k >= H_RING:
                    dve.wait_ge(s_y_e_ps, k - H_RING + 1)
                V.tensor_scalar(hh[:, k % H_RING, j, :], h_last(k),
                                wp[:, k % W_RING, 2 * F + j:2 * F + j + 1], 0.0, ALU.add, ALU.max).then_inc(s_hh_dve, 1)

            def out_z(k):
                dve.wait_ge(s_y_e_ps, k + 1)
                if k >= Z_RING:
                    dve.wait_ge(s_o_ready, k - Z_RING + 1)
                V.scalar_tensor_tensor(out=z[:, k % Z_RING, :], in0=dux_ps[:, k % 2, 0:P], scalar=xs[:, k, D_MODEL + 1:D_MODEL + 2],
                                       in1=xs[:, k, 0:D_MODEL], op0=ALU.mult, op1=ALU.add).then_inc(s_z_ready, 1)
                dve.wait_ge(s_z_ready, k + 1)
                V.bn_stats(st_o[:, k, :], z[:, k % Z_RING, :]).then_inc(s_sto_ready, 1)
                dve.wait_ge(s_sto_ready, k + 1)
                V.bn_aggr(mv_o[:, k, :], st_o[:, k, :]).then_inc(s_mvo_ready, 1)

            def out_norm(m):
                dve.wait_ge(s_rstdo_ready, m + 1)
                for k in pair(m):
                    V.tensor_scalar(o_sb[:, k, :], z[:, k % Z_RING, :], mv_o[:, k, 0:1], rstd_o[:, k:k + 1], ALU.subtract,
                                    ALU.mult).then_inc(s_o_ready, 1)

            in_stats(0)
            in_stats(1)
            for k in range(4):
                in_norm(k)
            for k in range(NS):
                if k % 2 == 0 and k // 2 + 2 < N_PAIRS:
                    in_stats(k // 2 + 2)
                relu_last(k)
                if k >= 1:
                    out_z(k - 1)
                if k % 2 == 1:
                    for i in (k + 3, k + 4):
                        if i < NS:
                            in_norm(i)
                elif k >= 4:
                    out_norm((k - 4) // 2)
            out_z(NS - 1)
            for m in range((NS - 5) // 2 + 1, N_PAIRS):
                out_norm(m)

        @block.gpsimd
        def _(pool):
            G_ = nc.gpsimd

            def rest(g, n, part):
                src, parts = ((delta, delta_p), (du, du_p))[n]
                pool.wait_ge(s_part_ready, 4 * g + 2 * n + part + 1)
                flat = lambda t, i: t[:, i, :, :].rearrange("p h t -> p (h t)")
                dst = flat(src, 1) if part == 0 else flat(parts, 2)
                if part:
                    pool.wait_ge(s_rest_ready, 4 * g + 2 * n + 1)
                    if 16 * 2 * PARTS * NR * g > 0:
                        pool.wait_ge(s_parts_in, 16 * 2 * PARTS * NR * g)
                G_.tensor_tensor(dst, flat(src, part), flat(parts, part), ALU.subtract).then_inc(s_rest_ready, 1)

            def c_times_s(G):
                g = G // GROUPS
                pool.wait_ge(s_scan_done, G + 1)
                if G % GROUPS == 0:
                    pool.wait_ge(s_bc_ready, 32 * (g + 1))
                if G // NK - P_RING // NK + 1 > 0:
                    pool.wait_ge(s_ysum_done, G // NK - P_RING // NK + 1)
                G_.tensor_tensor(cs[:, G % P_RING, :], s_sb[:, G % S_RING, :], c_rep[:, buf(g), :], ALU.mult).then_inc(s_cs_ready, 1)

            def send_rows(g):
                pool.wait_ge(s_pos_ready, g + 1)
                pool.wait_ge(s_alpha_ready, g + 1)
                pool.wait_ge(s_x1_ready, g + 1)
                if g == 0:
                    pool.wait_ge(s_tok_ready, 2)
                for t in range(TT * g, TT * g + TT):
                    G_.indirect_dma_start(xs_dram, bass.IndirectOffsetOnAxis(ap=pos[:, t:t + 1], axis=0), rows[:, t, :], None).then_inc(s_scattered, 16)

            G_.dma_start(const_sb[:], consts).then_inc(s_late_in, 16)
            G_.dma_start(route_sb[:], route_c).then_inc(s_late_in, 16)
            G_.dma_start(tok[:], tok_c).then_inc(s_late_in, 16)
            G_.dma_start(w_out[:], out_w).then_inc(s_late_in, 16)
            pieces = {20: [lambda g: rest(g, 0, 0)], 21: [lambda g: rest(g, 0, 1)], 22: [lambda g: rest(g, 1, 0)],
                      23: [lambda g: rest(g, 1, 1)]}
            for s in sorted(pieces):
                for f in pieces[s]:
                    f(0)
            for G in range(NG):
                g, s = G // GROUPS, G % GROUPS
                c_times_s(G)
                if g + 1 < NCH:
                    for f in pieces.get(s, []):
                        f(g + 1)
                if g >= 1 and s == 28:
                    send_rows(g - 1)
            send_rows(NCH - 1)

            def b2_diag(k):
                pool.wait_ge(s_w_e[k % W_RING], 16 * (k // W_RING + 1))
                if k >= H_RING:
                    pool.wait_ge(s_y_e_ps, k - H_RING + 1)
                c = 2 * F + FJ + 2
                G_.tensor_scalar(b2d[:, k % H_RING, :], ident[:], wp[:, k % W_RING, c:c + 1], None, ALU.mult).then_inc(s_b2d_ready, 1)

            def store_rows(k):
                pool.wait_ge(s_o_ready, k + 1)
                G_.indirect_dma_start(out_rows, bass.IndirectOffsetOnAxis(ap=xs[:, k, D_MODEL:D_MODEL + 1].bitcast(U32), axis=0),
                                      o_sb[:, k, :], None, bounds_check=N_TOK - 1, oob_is_err=False).then_inc(s_stored, 16)

            for k in range(3):
                b2_diag(k)
            for k in range(NS):
                if k + 3 < NS:
                    b2_diag(k + 3)
                if k >= 4:
                    store_rows(k - 4)
            for k in range(NS - 4, NS):
                store_rows(k)


def kernel(**inputs):
    import numpy as np
    import concourse.bacc as bacc
    from concourse.bass_utils import run_bass_kernel_spmd

    a = {k: np.asarray(v) for k, v in inputs.items()}
    B, L, D = a["L0_attn_x"].shape
    NT = B * L // P
    NS = NT + E - 1
    y_order = np.arange(P).reshape(NR, NK, CG).transpose(1, 0, 2).reshape(-1)
    in_w = a["L0_attn_in_w"]
    w_r = in_w[:, D_INNER:].reshape(D, H, P)[:, :, y_order].reshape(D, D_INNER)
    w_out = a["L0_attn_out_w"].reshape(H, P, D)[:, y_order, :].transpose(1, 0, 2)
    by_half = lambda v: v.reshape(H, P, -1).transpose(1, 0, 2)
    a_log = a["L0_attn_A_log"].reshape(H, NR, NK, CG, D_STATE).transpose(4, 3, 0, 1, 2).reshape(P, GROUPS)
    w2 = a["L0_ffn_w2"].reshape(E, FJ, P, D).transpose(0, 2, 1, 3).reshape(E, P, FJ * D)
    b1 = a["L0_ffn_b1"].reshape(E, FJ, P).transpose(0, 2, 1)
    columns = [a[f"L0_ffn_{n}"][:, :, None] for n in ("ln_g", "ln_b", "b2")]
    w_pack = np.concatenate([a["L0_ffn_w1"], w2, b1, *columns], axis=2)
    sel = np.zeros((PARTS, NK, CG, NK, D_STATE, CG), np.float32)
    for k in range(NK):
        for i in range(CG):
            sel[:, k, i, k, :, i] = 1
    sely = np.zeros((D_STATE, CG, NR, NR, CG), np.float32)
    for r in range(NR):
        for i in range(CG):
            sely[:, i, r, r, i] = 1
    perm = np.zeros((P, P), np.float32)
    perm[y_order, np.arange(P)] = 1
    rows = lambda v: np.broadcast_to(v.astype(np.float32), (P, v.size))
    region = B * L + 2 * P
    consts = np.concatenate([sely.reshape(P, P), perm, np.triu(np.ones((P, P), np.float32), 1)], axis=1)
    route = np.concatenate([rows(np.arange(E)), rows(P * np.arange(NT)), rows(np.arange(NS)), rows(region * np.arange(E)),
                            rows(np.tile(region * np.arange(E), TT))], axis=1)
    tok = np.arange(NT)[None, :] * P + np.arange(P)[:, None]
    tok = np.concatenate([tok, np.full((P, 1), 2 * B * L)], axis=1).astype(np.uint32)
    small = np.concatenate([a["L0_attn_norm_w"][:, None], by_half(a["L0_attn_conv_w"]).reshape(P, -1),
                            by_half(a["L0_attn_conv_b"])[:, :, 0], by_half(a["L0_attn_dt_b"])[:, :, 0],
                            by_half(a["L0_attn_D"])[:, :, 0], a_log, a["L0_ffn_centroids"].T], axis=1)
    arrays = {
        "x": a["L0_attn_x"], "in_w": np.concatenate([w_r, in_w[:, :D_INNER]], axis=1),
        "x_proj_w": by_half(a["L0_attn_x_proj_w"]), "dt_w": a["L0_attn_dt_w"], "out_w": w_out, "small": small,
        "w_pack": w_pack, "ident_c": np.eye(P, dtype=np.float32), "sel_c": sel.reshape(PARTS * QROWS, NK, P),
        "route_c": route, "tok_c": tok, "consts": consts,
    }
    nc = bacc.Bacc("TRN2", target_bir_lowering=False, num_devices=1)
    feed, args = {}, []
    for name, v in arrays.items():
        v = np.ascontiguousarray(v)
        feed[f"in_{name}"] = v
        args.append(nc.dram_tensor(f"in_{name}", v.shape, mybir.dt.from_np(v.dtype), kind="ExternalInput").ap())
    args.append(nc.dram_tensor("out_0", (B, L, D), F32, kind="ExternalOutput").ap())
    args.append(nc.dram_tensor("xs_dram", (E * region, ROW), F32, kind="Internal").ap())
    fused_mamba_routed_ffn(nc, *args)
    r = run_bass_kernel_spmd(nc, [feed], core_ids=[0])
    return r.results[0]["out_0"]
```

```python
from contextlib import ExitStack

import concourse.bass as bass
from concourse import mybir

ALU = mybir.AluOpType
ACT = mybir.ActivationFunctionType
F32 = mybir.dt.float32
BF16 = mybir.dt.bfloat16
U32 = mybir.dt.uint32
AX_X = mybir.AxisListType.X

P = 128
D_MODEL = 128
D_INNER = 256
D_STATE = 16
DT_RANK = 64
D_CONV = 4
E = 8
F = 512
EPS = 1e-5

T = 512
TT = T // P
H = D_INNER // P
CG = P // D_STATE
NK = 4
NR = P // (CG * NK)
GROUPS = H * NR * NK
PARTS = 3
QROWS = NK * CG

DA_RING = 3
DUX_RING = 2
DBU_RING = 3
S_RING = 8
P_RING = 12
GATE_LAG = -1
CS_EVERY = 94
CS_LAST = 4
SUM_LAG = 6
FJ = F // P
ROW = D_MODEL + 2
W_ROW = 2 * F + FJ + 2
XS_RING = 8
W_RING = 6
ROWS_AHEAD = 8
XN_RING = 8
XT_RING = 3
H_RING = 3
Z_RING = 8


def fused_mamba_routed_ffn(nc, x, in_w, conv_w, x_proj_w, dt_w, out_w, small, w_pack, b2_rows, b2_pick, ident_c, sel_c, route_c, tok_c, consts, out, xs_dram):
    B, L, _ = x.shape
    CPB = L // T
    NCH = B * CPB
    NT = B * L // P
    NS = NT + E - 1
    NG = NCH * GROUPS
    REGION = B * L + 2 * P
    N_TOK = B * L
    NE = (N_TOK - T - E * (P - 1) + P - 1) // P
    NL = NS - NE

    x_v = x.rearrange("b (t p) d -> p (b t) d", p=P)
    out_rows = out.rearrange("b t d -> (b t) d")

    with ExitStack() as ctx:
        def sb(name, shape, dt=F32):
            return ctx.enter_context(nc.sbuf_tensor(name, shape, dt))

        def ps(name, shape, dt=F32):
            return ctx.enter_context(nc.psum_tensor(name, shape, dt))

        def sem(name):
            return ctx.enter_context(nc.semaphore(name))

        dA_ps = ps("dA_ps", [P, DA_RING, T])
        dux_ps = ps("dux_ps", [P, DUX_RING, T])
        y_ps = ps("y_ps", [P, T])
        m_ps = ps("m_ps", [P, 2, T])

        ident = sb("ident", [P, P])
        sel_f = sb("sel_f", [PARTS * QROWS, NK, P])
        sel = sb("sel", [PARTS * QROWS, NK, P], BF16)
        const_sb = sb("const_sb", [P, consts.shape[1]])
        sely = const_sb[:, 0:NR * QROWS].rearrange("p (r m) -> p r m", r=NR)
        perm = const_sb[:, P:2 * P]
        ltri_f = const_sb[:, 2 * P:3 * P]
        route_sb = sb("route_sb", [P, route_c.shape[1]])
        taken_cols = [0]

        def view(t, n):
            taken_cols[0] += n
            return t[:, taken_cols[0] - n:taken_cols[0]]

        iota8 = view(route_sb, E)
        steps = view(route_sb, NT)
        kidx = view(route_sb, NS)
        region0 = view(route_sb, E)
        region_b = sb("region_b", [1, TT, E], BF16)
        tok = sb("tok", [P, NT + 1], U32)
        dperm = sb("dperm", [P, H, P])
        ltri = sb("ltri", [P, P], BF16)
        ones_b = sb("ones_b", [P, P], BF16)
        zeros = sb("zeros", [P, 8])
        zrow = sb("zrow", [P, 2, ROW])
        w_in = sb("w_in", [P, 2 * D_INNER])
        w_r, w_u = w_in[:, 0:D_INNER], w_in[:, D_INNER:2 * D_INNER]
        w_uk = sb("w_uk", [P, D_CONV, D_INNER])
        w_xp = sb("w_xp", [P, H, DT_RANK + 2 * D_STATE])
        w_dt = sb("w_dt", [DT_RANK, D_INNER])
        w_out = sb("w_out", [P, H, D_MODEL])
        small_sb = sb("small_sb", [P, small.shape[1]])
        taken_cols[0] = 0
        w_norm = view(small_sb, 1)
        b_conv = view(small_sb, H)
        b_dt = view(small_sb, H)
        d_in = view(small_sb, H)
        a_in = view(small_sb, GROUPS)
        cent = view(small_sb, E)
        a_exp = sb("a_exp", [P, GROUPS])
        a_neg = sb("a_neg", [P, GROUPS])

        x_sb = sb("x_sb", [P, NT, D_MODEL])
        junk = sb("junk", [P, TT, P])
        ss = sb("ss", [P, NT])
        lnss = sb("lnss", [P, NT])
        rms = sb("rms", [P, NT])
        h_sb = sb("h_sb", [P, TT, P])
        hT = sb("hT", [P, D_CONV - 1 + T])
        late = sb("late", [P, 2, 2, H, T])
        u_sb, yg = late[:, 0, :, :, :], late[:, 1, :, :, :]
        res_raw = sb("res_raw", [P, H, T])
        res_sb = sb("res_sb", [P, 2, H, T])
        xdbl = sb("xdbl", [DT_RANK + 2 * D_STATE, T])
        b_rep = sb("b_rep", [P, 2, T])
        c_rep = sb("c_rep", [P, 2, T])
        early_sb = sb("early", [P, max(6 * H * T, W_RING * W_ROW)])
        early = early_sb[:, 0:6 * H * T].rearrange("p (a h t) -> p a h t", a=6, h=H)
        delta, du = early[:, 0:2, :, :], early[:, 2:4, :, :]
        dt_abs, dt_pos = early[:, 4, :, :], early[:, 5, :, :]
        delta_p = sb("delta_p", [P, PARTS, H, T], BF16)
        du_p = sb("du_p", [P, PARTS, H, T], BF16)
        delta_q = sb("delta_q", [PARTS * QROWS, 2, H * NR, T], BF16)
        du_q = sb("du_q", [PARTS * QROWS, 2, H * NR, T], BF16)
        dbu = sb("dbu", [P, DBU_RING, T])
        s_sb = sb("s_sb", [P, S_RING, T])
        carry = sb("carry", [P, GROUPS])
        cs = sb("cs", [P, P_RING, T])
        v_sb = sb("v_sb", [P, TT, P])
        st = sb("st", [P, TT, 6])
        mv = sb("mv", [P, TT, 2])
        lnv = sb("lnv", [P, TT])
        rstd = sb("rstd", [P, TT])
        nmr = sb("nmr", [P, TT])
        rows = sb("rows", [P, NT, ROW])
        x2 = rows[:, :, 0:D_MODEL]
        x1T = sb("x1T", [P, T])
        aff = sb("aff", [P, TT, E])
        top = sb("top", [P, NT, 8])
        topi = sb("topi", [P, TT, 8], U32)
        eid = sb("eid", [P, TT])
        onehot = sb("onehot", [P, NT, E], BF16)

        eps_t = sb("eps_t", [P, 1])
        eps_ap = eps_t[:, 0:1]
        eps4_t = sb("eps4_t", [P, 1])
        eps4_ap = eps4_t[:, 0:1]
        epsq_t = sb("epsq_t", [P, 1])
        epsq_ap = epsq_t[:, 0:1]
        ones8 = sb("ones8", [P, E])
        one_ap = ones8[:, 0:1]
        al_e = sb("al_e", [P, TT])
        al_1 = sb("al_1", [P, TT])
        rank = sb("rank", [P, TT, E])
        posf = sb("posf", [P, TT])
        pos = sb("pos", [P, NT], U32)
        cnt_e = sb("cnt_e", [P, E])
        full = sb("full", [P, E, NT])
        nfull = sb("nfull", [P, E])
        fend = sb("fend", [P, E])
        fleft = sb("fleft", [P, E])
        taken = sb("taken", [P, E])
        taken0 = sb("taken0", [P, 1])
        jump_e = sb("jump_e", [P, E])
        beyond_e = sb("beyond_e", [P, NE, E])
        jumps_e = sb("jumps_e", [P, NE, E])
        etf_e = sb("etf_e", [P, NE])
        rowf_e = sb("rowf_e", [P, 2, NE])
        et_e = sb("et_e", [P, NE], U32)
        row0_e = sb("row0_e", [P, NE], U32)
        nleft = sb("nleft", [P, E])
        cnt = sb("cnt", [P, E])
        fill_row = sb("fill_row", [P, E], U32)
        past = sb("past", [P, E, NT])
        ntile = sb("ntile", [P, E])
        tend = sb("tend", [P, E])
        jump = sb("jump", [P, E])
        lim = sb("lim", [P, 1])
        beyond = sb("beyond", [P, NL, E])
        etf = sb("etf", [P, NL])
        et = sb("et", [P, NL], U32)
        jumps = sb("jumps", [P, NL, E])
        rowf = sb("rowf", [P, NL])
        row0 = sb("row0", [P, NL], U32)
        b2_f = sb("b2_f", [PARTS * E, D_MODEL])
        b2_of = sb("b2_of", [PARTS * E, PARTS + 1])
        b2_part = sb("b2_part", [PARTS * E, 2, D_MODEL], BF16)
        b2_rest = sb("b2_rest", [PARTS * E, 2, D_MODEL])
        b2_acc = sb("b2_acc", [PARTS * E, 2, D_MODEL])
        b2_p = sb("b2_p", [PARTS * E, D_MODEL], BF16)
        b2_on = sb("b2_on", [PARTS * E, NS], BF16)
        flat = lambda t: t.rearrange("p a b c -> p (a b c)")
        xs = cs[:].rearrange("p a t -> p (a t)")[:, 0:NS * ROW].rearrange("p (k d) -> p k d", d=ROW)
        wp = early_sb[:, 0:W_RING * W_ROW].rearrange("p (k f) -> p k f", f=W_ROW)
        s_flat = s_sb[:].rearrange("p a t -> p (a t)")
        hh = s_flat[:, 0:H_RING * F].rearrange("p (k j d) -> p k j d", k=H_RING, d=P)
        s_off = H_RING * F
        xn = s_flat[:, s_off:s_off + XN_RING * P].rearrange("p (k d) -> p k d", d=P)
        s_off += XN_RING * P
        xsT = s_flat[:, s_off:s_off + XT_RING * P].rearrange("p (k d) -> p k d", d=P)
        z = dbu[:].rearrange("p a t -> p (a t)")[:, 0:Z_RING * P].rearrange("p (k d) -> p k d", d=P)
        o_sb = late[:].rearrange("p a b c t -> p (a b c t)")[:, 0:NS * P].rearrange("p (k d) -> p k d", d=P)
        st_i = sb("st_i", [P, NS, 6])
        mv_i = sb("mv_i", [P, NS, 2])
        ln_i = sb("ln_i", [P, NS])
        rstd_i = sb("rstd_i", [P, NS])
        st_o = sb("st_o", [P, NS, 6])
        mv_o = sb("mv_o", [P, NS, 2])
        ln_o = sb("ln_o", [P, NS])
        rstd_o = sb("rstd_o", [P, NS])

        s_x_in = [sem(f"x_in{g}") for g in range(NCH)]
        s_ident_in = sem("ident_in")
        s_in_w_in = sem("in_w_in")
        s_taps_in = sem("taps_in")
        s_w_uk_ready = sem("w_uk_ready")
        s_small_in = sem("small_in")
        s_xp_in = sem("xp_in")
        s_dt_in = sem("dt_in")
        s_sel_in = sem("sel_in")
        s_late_in = sem("late_in")
        s_vconst_ready = sem("vconst_ready")
        s_dperm_ready = sem("dperm_ready")
        s_tok_ready = sem("tok_ready")
        s_const_ready = sem("const_ready")
        s_aneg_ready = sem("aneg_ready")
        s_ss_ready = sem("ss_ready")
        s_lnss_ready = sem("lnss_ready")
        s_rms_ready = sem("rms_ready")
        s_h_ready = sem("h_ready")
        s_hT_ps = sem("hT_ps")
        s_hT_ready = sem("hT_ready")
        s_res_ps = sem("res_ps")
        s_res_raw_ready = sem("res_raw_ready")
        s_u_ps = sem("u_ps")
        s_u_ready = sem("u_ready")
        s_res_ready = sem("res_ready")
        s_xdbl_ps = sem("xdbl_ps")
        s_xdbl_ready = sem("xdbl_ready")
        s_bc_ready = sem("bc_ready")
        s_dt_ps = sem("dt_ps")
        s_dt_parts = sem("dt_parts")
        s_dt_exp = sem("dt_exp")
        s_dt_log = sem("dt_log")
        s_delta_ready = sem("delta_ready")
        s_du_ready = sem("du_ready")
        s_part_ready = [sem(f"part_ready{n}") for n in range(2)]
        s_rest_ready = [sem(f"rest_ready{n}") for n in range(2)]
        s_parts_in = [sem(f"parts_in{r}") for r in range(NR)]
        s_dlx_ready = sem("dlx_ready")
        s_dA_ready = sem("dA_ready")
        s_dux_ready = sem("dux_ready")
        s_dbu_done = sem("dbu_done")
        s_scan_done = sem("scan_done")
        s_carry_done = sem("carry_done")
        s_cs_pool = sem("cs_pool")
        s_cs_dve = sem("cs_dve")
        s_ysum_done = sem("ysum_done")
        s_yg_ready = sem("yg_ready")
        s_out_ps = sem("out_ps")
        s_v_ready = sem("v_ready")
        s_st_done = sem("st_done")
        s_mv_done = sem("mv_done")
        s_lnv_ready = sem("lnv_ready")
        s_rstd_ready = sem("rstd_ready")
        s_shift_ready = sem("shift_ready")
        s_x1_ready = sem("x1_ready")
        s_x1T_ps = sem("x1T_ps")
        s_x1T_ready = sem("x1T_ready")
        s_aff_ps = sem("aff_ps")
        s_aff_ready = sem("aff_ready")
        s_top_ready = sem("top_ready")
        s_topi_ready = sem("topi_ready")
        s_eid_ready = sem("eid_ready")
        s_onehot_ready = sem("onehot_ready")
        s_al_ready = sem("al_ready")
        s_al1_ready = sem("al1_ready")
        s_alpha_ready = sem("alpha_ready")
        s_rank_ps = sem("rank_ps")
        s_rank_ready = sem("rank_ready")
        s_posf_ready = sem("posf_ready")
        s_pos_ready = sem("pos_ready")
        s_count_ps = sem("count_ps")
        s_route = sem("route")
        s_fill_ready = sem("fill_ready")
        s_slots_ready = sem("slots_ready")
        s_filled = sem("filled")
        s_scattered = sem("scattered")
        s_last_scattered = sem("last_scattered")
        s_early = sem("early_step")
        s_early_count_ps = sem("early_count_ps")
        s_early_ready = sem("early_ready")
        s_halo_ready = sem("halo_ready")
        s_xs_in = [sem(f"xs_in{i}") for i in range(XS_RING)]
        s_w_e = [sem(f"w_e{i}") for i in range(W_RING)]
        s_sti_ready = sem("sti_ready")
        s_mvi_ready = sem("mvi_ready")
        s_lni_ready = sem("lni_ready")
        s_rstdi_ready = sem("rstdi_ready")
        s_xn_ready = sem("xn_ready")
        s_xsT_ps = sem("xsT_ps")
        s_xsT_ready = sem("xsT_ready")
        s_h_ps = sem("h_ps")
        s_h_last_ps = sem("h_last_ps")
        s_hh_act = sem("hh_act")
        s_hh_dve = sem("hh_dve")
        s_b2_step = sem("b2_step")
        s_b2_ready = sem("b2_ready")
        s_y_e_ps = sem("y_e_ps")
        s_z_ready = sem("z_ready")
        s_sto_ready = sem("sto_ready")
        s_mvo_ready = sem("mvo_ready")
        s_lno_ready = sem("lno_ready")
        s_rstdo_ready = sem("rstdo_ready")
        s_o_ready = sem("o_ready")
        s_stored = sem("stored")

        block = ctx.enter_context(nc.Block())

        def buf(g):
            return g % 2

        def tiles(g):
            return slice(TT * g, TT * g + TT)

        PAIRS = [range(k, min(k + 2, NE)) for k in range(0, NE, 2)] + [range(k, min(k + 2, NS)) for k in range(NE, NS, 2)]
        PAIRS_E = (NE + 1) // 2
        PAIR_OF = [m for m, ks in enumerate(PAIRS) for _ in ks]
        STATS_AT = [NE - 2, NE - 2, NE - 1] + [NE + 2 * j for j in range(len(PAIRS) - PAIRS_E - 3)]
        NORM_AT = STATS_AT[:3] + [k + 1 for k in STATS_AT[3:]]

        def pairs_at(steps_of, k):
            return [PAIRS_E + j for j, at in enumerate(steps_of) if at == k]

        def registers(engine, values, k, most):
            _, r = nc.values_load_multi_w_load_instructions(values[0:1, k:min(k + 4, values.shape[1])],
                                                            engines=[engine], min_val=0, max_val=most)
            return r

        def fill_rows(eng, rows_of_fill):
            for row in rows_of_fill:
                eng.dma_start(xs_dram[bass.ds(row, 2 * P), :].rearrange("(p a) d -> p a d", a=2), zrow[:]).then_inc(s_filled, 16)

        def on_dve(G):
            return G % CS_EVERY == CS_EVERY - 1 or (G >= NG - CS_LAST and G % 2 == 1)

        def n_cs_dve(n):
            return sum(1 for G in range(n) if on_dve(G))

        def n_cs_pool(n):
            return n - n_cs_dve(n)

        def h_last(k):
            return (y_ps[:] if k % 2 else dA_ps[:, 2, :])[:, 0:P]

        @block.sync
        def _(sp):
            sp.dma_start(x_sb[:, tiles(0), :], x_v[:, tiles(0), :]).then_inc(s_x_in[0], 16)
            sp.dma_start(ident[:], ident_c).then_inc(s_ident_in, 16)
            sp.dma_start(w_in[:], in_w).then_inc(s_in_w_in, 16)
            sp.dma_start(w_uk[:].rearrange("p k c -> p (k c)"), conv_w.to_broadcast([P, D_CONV * D_INNER])).then_inc(s_taps_in, 16)
            sp.dma_start(w_xp[:], x_proj_w).then_inc(s_xp_in, 16)
            sp.dma_start(w_dt[:], dt_w).then_inc(s_dt_in, 16)
            sp.dma_start(sel_f[:], sel_c).then_inc(s_sel_in, 16)
            for g in range(1, NCH):
                sp.dma_start(x_sb[:, tiles(g), :], x_v[:, tiles(g), :]).then_inc(s_x_in[g], 16)

            def bc(g):
                sp.wait_ge(s_xdbl_ready, g + 1)
                if g >= 2:
                    sp.wait_ge(s_cs_pool, n_cs_pool(GROUPS * (g - 1)))
                    sp.wait_ge(s_cs_dve, n_cs_dve(GROUPS * (g - 1)))
                if GROUPS * (g - 1) > 0:
                    sp.wait_ge(s_dbu_done, GROUPS * (g - 1))
                for row, dst in ((DT_RANK, b_rep), (DT_RANK + D_STATE, c_rep)):
                    src = xdbl[row:row + D_STATE, :].unsqueeze(1).to_broadcast([D_STATE, CG, T])
                    sp.dma_start(dst[:, buf(g), :], src).then_inc(s_bc_ready, 16)

            def parts(g):
                if GROUPS * (g - 1) > 0:
                    sp.wait_ge(s_dux_ready, GROUPS * (g - 1))
                def move(n, part, r):
                    if part < 2:
                        sp.wait_ge(s_part_ready[n], 2 * g + part + 1)
                    else:
                        sp.wait_ge(s_rest_ready[n], 2 * g + 2)
                    src, dst = ((delta_p, delta_q), (du_p, du_q))[n]
                    sp.dma_start(dst[part * QROWS:(part + 1) * QROWS, buf(g), r::NR, :],
                                 src[r * QROWS:(r + 1) * QROWS, part, :, :]).then_inc(s_parts_in[r], 16)

                for n, r in ((0, 0), (0, 1), (0, 2), (0, 3), (1, 0), (1, 1)):
                    move(n, 0, r)
                for r in range(NR):
                    if r >= 2:
                        move(1, 0, r)
                    for part in range(1, PARTS):
                        for n in range(2):
                            move(n, part, r)

            for g in range(NCH):
                bc(g)
                parts(g)

            def load_rows(k, row):
                if k >= XS_RING:
                    sp.wait_ge(s_xn_ready, k - XS_RING + 1)
                sp.dma_start(xs[:, k, :], xs_dram[bass.ds(row, P), :]).then_inc(s_xs_in[k % XS_RING], 16)

            def load_weights(k, e):
                if k >= W_RING:
                    sp.wait_ge(s_y_e_ps, k - W_RING + 1)
                sp.dma_start(wp[:, k % W_RING, :], w_pack[bass.ds(e, 1), :, :].rearrange("e p f -> (e p) f")).then_inc(s_w_e[k % W_RING], 16)

            SP = mybir.EngineType.SP
            sp.wait_ge(s_early_ready, 2)
            row_of = [r for k in range(0, NE, 4) for r in registers(SP, row0_e, k, E * REGION - P)]
            expert_of = [e for k in range(0, NE, 4) for e in registers(SP, et_e, k, E - 1)]
            sp.wait_ge(s_scattered, 16 * (NT - TT))
            sp.wait_ge(s_ysum_done, NG // NK)
            for k in range(NE):
                load_rows(k, row_of[k])
                load_weights(k, expert_of[k])
            sp.wait_ge(s_fill_ready, 1)
            fill_rows(sp, registers(SP, fill_row, 0, E * REGION - 2 * P))
            sp.wait_ge(s_slots_ready, 2)
            expert_of = registers(SP, et, 0, E - 1)
            row_of = [registers(SP, row0, k, E * REGION - P) for k in (0, 4)]
            load_weights(NE, expert_of[0])
            sp.wait_ge(s_filled, 16 * E)
            sp.wait_ge(s_last_scattered, 16 * TT)
            for i in range(ROWS_AHEAD):
                load_rows(NE + i, row_of[i // 4][i % 4])
                if i == 2 or i == 4:
                    load_weights(NE + i // 2, expert_of[i // 2])
            row_of = row_of[1]
            for i in range(3, NL):
                if i % 4 == 0:
                    expert_of = registers(SP, et, i, E - 1)
                load_weights(NE + i, expert_of[i % 4])
                r = i + ROWS_AHEAD - 3
                if r < NL:
                    if r % 4 == 0:
                        row_of = registers(SP, row0, r, E * REGION - P)
                    load_rows(NE + r, row_of[r % 4])
            sp.wait_ge(s_stored, 16 * NS)

        @block.tensor
        def _(pe):
            mm = nc.tensor.matmul

            def hT_fill(g):
                if g == 0:
                    pe.wait_ge(s_ident_in, 16)
                pe.wait_ge(s_h_ready, g + 1)
                if g == 1:
                    pe.wait_ge(s_res_raw_ready, 2)
                if g >= 3:
                    pe.wait_ge(s_aff_ready, g - 2)
                if 2 * g > 0:
                    pe.wait_ge(s_dt_parts, 2 * g)
                for j in range(TT):
                    last = nc.tensor.transpose(m_ps[:, 0, j * P:(j + 1) * P], h_sb[:, j, :], ident[:])
                last.then_inc(s_hT_ps, 1)

            def res_fill(g, h):
                if g == 0:
                    pe.wait_ge(s_dt_parts, h + 1)
                elif h == 0:
                    pe.wait_ge(s_hT_ready, g + 1)
                    pe.wait_ge(s_dt_parts, 2 * g - 1)
                    if g == 1:
                        pe.wait_ge(s_res_raw_ready, 1)
                    if g >= 3:
                        pe.wait_ge(s_rank_ready, g - 2)
                mm(m_ps[:, 1 - h, :], w_r[:, h * P:(h + 1) * P], hT[:, D_CONV - 1:], start=True, stop=True).then_inc(s_res_ps, 1)

            def u_fill(g, h, k):
                if g == 0:
                    pe.wait_ge(s_w_uk_ready, 1)
                if k == 0 and g > 0:
                    pe.wait_ge(s_res_raw_ready, 2 * g + h + 1)
                if k == 0 and g == 0:
                    pe.wait_ge(s_in_w_in, 16)
                    pe.wait_ge(s_hT_ready, 1)
                last = mm(m_ps[:, 1 - h, :], w_uk[:, k, h * P:(h + 1) * P], hT[:, k:k + T], start=(k == 0), stop=(k == D_CONV - 1),
                          skip_group_check=True)
                if k == D_CONV - 1:
                    last.then_inc(s_u_ps, 1)

            def xdbl_fill(g):
                if g == 0:
                    pe.wait_ge(s_xp_in, 16)
                pe.wait_ge(s_u_ready, 2 * g + 2)
                n = DT_RANK + 2 * D_STATE
                for h in range(H):
                    last = mm(m_ps[0:n, 1, :], w_xp[:, h, :], u_sb[:, buf(g), h, :], start=(h == 0), stop=(h == H - 1))
                last.then_inc(s_xdbl_ps, 1)

            def dt_fill(g, h):
                if g == 0:
                    pe.wait_ge(s_dt_in, 16)
                pe.wait_ge(s_xdbl_ready, g + 1)
                if h == 1 and g >= 2:
                    pe.wait_ge(s_v_ready, g - 1)
                mm(m_ps[:, 1 - h, :], w_dt[:, h * P:(h + 1) * P], xdbl[0:DT_RANK, :], start=True, stop=True).then_inc(s_dt_ps, 1)

            def out_fill(g):
                pe.wait_ge(s_yg_ready, H * (g + 1))
                pe.wait_ge(s_u_ready, min(2 * (g + 3), 2 * NCH))
                if g > 0:
                    pe.wait_ge(s_aff_ready, g)
                for j in range(TT):
                    for h in range(H):
                        last = mm(m_ps[:, 0, j * P:(j + 1) * P], yg[:, buf(g), h, j * P:(j + 1) * P], w_out[:, h, :],
                                  start=(h == 0), stop=(h == H - 1))
                last.then_inc(s_out_ps, 1)

            def x1T_fill(g):
                pe.wait_ge(s_x1_ready, g + 1)
                pe.wait_ge(s_dt_parts, min(2 * (g + 3), 2 * NCH) - 1)
                if g == NCH - 1:
                    pe.wait_ge(s_early, 1)
                if g > 0:
                    pe.wait_ge(s_rank_ready, g)
                for j in range(TT):
                    last = nc.tensor.transpose(m_ps[:, 1, j * P:(j + 1) * P], x2[:, TT * g + j, :], ident[:])
                last.then_inc(s_x1T_ps, 1)

            def aff_fill(g):
                pe.wait_ge(s_x1T_ready, g + 1)
                pe.wait_ge(s_dt_parts, min(2 * (g + 3), 2 * NCH))
                for j in range(TT):
                    last = mm(m_ps[:, 0, j * E:(j + 1) * E], x1T[:, j * P:(j + 1) * P], cent[:], start=True, stop=True)
                last.then_inc(s_aff_ps, 1)

            def rank_fill(g):
                pe.wait_ge(s_onehot_ready, g + 1)
                pe.wait_ge(s_x1T_ready, g + 1)
                o = m_ps[:, 1, 0:TT * E]
                mm(o, ones_b[0:1, :], region_b[:].rearrange("p t e -> p (t e)"), start=True, stop=False, skip_group_check=True)
                for t in range(TT * g):
                    mm(o.rearrange("p (t e) -> p t e", t=TT), ones_b[:], onehot[:, t:t + 1, :].to_broadcast([P, TT, E]),
                       start=False, stop=False, skip_group_check=True)
                for j in range(1, TT):
                    mm(m_ps[:, 1, j * E:TT * E].rearrange("p (t e) -> p t e", e=E), ones_b[:], onehot[:, TT * g:TT * g + TT - j, :],
                       start=False, stop=False, skip_group_check=True)
                last = mm(o.rearrange("p (t e) -> p t e", t=TT), ltri[:], onehot[:, tiles(g), :], start=False, stop=True,
                          skip_group_check=True)
                if g == NCH - 2:
                    n = TT * (NCH - 1)
                    for t in range(n):
                        last = mm(m_ps[:, 1, TT * E:TT * E + E], ones_b[:], onehot[:, t, :], start=(t == 0), stop=(t == n - 1),
                                  skip_group_check=True)
                last.then_inc(s_rank_ps, 1)

            def count_fill():
                pe.wait_ge(s_yg_ready, H * NCH)
                o = y_ps[:, 0:E]
                for t in range(NT):
                    last = mm(o, ones_b[:], onehot[:, t, :], start=(t == 0), stop=(t == NT - 1))
                last.then_inc(s_count_ps, 1)

            def expand(G):
                g, q, k = G // GROUPS, G % GROUPS // NK, G % NK
                if G == 0:
                    pe.wait_ge(s_const_ready, 1)
                if G % NK == 0 and q < NR:
                    pe.wait_ge(s_parts_in[q], 16 * 2 * PARTS * (g + 1))
                if G - DA_RING + 1 > 0:
                    pe.wait_ge(s_scan_done, G - DA_RING + 1)
                mm(dA_ps[:, G % DA_RING, :], sel[:, k, :], delta_q[:, buf(g), q, :], start=True, stop=True).then_inc(s_dlx_ready, 1)
                if G - DUX_RING + 1 > 0:
                    pe.wait_ge(s_dbu_done, G - DUX_RING + 1)
                mm(dux_ps[:, G % DUX_RING, :], sel[:, k, :], du_q[:, buf(g), q, :], start=True, stop=True).then_inc(s_dux_ready, 1)

            def state_sum(Q):
                g, h, r = Q // (H * NR), Q // NR % H, Q % NR
                if r == 0:
                    if Q // NR > 0:
                        pe.wait_ge(s_yg_ready, Q // NR)
                    else:
                        pe.wait_ge(s_dperm_ready, 1)
                    mm(y_ps[:], dperm[:, h, :], u_sb[:, buf(g), h, :], start=True, stop=False, skip_group_check=True)
                pe.wait_ge(s_cs_pool, n_cs_pool(NK * (Q + 1)))
                if n_cs_dve(NK * (Q + 1)) > 0:
                    pe.wait_ge(s_cs_dve, n_cs_dve(NK * (Q + 1)))
                for k in range(NK):
                    last = mm(y_ps[k * QROWS:(k + 1) * QROWS, :], sely[:, r, :], cs[:, (Q * NK + k) % P_RING, :], start=False,
                              stop=(r == NR - 1), skip_group_check=True, tile_position=(0, k * QROWS))
                last.then_inc(s_ysum_done, 1)

            pieces = [
                (0, 1, lambda g: res_fill(g, 0)), (2, 1, lambda g: res_fill(g, 1)),
                (3, 1, lambda g: u_fill(g, 0, 0)), (4, 1, lambda g: u_fill(g, 0, 1)), (6, 1, lambda g: u_fill(g, 0, 2)),
                (7, 1, lambda g: u_fill(g, 0, 3)), (8, 1, lambda g: u_fill(g, 1, 0)), (10, 1, lambda g: u_fill(g, 1, 1)),
                (11, 1, lambda g: u_fill(g, 1, 2)), (13, 1, lambda g: u_fill(g, 1, 3)), (15, 1, xdbl_fill), (15, -1, out_fill),
                (17, 1, lambda g: dt_fill(g, 0)), (18, 1, lambda g: dt_fill(g, 1)), (23, -1, x1T_fill), (28, -1, aff_fill),
                (30, -1, rank_fill), (31, 2, hT_fill)]
            hT_fill(0)
            for h in range(H):
                for k in range(D_CONV):
                    u_fill(0, h, k)
            xdbl_fill(0)
            for h in range(H):
                dt_fill(0, h)
            for h in range(H):
                res_fill(0, h)
            hT_fill(1)
            for G in range(NG):
                g, s = G // GROUPS, G % GROUPS
                expand(G)
                Gs = G - SUM_LAG
                if Gs >= 0 and Gs % NK == NK - 1:
                    state_sum(Gs // NK)
                for at, ahead, piece in pieces:
                    if at == s and 0 <= g + ahead < NCH:
                        piece(g + ahead)
            for Q in range((NG - SUM_LAG - NK) // NK + 1, NG // NK):
                state_sum(Q)
            for at, ahead, piece in pieces:
                if ahead == -1:
                    piece(NCH - 1)

            count_fill()

            def ffn_T(k):
                pe.wait_ge(s_xn_ready, k + 1)
                if k >= 2:
                    pe.wait_ge(s_xsT_ready, k - 1)
                elif k == 1:
                    pe.wait_ge(s_rank_ready, NCH)
                nc.tensor.transpose(m_ps[:, k % 2, 0:P], xn[:, k % XN_RING, :], ident[:]).then_inc(s_xsT_ps, 1)

            def ffn_up(k):
                pe.wait_ge(s_xsT_ready, k + 1)
                pe.wait_ge(s_w_e[k % W_RING], 16 * (k // W_RING + 1))
                if k >= 2:
                    pe.wait_ge(s_hh_dve, k - 1)
                elif k == 1:
                    pe.wait_ge(s_route, 1)
                mm(h_last(k), wp[:, k % W_RING, (FJ - 1) * P:FJ * P], xsT[:, k % XT_RING, :], start=True, stop=True).then_inc(s_h_last_ps, 1)
                if k >= 2:
                    pe.wait_ge(s_hh_act, (FJ - 1) * (k - 1))
                for j in range(FJ - 1):
                    last = mm(dA_ps[:, k % 2, j * P:(j + 1) * P], wp[:, k % W_RING, j * P:(j + 1) * P], xsT[:, k % XT_RING, :],
                              start=True, stop=True)
                last.then_inc(s_h_ps, 1)

            def ffn_down(k):
                if k == 0:
                    pe.wait_ge(s_b2_ready, 2)
                if k == NE:
                    pe.wait_ge(s_b2_ready, 3)
                if k >= 2:
                    pe.wait_ge(s_z_ready, k - 1)
                o = dux_ps[:, k % 2, 0:P]
                mm(o, b2_on[:, k:k + 1].to_broadcast([PARTS * E, P]), b2_p[:], start=True, stop=False)
                pe.wait_ge(s_hh_act, (FJ - 1) * (k + 1))
                pe.wait_ge(s_hh_dve, k + 1)
                for j in range(FJ):
                    last = mm(o, hh[:, k % H_RING, j, :], wp[:, k % W_RING, F + j * P:F + (j + 1) * P], start=False, stop=(j == FJ - 1))
                last.then_inc(s_y_e_ps, 1)

            ffn_T(0)
            ffn_T(1)
            for k in range(NS + 1):
                if k < NS:
                    ffn_up(k)
                if k >= 1:
                    ffn_down(k - 1)
                if k + 2 < NS:
                    ffn_T(k + 2)

        @block.scalar
        def _(act):
            A = nc.scalar.activation

            def ln_exp():
                nc.scalar.preload_act_table_set("natural_log_exp_and_others")

            def rms_scale(g):
                act.wait_ge(s_x_in[g], 16)
                if TT * g > 0:
                    act.wait_ge(s_ss_ready, TT * g)
                for j in range(TT):
                    A(junk[:, j, :], x_sb[:, TT * g + j, :], ACT.Square, accum_out=ss[:, TT * g + j:TT * g + j + 1]).then_inc(s_ss_ready, 1)
                act.wait_ge(s_ss_ready, TT * (g + 1))
                A(lnss[:, tiles(g)], ss[:, tiles(g)], ACT.Ln, scale=1.0 / D_MODEL, bias=eps_ap).then_inc(s_lnss_ready, 1)
                act.wait_ge(s_lnss_ready, g + 1)
                A(rms[:, tiles(g)], lnss[:, tiles(g)], ACT.Exp, scale=-0.5).then_inc(s_rms_ready, 1)
                act.wait_ge(s_rms_ready, g + 1)
                if g > 0:
                    act.wait_ge(s_hT_ps, g)
                if g > 0:
                    act.wait_ge(s_h_ready, g)
                for j in range(TT):
                    last = A(h_sb[:, j, :], x_sb[:, TT * g + j, :], ACT.Copy, scale=rms[:, TT * g + j:TT * g + j + 1])
                last.then_inc(s_h_ready, 1)

            def hT_copy(g):
                if g == 0:
                    act.wait_ge(s_small_in, 16)
                act.wait_ge(s_hT_ps, g + 1)
                if g == 1:
                    act.wait_ge(s_res_ps, 2)
                if 2 * g > 0:
                    act.wait_ge(s_u_ps, 2 * g)
                if g % CPB == 0:
                    A(hT[:, 0:D_CONV - 1], zeros[:, 0:D_CONV - 1], ACT.Copy).then_inc(s_halo_ready, 1)
                else:
                    A(hT[:, 0:D_CONV - 1], hT[:, T:T + D_CONV - 1], ACT.Copy).then_inc(s_halo_ready, 1)
                act.wait_ge(s_halo_ready, g + 1)
                A(hT[:, D_CONV - 1:], m_ps[:, 0, :], ACT.Copy, scale=w_norm[:, 0:1]).then_inc(s_hT_ready, 1)

            def res_copy(g, h):
                act.wait_ge(s_res_ps, 2 * g + h + 1)
                A(res_raw[:, h, :], m_ps[:, 1 - h, :], ACT.Copy).then_inc(s_res_raw_ready, 1)

            def silu_u(g):
                if g >= 2:
                    act.wait_ge(s_ysum_done, H * NR * (g - 1))
                for h in range(H):
                    act.wait_ge(s_u_ps, 2 * g + h + 1)
                    A(u_sb[:, buf(g), h, :], m_ps[:, 1 - h, :], ACT.Silu, bias=b_conv[:, h:h + 1]).then_inc(s_u_ready, 1)

            def silu_res(g):
                if H * (g - 1) > 0:
                    act.wait_ge(s_yg_ready, H * (g - 1))
                act.wait_ge(s_res_raw_ready, 2 * g + 2)
                A(res_sb[:, buf(g), :, :], res_raw[:], ACT.Silu).then_inc(s_res_ready, 1)

            def silu(g):
                silu_u(g)
                silu_res(g)
                ln_exp()

            def xdbl_copy(g):
                act.wait_ge(s_xdbl_ps, g + 1)
                if 32 * g > 0:
                    act.wait_ge(s_bc_ready, 32 * g)
                if 2 * g > 0:
                    act.wait_ge(s_dt_ps, 2 * g)
                A(xdbl[:], m_ps[0:DT_RANK + 2 * D_STATE, 1, :], ACT.Copy).then_inc(s_xdbl_ready, 1)

            def softplus_in(g, h):
                act.wait_ge(s_dt_ps, 2 * g + h + 1)
                if g > 0:
                    act.wait_ge(s_delta_ready, g)
                A(dt_abs[:, h, :], m_ps[:, 1 - h, :], ACT.Abs, bias=b_dt[:, h:h + 1])
                A(dt_pos[:, h, :], m_ps[:, 1 - h, :], ACT.Relu, bias=b_dt[:, h:h + 1]).then_inc(s_dt_parts, 1)

            def softplus_log(g):
                act.wait_ge(s_dt_parts, 2 * g + 2)
                A(dt_abs[:], dt_abs[:], ACT.Exp, scale=-1.0).then_inc(s_dt_exp, 1)
                act.wait_ge(s_dt_exp, g + 1)
                A(dt_abs[:], dt_abs[:], ACT.Ln, bias=one_ap).then_inc(s_dt_log, 1)

            def cast_part(g, n, part):
                src, parts = ((delta, delta_p), (du, du_p))[n]
                act.wait_ge(s_delta_ready if n == 0 else s_du_ready, g + 1)
                if part:
                    act.wait_ge(s_rest_ready[n], 2 * g + 1)
                if g > 0:
                    for r in range(NR):
                        act.wait_ge(s_parts_in[r], 16 * 2 * PARTS * g)
                A(parts[:, part, :, :], src[:, part, :, :], ACT.Copy).then_inc(s_part_ready[n], 1)

            def decay(G):
                act.wait_ge(s_dlx_ready, G + 1)
                A(dA_ps[:, G % DA_RING, :], dA_ps[:, G % DA_RING, :], ACT.Exp, scale=a_neg[:, G % GROUPS:G % GROUPS + 1]).then_inc(s_dA_ready, 1)

            def keep_state(G):
                if G >= 0 and G // GROUPS % CPB < CPB - 1:
                    act.wait_ge(s_scan_done, G + 1)
                    A(carry[:, G % GROUPS:G % GROUPS + 1], s_sb[:, G % S_RING, T - 1:T], ACT.Copy).then_inc(s_carry_done, 1)

            def rstd_of(g):
                act.wait_ge(s_mv_done, TT * (g + 1))
                A(lnv[:], mv[:, :, 1], ACT.Ln, scale=0.25, bias=epsq_ap).then_inc(s_lnv_ready, 1)
                act.wait_ge(s_lnv_ready, g + 1)
                A(rstd[:], lnv[:], ACT.Exp, scale=-0.5).then_inc(s_rstd_ready, 1)

            def normed(g):
                act.wait_ge(s_shift_ready, g + 1)
                for j in range(TT):
                    last = A(x2[:, TT * g + j, :], v_sb[:, j, :], ACT.Identity, scale=rstd[:, j:j + 1], bias=nmr[:, j:j + 1])
                last.then_inc(s_x1_ready, 1)

            def alpha_exp(g):
                act.wait_ge(s_top_ready, TT * (g + 1))
                if g > 0:
                    act.wait_ge(s_al1_ready, g)
                A(al_e[:], top[:, tiles(g), 0], ACT.Exp, scale=-0.5).then_inc(s_al_ready, 1)

            def x1T_copy(g):
                act.wait_ge(s_x1T_ps, g + 1)
                if g > 0:
                    act.wait_ge(s_aff_ps, g)
                A(x1T[:], m_ps[:, 1, :], ACT.Copy).then_inc(s_x1T_ready, 1)

            pieces = [
                (28, 2, rms_scale), (29, 2, hT_copy), (1, 1, lambda g: res_copy(g, 0)), (5, 1, lambda g: res_copy(g, 1)), (13, 1, silu),
                (15, 1, xdbl_copy), (20, -1, rstd_of), (21, -1, normed), (18, 1, lambda g: softplus_in(g, 0)), (19, 1, lambda g: softplus_in(g, 1)),
                (20, 1, softplus_log), (23, 1, lambda g: cast_part(g, 0, 0)), (26, -1, x1T_copy), (24, 1, lambda g: cast_part(g, 1, 0)),
                (23, 1, lambda g: cast_part(g, 0, 1)), (26, 1, lambda g: cast_part(g, 1, 1)), (28, -1, alpha_exp)]
            act.dma_start(small_sb[:], small).then_inc(s_small_in, 16)
            ln_exp()
            act.wait_ge(s_vconst_ready, 1)
            rms_scale(0)
            hT_copy(0)
            A(a_exp[:], a_in[:], ACT.Exp).then_inc(s_aneg_ready, 1)
            rms_scale(1)
            silu_u(0)
            ln_exp()
            xdbl_copy(0)
            for h in range(H):
                softplus_in(0, h)
            softplus_log(0)
            for part in range(2):
                for n in range(2):
                    cast_part(0, n, part)
            for h in range(H):
                res_copy(0, h)
            silu_res(0)
            hT_copy(1)
            ln_exp()
            act.wait_ge(s_aneg_ready, 2)
            for G in range(NG):
                g, s = G // GROUPS, G % GROUPS
                decay(G)
                keep_state(G - DA_RING)
                for at, ahead, piece in pieces:
                    if at == s and 0 <= g + ahead < NCH:
                        piece(g + ahead)

            def in_rstd(m):
                ks = PAIRS[m]
                act.wait_ge(s_mvi_ready, ks[-1] + 1)
                i = slice(ks[0], ks[-1] + 1)
                A(ln_i[:, i], mv_i[:, i, 1], ACT.Ln, bias=eps4_ap).then_inc(s_lni_ready, 1)
                act.wait_ge(s_lni_ready, m + 1)
                A(rstd_i[:, i], ln_i[:, i], ACT.Exp, scale=-0.5).then_inc(s_rstdi_ready, 1)

            def out_rstd(k):
                act.wait_ge(s_mvo_ready, k + 1)
                A(ln_o[:, k:k + 1], mv_o[:, k, 1:2], ACT.Ln, bias=eps_ap).then_inc(s_lno_ready, 1)
                act.wait_ge(s_lno_ready, k + 1)
                A(rstd_o[:, k:k + 1], ln_o[:, k:k + 1], ACT.Exp, scale=-0.5).then_inc(s_rstdo_ready, 1)

            def xsT_affine(k):
                act.wait_ge(s_xsT_ps, k + 1)
                act.wait_ge(s_w_e[k % W_RING], 16 * (k // W_RING + 1))
                if k >= XT_RING:
                    act.wait_ge(s_h_ps, k - XT_RING + 1)
                c = 2 * F + FJ
                A(xsT[:, k % XT_RING, :], m_ps[:, k % 2, 0:P], ACT.Identity, scale=wp[:, k % W_RING, c:c + 1],
                  bias=wp[:, k % W_RING, c + 1:c + 2]).then_inc(s_xsT_ready, 1)

            def relu(k):
                if k >= H_RING:
                    act.wait_ge(s_y_e_ps, k - H_RING + 1)
                act.wait_ge(s_h_ps, k + 1)
                for j in range(FJ - 1):
                    A(hh[:, k % H_RING, j, :], dA_ps[:, k % 2, j * P:(j + 1) * P], ACT.Relu,
                      bias=wp[:, k % W_RING, 2 * F + j:2 * F + j + 1]).then_inc(s_hh_act, 1)

            rstd_of(NCH - 1)
            normed(NCH - 1)
            x1T_copy(NCH - 1)
            for m in range(PAIRS_E):
                in_rstd(m)
            alpha_exp(NCH - 1)
            act.wait_ge(s_fill_ready, 1)
            fill_rows(act, registers(mybir.EngineType.Activation, fill_row, 4, E * REGION - 2 * P))
            xsT_affine(0)
            xsT_affine(1)
            for k in range(NS):
                relu(k)
                for m in pairs_at(STATS_AT, k):
                    in_rstd(m)
                if k + 2 < NS:
                    xsT_affine(k + 2)
                if k >= 2:
                    out_rstd(k - 2)
            out_rstd(NS - 2)
            out_rstd(NS - 1)

        @block.vector
        def _(dve):
            V = nc.vector

            def make_delta(g):
                dve.wait_ge(s_dt_log, g + 1)
                if g > 0:
                    dve.wait_ge(s_rest_ready[0], 2 * g)
                if g > 0:
                    dve.wait_ge(s_du_ready, g)
                if g > 0:
                    dve.wait_ge(s_part_ready[0], 2 * g)
                V.tensor_tensor(delta[:, 0, :, :], dt_pos[:], dt_abs[:], ALU.add).then_inc(s_delta_ready, 1)

            def make_du(g):
                dve.wait_ge(s_delta_ready, g + 1)
                dve.wait_ge(s_u_ready, 2 * g + 2)
                if g > 0:
                    dve.wait_ge(s_rest_ready[1], 2 * g)
                    dve.wait_ge(s_part_ready[1], 2 * g)
                V.tensor_tensor(du[:, 0, :, :], delta[:, 0, :, :], u_sb[:, buf(g), :, :], ALU.mult).then_inc(s_du_ready, 1)

            def rest_du(g, part):
                dve.wait_ge(s_part_ready[1], 2 * g + part + 1)
                if part == 0:
                    V.tensor_tensor(du[:, 1, :, :], du[:, 0, :, :], du_p[:, 0, :, :], ALU.subtract).then_inc(s_rest_ready[1], 1)
                else:
                    dve.wait_ge(s_rest_ready[1], 2 * g + 1)
                    if g > 0:
                        for r in range(NR):
                            dve.wait_ge(s_parts_in[r], 16 * 2 * PARTS * g)
                    V.tensor_tensor(du_p[:, 2, :, :], du[:, 1, :, :], du_p[:, 1, :, :], ALU.subtract).then_inc(s_rest_ready[1], 1)

            def dbu_of(G):
                if G >= NG:
                    return
                g = G // GROUPS
                dve.wait_ge(s_dux_ready, G + 1)
                if G - DBU_RING + 1 > 0:
                    dve.wait_ge(s_scan_done, G - DBU_RING + 1)
                if G % GROUPS == 0:
                    dve.wait_ge(s_bc_ready, 32 * (g + 1))
                V.tensor_tensor(dbu[:, G % DBU_RING, :], b_rep[:, buf(g), :], dux_ps[:, G % DUX_RING, :], ALU.mult).then_inc(s_dbu_done, 1)

            def scan(G):
                g, n = G // GROUPS, G % GROUPS
                dve.wait_ge(s_dA_ready, G + 1)
                dve.wait_ge(s_dbu_done, G + 1)
                if G - S_RING + 1 > 0:
                    dve.wait_ge(s_cs_pool, n_cs_pool(G - S_RING + 1))
                    if n_cs_dve(G - S_RING + 1) > 0:
                        dve.wait_ge(s_cs_dve, n_cs_dve(G - S_RING + 1))
                if G >= S_RING:
                    Gp = G - S_RING
                    kept = sum(1 for i in range(Gp + 1) if i // GROUPS % CPB < CPB - 1)
                    if kept > 0:
                        dve.wait_ge(s_carry_done, kept)
                init = 0.0
                if g % CPB:
                    if g // CPB * GROUPS * (CPB - 1) + (g % CPB - 1) * GROUPS + n + 1 > 0:
                        dve.wait_ge(s_carry_done, g // CPB * GROUPS * (CPB - 1) + (g % CPB - 1) * GROUPS + n + 1)
                    init = carry[:, n:n + 1]
                V.tensor_tensor_scan(s_sb[:, G % S_RING, :], dA_ps[:, G % DA_RING, :], dbu[:, G % DBU_RING, :], init,
                                     ALU.mult, ALU.add).then_inc(s_scan_done, 1)

            def c_times_s_dve(G):
                dve.wait_ge(s_scan_done, G + 1)
                if G // NK - P_RING // NK + 1 > 0:
                    dve.wait_ge(s_ysum_done, G // NK - P_RING // NK + 1)
                V.tensor_tensor(cs[:, G % P_RING, :], s_sb[:, G % S_RING, :], c_rep[:, buf(G // GROUPS), :], ALU.mult).then_inc(s_cs_dve, 1)

            def gate(Hi):
                g, h = Hi // H, Hi % H
                dve.wait_ge(s_ysum_done, NR * (Hi + 1))
                dve.wait_ge(s_res_ready, g + 1)
                if g - 1 > 0:
                    dve.wait_ge(s_out_ps, g - 1)
                V.tensor_tensor(yg[:, buf(g), h, :], res_sb[:, buf(g), h, :], y_ps[:], ALU.mult).then_inc(s_yg_ready, 1)

            def residual(g):
                if g > 0:
                    dve.wait_ge(s_x1_ready, g)
                dve.wait_ge(s_out_ps, g + 1)
                V.scalar_tensor_tensor(out=v_sb[:], in0=x_sb[:, tiles(g), :], scalar=2.0,
                                       in1=m_ps[:, 0, :].rearrange("p (t d) -> p t d", t=TT), op0=ALU.mult, op1=ALU.add).then_inc(s_v_ready, 1)

            def stats(g):
                dve.wait_ge(s_v_ready, g + 1)
                for j in range(TT):
                    V.bn_stats(st[:, j, :], v_sb[:, j, :]).then_inc(s_st_done, 1)
                for j in range(TT):
                    dve.wait_ge(s_st_done, TT * g + j + 1)
                    V.bn_aggr(mv[:, j, :], st[:, j, :]).then_inc(s_mv_done, 1)

            def shift(g):
                dve.wait_ge(s_rstd_ready, g + 1)
                if g > 0:
                    dve.wait_ge(s_x1_ready, g)
                V.scalar_tensor_tensor(out=nmr[:], in0=mv[:, :, 0], scalar=-1.0, in1=rstd[:], op0=ALU.mult, op1=ALU.mult).then_inc(s_shift_ready, 1)

            def route_tokens(g):
                dve.wait_ge(s_aff_ps, g + 1)
                V.tensor_copy(aff[:], m_ps[:, 0, 0:TT * E].rearrange("p (t e) -> p t e", t=TT)).then_inc(s_aff_ready, 1)
                dve.wait_ge(s_aff_ready, g + 1)
                for j in range(TT):
                    V.max(top[:, TT * g + j, :], aff[:, j, :]).then_inc(s_top_ready, 1)
                for j in range(TT):
                    dve.wait_ge(s_top_ready, TT * g + j + 1)
                    V.max_index(topi[:, j, :], top[:, TT * g + j, :], aff[:, j, :]).then_inc(s_topi_ready, 1)
                dve.wait_ge(s_topi_ready, TT * (g + 1))
                V.tensor_copy(eid[:], topi[:, :, 0]).then_inc(s_eid_ready, 1)
                dve.wait_ge(s_eid_ready, g + 1)
                V.tensor_tensor(onehot[:, tiles(g), :], iota8[:].unsqueeze(1).to_broadcast([P, TT, E]),
                                eid[:].unsqueeze(2).to_broadcast([P, TT, E]), ALU.is_equal).then_inc(s_onehot_ready, 1)

            def rank_tokens(g):
                dve.wait_ge(s_rank_ps, g + 1)
                if g > 0:
                    dve.wait_ge(s_posf_ready, g)
                V.tensor_tensor(rank[:], onehot[:, tiles(g), :], m_ps[:, 1, 0:TT * E].rearrange("p (t e) -> p t e", t=TT), ALU.mult).then_inc(s_rank_ready, 1)
                dve.wait_ge(s_rank_ready, g + 1)
                if g > 0:
                    dve.wait_ge(s_pos_ready, g)
                V.tensor_reduce(posf[:], rank[:], AX_X, ALU.add).then_inc(s_posf_ready, 1)
                dve.wait_ge(s_posf_ready, g + 1)
                V.tensor_copy(pos[:, tiles(g)], posf[:]).then_inc(s_pos_ready, 1)
                if g == NCH - 2:
                    early_slots()

            def early_slots():
                n_early = [0]

                def step(ins):
                    n_early[0] += 1
                    ins.then_inc(s_early, 1)

                k = kidx[:, 0:NE].unsqueeze(2)
                step(V.tensor_copy(cnt_e[:], m_ps[:, 1, TT * E:TT * E + E]))
                dve.wait_ge(s_early, n_early[0])
                step(V.tensor_tensor(full[:, :, 0:NT - 1], cnt_e[:].unsqueeze(2).to_broadcast([P, E, NT - 1]),
                                     steps[:, 1:NT].unsqueeze(1).to_broadcast([P, E, NT - 1]), ALU.is_ge))
                dve.wait_ge(s_early, n_early[0])
                step(V.tensor_reduce(nfull[:], full[:, :, 0:NT - 1], AX_X, ALU.add))
                dve.wait_ge(s_early, n_early[0])
                step(V.tensor_tensor_scan(fend[:], ones8[:], nfull[:], 0.0, ALU.mult, ALU.add))
                step(V.tensor_scalar(jump_e[:], nfull[:], -float(P), float(REGION), ALU.mult, ALU.add))
                dve.wait_ge(s_early, n_early[0])
                step(V.tensor_tensor(beyond_e[:], k.to_broadcast([P, NE, E]), fend[:].unsqueeze(1).to_broadcast([P, NE, E]), ALU.is_ge))
                step(V.tensor_tensor(fleft[:], nfull[:], fend[:], ALU.subtract))
                dve.wait_ge(s_early, n_early[0])
                step(V.tensor_reduce(etf_e[:], beyond_e[:], AX_X, ALU.add))
                step(V.tensor_tensor(jumps_e[:], beyond_e[:], jump_e[:].unsqueeze(1).to_broadcast([P, NE, E]), ALU.mult))
                step(V.tensor_scalar(taken[:], fleft[:], float(NE), 0.0, ALU.add, ALU.max))
                dve.wait_ge(s_early, n_early[0])
                V.tensor_copy(et_e[:], etf_e[:]).then_inc(s_early_ready, 1)
                V.tensor_scalar(b2_on[:, 0:NE], etf_e[0:PARTS * E, :], b2_of[:, PARTS:], None, ALU.is_equal).then_inc(s_b2_ready, 1)
                step(V.tensor_reduce(rowf_e[:, 0, :], jumps_e[:], AX_X, ALU.add))
                step(V.tensor_tensor(taken[:], taken[:], nfull[:], ALU.min))
                dve.wait_ge(s_early, n_early[0])
                V.tensor_scalar(taken0[:], taken[:, 0:1], float(P), None, ALU.mult)
                step(V.scalar_tensor_tensor(out=rowf_e[:, 1, :], in0=kidx[:, 0:NE], scalar=float(P), in1=rowf_e[:, 0, :],
                                            op0=ALU.mult, op1=ALU.add))
                dve.wait_ge(s_early, n_early[0])
                V.tensor_copy(row0_e[:], rowf_e[:, 1, :]).then_inc(s_early_ready, 1)

            def make_alpha(g):
                dve.wait_ge(s_al_ready, g + 1)
                if g > 0:
                    dve.wait_ge(s_alpha_ready, g)
                V.tensor_scalar(al_1[:], al_e[:], 1.0, None, ALU.add).then_inc(s_al1_ready, 1)
                dve.wait_ge(s_al1_ready, g + 1)
                V.reciprocal(rows[:, tiles(g), D_MODEL + 1], al_1[:]).then_inc(s_alpha_ready, 1)

            V.memset(zeros[:], 0.0)
            V.memset(eps_t[:], EPS)
            V.memset(eps4_t[:], 4 * EPS)
            V.memset(epsq_t[:], EPS / 4)
            V.memset(ones8[:], 1.0).then_inc(s_vconst_ready, 1)
            V.memset(ones_b[:], 1.0)
            V.memset(zrow[:], 0.0).then_inc(s_tok_ready, 1)
            dve.wait_ge(s_in_w_in, 16)
            dve.wait_ge(s_taps_in, 16)
            V.tensor_tensor(w_uk[:], w_uk[:], w_u.unsqueeze(1).to_broadcast([P, D_CONV, D_INNER]), ALU.mult).then_inc(s_w_uk_ready, 1)
            dve.wait_ge(s_sel_in, 16)
            V.tensor_copy(sel[:], sel_f[:]).then_inc(s_const_ready, 1)

            pieces = [
                (14, -1, residual), (16, -1, stats), (19, -1, shift), (20, 1, make_delta), (23, 1, make_du), (24, 1, lambda g: rest_du(g, 0)),
                (28, -1, route_tokens), (28, 1, lambda g: rest_du(g, 1)), (31, -1, make_alpha), (29, -1, rank_tokens)]
            dve.wait_ge(s_small_in, 16)
            dve.wait_ge(s_aneg_ready, 1)
            V.tensor_scalar(a_neg[:], a_exp[:], -1.0, None, ALU.mult).then_inc(s_aneg_ready, 1)
            dve.wait_ge(s_late_in, 16 * 6)
            V.tensor_copy(ltri[:], ltri_f)
            V.tensor_copy(region_b[:], route_sb[0:1, E + NT + NS + E:].rearrange("p (t e) -> p t e", t=TT))
            V.tensor_copy(rows[:, :, D_MODEL].bitcast(U32), tok[:, 0:NT])
            dve.wait_ge(s_tok_ready, 1)
            V.tensor_copy(zrow[:, :, D_MODEL].bitcast(U32), tok[:, NT:NT + 1].to_broadcast([P, 2])).then_inc(s_tok_ready, 1)
            for h in range(H):
                last = V.tensor_scalar(dperm[:, h, :], perm, d_in[:, h:h + 1], None, ALU.mult)
            last.then_inc(s_dperm_ready, 1)
            V.tensor_copy(b2_part[:, 0, :], b2_f[:]).then_inc(s_b2_step, 1)
            dve.wait_ge(s_b2_step, 1)
            V.tensor_tensor(b2_rest[:, 0, :], b2_f[:], b2_part[:, 0, :], ALU.subtract).then_inc(s_b2_step, 1)
            V.tensor_scalar(b2_acc[:, 0, :], b2_part[:, 0, :], b2_of[:, 0:1], None, ALU.mult)
            dve.wait_ge(s_b2_step, 2)
            V.tensor_copy(b2_part[:, 1, :], b2_rest[:, 0, :]).then_inc(s_b2_step, 1)
            dve.wait_ge(s_b2_step, 3)
            V.tensor_tensor(b2_rest[:, 1, :], b2_rest[:, 0, :], b2_part[:, 1, :], ALU.subtract)
            V.scalar_tensor_tensor(out=b2_acc[:, 1, :], in0=b2_part[:, 1, :], scalar=b2_of[:, 1:2], in1=b2_acc[:, 0, :],
                                   op0=ALU.mult, op1=ALU.add).then_inc(s_b2_step, 1)
            dve.wait_ge(s_b2_step, 4)
            V.scalar_tensor_tensor(out=b2_p[:], in0=b2_rest[:, 1, :], scalar=b2_of[:, 2:3], in1=b2_acc[:, 1, :],
                                   op0=ALU.mult, op1=ALU.add).then_inc(s_b2_ready, 1)
            for at, ahead, piece in pieces:
                if ahead == 1:
                    piece(0)
            dbu_of(0)
            for G in range(NG):
                g, s = G // GROUPS, G % GROUPS
                dbu_of(G + 1)
                scan(G)
                if G >= 1 and on_dve(G - 1):
                    c_times_s_dve(G - 1)
                Gs = G - SUM_LAG - GATE_LAG
                if Gs >= 0 and (Gs + 1) % (NK * NR) == 0:
                    gate(Gs // (NK * NR))
                for at, ahead, piece in pieces:
                    if at == s and 0 <= g + ahead < NCH:
                        piece(g + ahead)
            if on_dve(NG - 1):
                c_times_s_dve(NG - 1)
            gate(NCH * H - 1)
            def in_stats(m):
                for k in PAIRS[m]:
                    dve.wait_ge(s_xs_in[k % XS_RING], 16 * (k // XS_RING + 1))
                    V.bn_stats(st_i[:, k, :], xs[:, k, 0:D_MODEL]).then_inc(s_sti_ready, 1)
                for k in PAIRS[m]:
                    dve.wait_ge(s_sti_ready, k + 1)
                    V.bn_aggr(mv_i[:, k, :], st_i[:, k, :]).then_inc(s_mvi_ready, 1)

            def in_norm(k):
                dve.wait_ge(s_rstdi_ready, PAIR_OF[k] + 1)
                if k >= XN_RING:
                    dve.wait_ge(s_xsT_ps, k - XN_RING + 1)
                V.tensor_scalar(xn[:, k % XN_RING, :], xs[:, k, 0:D_MODEL], mv_i[:, k, 0:1], rstd_i[:, k:k + 1], ALU.subtract,
                                ALU.mult).then_inc(s_xn_ready, 1)

            def relu_last(k):
                j = FJ - 1
                dve.wait_ge(s_h_last_ps, k + 1)
                if k >= H_RING:
                    dve.wait_ge(s_y_e_ps, k - H_RING + 1)
                V.tensor_scalar(hh[:, k % H_RING, j, :], h_last(k),
                                wp[:, k % W_RING, 2 * F + j:2 * F + j + 1], 0.0, ALU.add, ALU.max).then_inc(s_hh_dve, 1)

            def out_z(k):
                dve.wait_ge(s_y_e_ps, k + 1)
                if k >= Z_RING:
                    dve.wait_ge(s_o_ready, k - Z_RING + 1)
                V.scalar_tensor_tensor(out=z[:, k % Z_RING, :], in0=dux_ps[:, k % 2, 0:P], scalar=xs[:, k, D_MODEL + 1:D_MODEL + 2],
                                       in1=xs[:, k, 0:D_MODEL], op0=ALU.mult, op1=ALU.add).then_inc(s_z_ready, 1)
                dve.wait_ge(s_z_ready, k + 1)
                V.bn_stats(st_o[:, k, :], z[:, k % Z_RING, :]).then_inc(s_sto_ready, 1)
                dve.wait_ge(s_sto_ready, k + 1)
                V.bn_aggr(mv_o[:, k, :], st_o[:, k, :]).then_inc(s_mvo_ready, 1)

            def out_norm(k):
                dve.wait_ge(s_rstdo_ready, k + 1)
                V.tensor_scalar(o_sb[:, k, :], z[:, k % Z_RING, :], mv_o[:, k, 0:1], rstd_o[:, k:k + 1], ALU.subtract,
                                ALU.mult).then_inc(s_o_ready, 1)

            residual(NCH - 1)
            stats(NCH - 1)
            shift(NCH - 1)
            for m in range(PAIRS_E):
                in_stats(m)
            for k in range(NE):
                in_norm(k)
            route_tokens(NCH - 1)
            make_alpha(NCH - 1)
            rank_tokens(NCH - 1)

            n_route = [0]

            def routed(ins):
                n_route[0] += 1
                ins.then_inc(s_route, 1)

            dve.wait_ge(s_count_ps, 1)
            routed(V.tensor_copy(cnt[:], y_ps[:, 0:E]))
            dve.wait_ge(s_route, n_route[0])
            V.tensor_tensor(fill_row[:], cnt[:], region0, ALU.add).then_inc(s_fill_ready, 1)
            routed(V.tensor_tensor(past[:], cnt[:].unsqueeze(2).to_broadcast([P, E, NT]),
                                   steps.unsqueeze(1).to_broadcast([P, E, NT]), ALU.is_gt))
            dve.wait_ge(s_route, n_route[0])
            routed(V.tensor_reduce(ntile[:], past[:], AX_X, ALU.add))
            dve.wait_ge(s_route, n_route[0])
            routed(V.tensor_tensor(nleft[:], ntile[:], taken[:], ALU.subtract))
            routed(V.tensor_scalar(jump[:], ntile[:], -float(P), float(REGION), ALU.mult, ALU.add))
            dve.wait_ge(s_route, n_route[0])
            routed(V.tensor_tensor_scan(tend[:], ones8[:], nleft[:], 0.0, ALU.mult, ALU.add))
            routed(V.scalar_tensor_tensor(out=jump[:, 0:E - 1], in0=taken[:, 1:E], scalar=float(P), in1=jump[:, 0:E - 1],
                                          op0=ALU.mult, op1=ALU.add))
            routed(V.tensor_scalar(lim[:], ntile[:, E - 1:E], float(P), float((E - 1) * REGION), ALU.mult, ALU.add))
            dve.wait_ge(s_route, n_route[0])
            routed(V.tensor_tensor(beyond[:], kidx[:, 0:NL].unsqueeze(2).to_broadcast([P, NL, E]),
                                   tend[:].unsqueeze(1).to_broadcast([P, NL, E]), ALU.is_ge))
            dve.wait_ge(s_route, n_route[0])
            routed(V.tensor_reduce(etf[:], beyond[:, :, 0:E - 1], AX_X, ALU.add))
            routed(V.tensor_tensor(jumps[:, :, 0:E - 1], beyond[:, :, 0:E - 1],
                                   jump[:, 0:E - 1].unsqueeze(1).to_broadcast([P, NL, E - 1]), ALU.mult))
            dve.wait_ge(s_route, n_route[0])
            V.tensor_copy(et[:], etf[:]).then_inc(s_slots_ready, 1)
            V.tensor_scalar(b2_on[:, NE:NS], etf[0:PARTS * E, :], b2_of[:, PARTS:], None, ALU.is_equal).then_inc(s_b2_ready, 1)
            routed(V.tensor_reduce(rowf[:], jumps[:, :, 0:E - 1], AX_X, ALU.add))
            dve.wait_ge(s_route, n_route[0])
            routed(V.scalar_tensor_tensor(out=rowf[:], in0=kidx[:, 0:NL], scalar=float(P), in1=rowf[:], op0=ALU.mult, op1=ALU.add))
            dve.wait_ge(s_route, n_route[0])
            V.tensor_scalar(row0[:], rowf[:], taken0[:, 0:1], lim[:, 0:1], ALU.add, ALU.min).then_inc(s_slots_ready, 1)

            for k in range(NS):
                for m in pairs_at(STATS_AT, k):
                    in_stats(m)
                relu_last(k)
                if k >= 1:
                    out_z(k - 1)
                for m in pairs_at(NORM_AT, k):
                    for i in PAIRS[m]:
                        in_norm(i)
                if k >= 2:
                    out_norm(k - 2)
            out_z(NS - 1)
            out_norm(NS - 2)
            out_norm(NS - 1)

        @block.gpsimd
        def _(pool):
            G_ = nc.gpsimd

            def rest_delta(g, part):
                pool.wait_ge(s_part_ready[0], 2 * g + part + 1)
                if part == 0:
                    G_.tensor_tensor(delta[:, 1, :, :], delta[:, 0, :, :], delta_p[:, 0, :, :], ALU.subtract).then_inc(s_rest_ready[0], 1)
                else:
                    pool.wait_ge(s_rest_ready[0], 2 * g + 1)
                    if g > 0:
                        for r in range(NR):
                            pool.wait_ge(s_parts_in[r], 16 * 2 * PARTS * g)
                    G_.tensor_tensor(delta_p[:, 2, :, :], delta[:, 1, :, :], delta_p[:, 1, :, :], ALU.subtract).then_inc(s_rest_ready[0], 1)

            def c_times_s(G):
                g = G // GROUPS
                pool.wait_ge(s_scan_done, G + 1)
                if G % GROUPS == 0:
                    pool.wait_ge(s_bc_ready, 32 * (g + 1))
                if G // NK - P_RING // NK + 1 > 0:
                    pool.wait_ge(s_ysum_done, G // NK - P_RING // NK + 1)
                G_.tensor_tensor(cs[:, G % P_RING, :], s_sb[:, G % S_RING, :], c_rep[:, buf(g), :], ALU.mult).then_inc(s_cs_pool, 1)

            def send_rows(g):
                pool.wait_ge(s_pos_ready, g + 1)
                pool.wait_ge(s_alpha_ready, g + 1)
                pool.wait_ge(s_x1_ready, g + 1)
                if g == 0:
                    pool.wait_ge(s_tok_ready, 2)
                for t in range(TT * g, TT * g + TT):
                    G_.indirect_dma_start(xs_dram, bass.IndirectOffsetOnAxis(ap=pos[:, t:t + 1], axis=0), rows[:, t, :], None).then_inc(s_scattered if g < NCH - 1 else s_last_scattered, 16)

            G_.dma_start(const_sb[:], consts).then_inc(s_late_in, 16)
            G_.dma_start(route_sb[:], route_c).then_inc(s_late_in, 16)
            G_.dma_start(tok[:], tok_c).then_inc(s_late_in, 16)
            G_.dma_start(w_out[:], out_w).then_inc(s_late_in, 16)
            G_.dma_start(b2_f[:], b2_rows).then_inc(s_late_in, 16)
            G_.dma_start(b2_of[:], b2_pick).then_inc(s_late_in, 16)
            pieces = [
                (19, 1, lambda g: rest_delta(g, 0)), (19, 1, lambda g: rest_delta(g, 1)), (31, -1, send_rows)]
            for at, ahead, piece in pieces:
                if ahead == 1:
                    piece(0)
            for G in range(NG):
                g, s = G // GROUPS, G % GROUPS
                if not on_dve(G):
                    c_times_s(G)
                for at, ahead, piece in pieces:
                    if at == s and 0 <= g + ahead < NCH:
                        piece(g + ahead)
            send_rows(NCH - 1)

            def store_rows(k):
                pool.wait_ge(s_o_ready, k + 1)
                G_.indirect_dma_start(out_rows, bass.IndirectOffsetOnAxis(ap=xs[:, k, D_MODEL:D_MODEL + 1].bitcast(U32), axis=0),
                                      o_sb[:, k, :], None, bounds_check=N_TOK - 1, oob_is_err=False).then_inc(s_stored, 16)

            for k in range(NS):
                store_rows(k)


def kernel(**inputs):
    import numpy as np
    import concourse.bacc as bacc
    from concourse.bass_utils import run_bass_kernel_spmd

    a = {k: np.asarray(v) for k, v in inputs.items()}
    B, L, D = a["L0_attn_x"].shape
    NT = B * L // P
    NS = NT + E - 1
    y_order = np.arange(P).reshape(NR, NK, CG).transpose(1, 0, 2).reshape(-1)
    in_w = a["L0_attn_in_w"]
    w_r = in_w[:, D_INNER:].reshape(D, H, P)[:, :, y_order].reshape(D, D_INNER)
    w_out = a["L0_attn_out_w"].reshape(H, P, D)[:, y_order, :].transpose(1, 0, 2)
    by_half = lambda v: v.reshape(H, P, -1).transpose(1, 0, 2)
    a_log = a["L0_attn_A_log"].reshape(H, NR, NK, CG, D_STATE).transpose(4, 3, 0, 1, 2).reshape(P, GROUPS)
    w2 = a["L0_ffn_w2"].reshape(E, FJ, P, D).transpose(0, 2, 1, 3).reshape(E, P, FJ * D)
    b1 = a["L0_ffn_b1"].reshape(E, FJ, P).transpose(0, 2, 1)
    columns = [a[f"L0_ffn_{n}"][:, :, None] for n in ("ln_g", "ln_b")]
    w_pack = np.concatenate([a["L0_ffn_w1"], w2, b1, *columns], axis=2)
    sel = np.zeros((PARTS, NK, CG, NK, D_STATE, CG), np.float32)
    for k in range(NK):
        for i in range(CG):
            sel[:, k, i, k, :, i] = 1
    sely = np.zeros((D_STATE, CG, NR, NR, CG), np.float32)
    for r in range(NR):
        for i in range(CG):
            sely[:, i, r, r, i] = 1
    perm = np.zeros((P, P), np.float32)
    perm[y_order, np.arange(P)] = 1
    rows = lambda v: np.broadcast_to(v.astype(np.float32), (P, v.size))
    b2_pick = np.concatenate([np.repeat(np.eye(PARTS), E, axis=0), np.tile(np.arange(E), PARTS)[:, None]], axis=1).astype(np.float32)
    region = B * L + 2 * P
    consts = np.concatenate([sely.reshape(P, P), perm, np.triu(np.ones((P, P), np.float32), 1)], axis=1)
    route = np.concatenate([rows(np.arange(E)), rows(P * np.arange(NT)), rows(np.arange(NS)), rows(region * np.arange(E)),
                            rows(np.tile(region * np.arange(E), TT))], axis=1)
    tok = np.arange(NT)[None, :] * P + np.arange(P)[:, None]
    tok = np.concatenate([tok, np.full((P, 1), 2 * B * L)], axis=1).astype(np.uint32)
    small = np.concatenate([a["L0_attn_norm_w"][:, None], by_half(a["L0_attn_conv_b"])[:, :, 0], by_half(a["L0_attn_dt_b"])[:, :, 0],
                            by_half(a["L0_attn_D"])[:, :, 0], a_log, a["L0_ffn_centroids"].T], axis=1)
    arrays = {
        "x": a["L0_attn_x"], "in_w": np.concatenate([w_r, in_w[:, :D_INNER]], axis=1),
        "conv_w": a["L0_attn_conv_w"].reshape(D_INNER, D_CONV).T.reshape(1, -1), "x_proj_w": by_half(a["L0_attn_x_proj_w"]), "dt_w": a["L0_attn_dt_w"], "out_w": w_out, "small": small,
        "w_pack": w_pack, "b2_rows": np.tile(a["L0_ffn_b2"], (PARTS, 1)), "b2_pick": b2_pick, "ident_c": np.eye(P, dtype=np.float32), "sel_c": sel.reshape(PARTS * QROWS, NK, P),
        "route_c": route, "tok_c": tok, "consts": consts,
    }
    nc = bacc.Bacc("TRN2", target_bir_lowering=False, num_devices=1)
    feed, args = {}, []
    for name, v in arrays.items():
        v = np.ascontiguousarray(v)
        feed[f"in_{name}"] = v
        args.append(nc.dram_tensor(f"in_{name}", v.shape, mybir.dt.from_np(v.dtype), kind="ExternalInput").ap())
    args.append(nc.dram_tensor("out_0", (B, L, D), F32, kind="ExternalOutput").ap())
    args.append(nc.dram_tensor("xs_dram", (E * region, ROW), F32, kind="Internal").ap())
    fused_mamba_routed_ffn(nc, *args)
    r = run_bass_kernel_spmd(nc, [feed], core_ids=[0])
    return r.results[0]["out_0"]
```
